# Optimizing a Trainium2 kernel written in Bass

```python
import numpy as np
import jax
import jax.numpy as jnp

def _softmax(x, axis=-1):
    return jax.nn.softmax(x, axis=axis)

def _gelu(x):
    return jax.nn.gelu(x, approximate=True)

def _silu(x):
    return jax.nn.silu(x)

def _sigmoid(x):
    return jax.nn.sigmoid(x)

def _layernorm(x, axis=-1, eps=1e-05):
    m = jnp.mean(x, axis=axis, keepdims=True)
    v = jnp.var(x, axis=axis, keepdims=True)
    return (x - m) / jnp.sqrt(v + eps)

def _scatter_add(tgt, idx, src, axis=0):
    return tgt.at[idx].add(src)

def _segment_sum(src, seg, n):
    return jax.ops.segment_sum(src, seg, n)
kernel_name = 'mk_lm_tower_d2_tok_ids512_r4_09aa1a'

def setup_inputs(seed: int=0):
    np.random.seed(seed)
    _w = jnp.asarray

    def _rec_inputs():
        import jax
        import jax.numpy as jnp
        _rk = jax.random.key(seed)
        x = jax.random.randint(jax.random.fold_in(_rk, 1), (4, 512), 0, 24991, jnp.int32)
        return x
    x = _rec_inputs()

    def _L0_tok_setup():
        import jax, jax.numpy as jnp
        import numpy as np
        V, DIM, EMB, H = (25000, 75, 128, 10)
        B, S = (8, 512)

        def _gate(e, W1, b1, W2, b2):
            h = jnp.einsum('bsd,hd->bsh', e, W1) + b1
            return jnp.einsum('bsh,oh->bso', h, W2) + b2
        key = jax.random.key(seed)
        ks = jax.random.split(key, 20)
        inp = {'word': jax.random.randint(ks[0], (B, S), 0, V, dtype=jnp.int32), 'glove_tab': jax.random.normal(ks[1], (V, DIM), jnp.float32) * 0.1, 'fast_tab': jax.random.normal(ks[2], (V, DIM), jnp.float32) * 0.1, 'levy_tab': jax.random.normal(ks[3], (V, DIM), jnp.float32) * 0.1, 'W_glove': jax.random.normal(ks[4], (EMB, DIM), jnp.float32) * 0.05, 'b_glove': jnp.zeros((EMB,), jnp.float32), 'W_fast': jax.random.normal(ks[5], (EMB, DIM), jnp.float32) * 0.05, 'b_fast': jnp.zeros((EMB,), jnp.float32), 'W_levy': jax.random.normal(ks[6], (EMB, DIM), jnp.float32) * 0.05, 'b_levy': jnp.zeros((EMB,), jnp.float32), 'gW1_glove': jax.random.normal(ks[7], (H, DIM), jnp.float32) * 0.05, 'gb1_glove': jnp.zeros((H,), jnp.float32), 'gW2_glove': jax.random.normal(ks[8], (1, H), jnp.float32) * 0.3, 'gb2_glove': jnp.zeros((1,), jnp.float32), 'gW1_fast': jax.random.normal(ks[9], (H, DIM), jnp.float32) * 0.05, 'gb1_fast': jnp.zeros((H,), jnp.float32), 'gW2_fast': jax.random.normal(ks[10], (1, H), jnp.float32) * 0.3, 'gb2_fast': jnp.zeros((1,), jnp.float32), 'gW1_levy': jax.random.normal(ks[11], (H, DIM), jnp.float32) * 0.05, 'gb1_levy': jnp.zeros((H,), jnp.float32), 'gW2_levy': jax.random.normal(ks[12], (1, H), jnp.float32) * 0.3, 'gb2_levy': jnp.zeros((1,), jnp.float32)}
        return inp
    _L0_tok_all = _L0_tok_setup()
    _L0_tok_in = {k: v for k, v in _L0_tok_all.items() if k in ('glove_tab', 'fast_tab', 'levy_tab', 'W_glove', 'b_glove', 'W_fast', 'b_fast', 'W_levy', 'b_levy', 'gW1_glove', 'gb1_glove', 'gW2_glove', 'gb2_glove', 'gW1_fast', 'gb1_fast', 'gW2_fast', 'gb2_fast', 'gW1_levy', 'gb1_levy', 'gW2_levy', 'gb2_levy')}
    del _L0_tok_all

    def _L0_attn_setup():
        import math
        import jax, jax.numpy as jnp
        import numpy as np
        NUM_HEADS = 8
        ALPHA = 20.0
        LN_EPS = 1e-05

        def _forward(x, qkv_w, qkv_b, ln_g, ln_b, out_w, out_b):
            B, N, C = x.shape
            H = NUM_HEADS
            D = C // H
            qkv = x @ qkv_w + qkv_b
            q, k, v = jnp.split(qkv, 3, axis=-1)

            def to_heads(t):
                return t.reshape(B, N, H, D).transpose(0, 2, 1, 3)
            q, k, v = (to_heads(q), to_heads(k), to_heads(v))
            q_norm = jnp.linalg.norm(q, axis=-1, keepdims=True)
            k_norm = jnp.linalg.norm(k, axis=-1, keepdims=True)
            q_t = q / q_norm
            dq = jnp.tanh(q / q_norm * ALPHA) * (math.pi / 4)
            dk = jnp.tanh(k / k_norm * ALPHA) * (math.pi / 4)
            k3 = jnp.abs(k) ** 3
            kf = jnp.concatenate([k3 * jnp.cos(dk), k3 * jnp.sin(dk)], axis=-1)
            power = 1.5 * (0.5 + jnp.tanh(q_norm))
            q_t = (q_t ** 2) ** power
            qf = jnp.concatenate([q_t * jnp.cos(dq), q_t * jnp.sin(dq)], axis=-1)
            k_mean = jnp.mean(kf, axis=2, keepdims=True)
            z = 1.0 / (jnp.einsum('bhnf,bhmf->bhnm', qf, k_mean) + 1e-06)
            scale = N ** (-0.5)
            kv = jnp.einsum('bhnf,bhnd->bhfd', kf * scale, v * scale)
            out = jnp.einsum('bhnf,bhfd->bhnd', qf, kv) * z
            out = out.transpose(0, 2, 1, 3).reshape(B, N, C)
            mu = jnp.mean(out, axis=-1, keepdims=True)
            var = jnp.var(out, axis=-1, keepdims=True)
            out = (out - mu) * jax.lax.rsqrt(var + LN_EPS) * ln_g + ln_b
            return out @ out_w + out_b
        key = jax.random.key(seed)
        ks = jax.random.split(key, 6)
        B, N, C = (8, 1024, 128)
        s = 1.0 / math.sqrt(C)
        return {'x': jax.random.normal(ks[0], (B, N, C), dtype=jnp.float32), 'qkv_w': jax.random.normal(ks[1], (C, 3 * C), dtype=jnp.float32) * s, 'qkv_b': jnp.zeros((3 * C,), dtype=jnp.float32), 'ln_g': jnp.ones((C,), dtype=jnp.float32), 'ln_b': jnp.zeros((C,), dtype=jnp.float32), 'out_w': jax.random.normal(ks[2], (C, C), dtype=jnp.float32) * s, 'out_b': jnp.zeros((C,), dtype=jnp.float32)}
    _L0_attn_all = _L0_attn_setup()
    _L0_attn_in = {k: v for k, v in _L0_attn_all.items() if k in ('qkv_w', 'qkv_b', 'ln_g', 'ln_b', 'out_w', 'out_b')}
    del _L0_attn_all

    def _L0_ffn_setup():
        import jax, jax.numpy as jnp
        import numpy as np
        B, S, D, F, E = (8, 1024, 128, 512, 8)
        INIT_LAMBDA = 0.2
        LN_EPS = 1e-05
        LN_MERGE = 0.03
        key = jax.random.key(seed)
        ks = jax.random.split(key, 12)
        n = lambda k, shp, s=1.0: jax.random.normal(k, shp, dtype=jnp.float32) * s
        return {'hidden_states': n(ks[0], (B, S, D)), 'gfc1_w': n(ks[1], (D, D), 0.01), 'gfc1_b': jnp.zeros((D,), jnp.float32), 'gfc2_w': n(ks[2], (E, D), 0.01), 'gfc2_b': jnp.full((E,), INIT_LAMBDA, dtype=jnp.float32), 'W1': n(ks[3], (F, D), 0.02), 'b1': jnp.zeros((F,), jnp.float32), 'W2': n(ks[4], (D, F), 0.02), 'b2': jnp.zeros((D,), jnp.float32), 'ln_g': jnp.ones((D,), jnp.float32), 'ln_b': jnp.zeros((D,), jnp.float32), 'tv_W1': n(ks[5], (E, F, D), 0.02), 'tv_b1': n(ks[6], (E, F), 0.02), 'tv_W2': n(ks[7], (E, D, F), 0.02), 'tv_b2': n(ks[8], (E, D), 0.02), 'tv_ln_g': n(ks[9], (E, D), 0.02), 'tv_ln_b': n(ks[10], (E, D), 0.02)}
    _L0_ffn_all = _L0_ffn_setup()
    _L0_ffn_in = {k: v for k, v in _L0_ffn_all.items() if k in ('gfc1_w', 'gfc1_b', 'gfc2_w', 'gfc2_b', 'W1', 'b1', 'W2', 'b2', 'ln_g', 'ln_b', 'tv_W1', 'tv_b1', 'tv_W2', 'tv_b2', 'tv_ln_g', 'tv_ln_b')}
    del _L0_ffn_all

    def _L1_attn_setup():
        import jax, jax.numpy as jnp
        import numpy as np
        DIM = 128
        HEADS = 8
        DIM_HEAD = 64
        DIM_INNER = HEADS * DIM_HEAD
        FRAC_GRAD = 0.5
        SCALE = DIM_HEAD ** (-0.5)
        EPS_CUMPROD = 1e-10
        EPS_INV = 1e-08

        def _rms_norm(x, gamma):
            nrm = jnp.linalg.norm(x, axis=-1, keepdims=True)
            return x / jnp.maximum(nrm, 1e-12) * DIM ** 0.5 * gamma

        def _safe_cumprod(t, axis):
            t = jnp.clip(t, EPS_CUMPROD, 1.0)
            return jnp.exp(jnp.cumsum(jnp.log(t), axis=axis))
        key = jax.random.key(seed)
        ks = jax.random.split(key, 8)
        b, n = (2, 512)
        x = jax.random.normal(ks[0], (b, n, DIM), dtype=jnp.float32)
        gamma = jnp.ones((DIM,), dtype=jnp.float32)
        w_qkv = jax.random.normal(ks[1], (DIM, 3 * DIM_INNER), dtype=jnp.float32) * 0.02
        b_qkv = jnp.zeros((3 * DIM_INNER,), dtype=jnp.float32)
        w_a = jax.random.normal(ks[2], (DIM, DIM_INNER), dtype=jnp.float32) * 0.02
        b_a = jnp.full((DIM_INNER,), 2.0, dtype=jnp.float32)
        w_out = jax.random.normal(ks[3], (DIM_INNER, DIM), dtype=jnp.float32) * 0.02
        b_out = jnp.zeros((DIM,), dtype=jnp.float32)
        return {'x': x, 'gamma': gamma, 'w_qkv': w_qkv, 'b_qkv': b_qkv, 'w_a': w_a, 'b_a': b_a, 'w_out': w_out, 'b_out': b_out}
    _L1_attn_all = _L1_attn_setup()
    _L1_attn_in = {k: v for k, v in _L1_attn_all.items() if k in ('gamma', 'w_qkv', 'b_qkv', 'w_a', 'b_a', 'w_out', 'b_out')}
    del _L1_attn_all

    def _L1_ffn_setup():
        import jax, jax.numpy as jnp
        import numpy as np
        NUM_EXPERTS = 8
        TOP_K = 2
        LN_EPS = 1e-05

        def _layernorm(x, g, b):
            mu = jnp.mean(x, axis=-1, keepdims=True)
            var = jnp.mean(jnp.square(x - mu), axis=-1, keepdims=True)
            return (x - mu) * jax.lax.rsqrt(var + LN_EPS) * g + b
        key = jax.random.key(seed)
        ks = jax.random.split(key, 8)
        B, S, D, F, E = (8, 1024, 128, 512, NUM_EXPERTS)
        return {'x': jax.random.normal(ks[0], (B, S, D), dtype=jnp.float32), 'gate_w': jax.random.normal(ks[1], (D, E), dtype=jnp.float32) * 0.02, 'w1': jax.random.normal(ks[2], (E, D, F), dtype=jnp.float32) * 0.02, 'b1': jnp.zeros((E, F), dtype=jnp.float32), 'w2': jax.random.normal(ks[3], (E, F, D), dtype=jnp.float32) * 0.02, 'b2': jnp.zeros((E, D), dtype=jnp.float32), 'ln_g': jnp.ones((D,), dtype=jnp.float32), 'ln_b': jnp.zeros((D,), dtype=jnp.float32)}
    _L1_ffn_all = _L1_ffn_setup()
    _L1_ffn_in = {k: v for k, v in _L1_ffn_all.items() if k in ('gate_w', 'w1', 'b1', 'w2', 'b2', 'ln_g', 'ln_b')}
    del _L1_ffn_all
    return {'x': x, 'L0_tok_glove_tab': _L0_tok_in['glove_tab'], 'L0_tok_fast_tab': _L0_tok_in['fast_tab'], 'L0_tok_levy_tab': _L0_tok_in['levy_tab'], 'L0_tok_W_glove': _L0_tok_in['W_glove'], 'L0_tok_b_glove': _L0_tok_in['b_glove'], 'L0_tok_W_fast': _L0_tok_in['W_fast'], 'L0_tok_b_fast': _L0_tok_in['b_fast'], 'L0_tok_W_levy': _L0_tok_in['W_levy'], 'L0_tok_b_levy': _L0_tok_in['b_levy'], 'L0_tok_gW1_glove': _L0_tok_in['gW1_glove'], 'L0_tok_gb1_glove': _L0_tok_in['gb1_glove'], 'L0_tok_gW2_glove': _L0_tok_in['gW2_glove'], 'L0_tok_gb2_glove': _L0_tok_in['gb2_glove'], 'L0_tok_gW1_fast': _L0_tok_in['gW1_fast'], 'L0_tok_gb1_fast': _L0_tok_in['gb1_fast'], 'L0_tok_gW2_fast': _L0_tok_in['gW2_fast'], 'L0_tok_gb2_fast': _L0_tok_in['gb2_fast'], 'L0_tok_gW1_levy': _L0_tok_in['gW1_levy'], 'L0_tok_gb1_levy': _L0_tok_in['gb1_levy'], 'L0_tok_gW2_levy': _L0_tok_in['gW2_levy'], 'L0_tok_gb2_levy': _L0_tok_in['gb2_levy'], 'L0_attn_qkv_w': _L0_attn_in['qkv_w'], 'L0_attn_qkv_b': _L0_attn_in['qkv_b'], 'L0_attn_ln_g': _L0_attn_in['ln_g'], 'L0_attn_ln_b': _L0_attn_in['ln_b'], 'L0_attn_out_w': _L0_attn_in['out_w'], 'L0_attn_out_b': _L0_attn_in['out_b'], 'L0_ffn_gfc1_w': _L0_ffn_in['gfc1_w'], 'L0_ffn_gfc1_b': _L0_ffn_in['gfc1_b'], 'L0_ffn_gfc2_w': _L0_ffn_in['gfc2_w'], 'L0_ffn_gfc2_b': _L0_ffn_in['gfc2_b'], 'L0_ffn_W1': _L0_ffn_in['W1'], 'L0_ffn_b1': _L0_ffn_in['b1'], 'L0_ffn_W2': _L0_ffn_in['W2'], 'L0_ffn_b2': _L0_ffn_in['b2'], 'L0_ffn_ln_g': _L0_ffn_in['ln_g'], 'L0_ffn_ln_b': _L0_ffn_in['ln_b'], 'L0_ffn_tv_W1': _L0_ffn_in['tv_W1'], 'L0_ffn_tv_b1': _L0_ffn_in['tv_b1'], 'L0_ffn_tv_W2': _L0_ffn_in['tv_W2'], 'L0_ffn_tv_b2': _L0_ffn_in['tv_b2'], 'L0_ffn_tv_ln_g': _L0_ffn_in['tv_ln_g'], 'L0_ffn_tv_ln_b': _L0_ffn_in['tv_ln_b'], 'L1_attn_gamma': _L1_attn_in['gamma'], 'L1_attn_w_qkv': _L1_attn_in['w_qkv'], 'L1_attn_b_qkv': _L1_attn_in['b_qkv'], 'L1_attn_w_a': _L1_attn_in['w_a'], 'L1_attn_b_a': _L1_attn_in['b_a'], 'L1_attn_w_out': _L1_attn_in['w_out'], 'L1_attn_b_out': _L1_attn_in['b_out'], 'L1_ffn_gate_w': _L1_ffn_in['gate_w'], 'L1_ffn_w1': _L1_ffn_in['w1'], 'L1_ffn_b1': _L1_ffn_in['b1'], 'L1_ffn_w2': _L1_ffn_in['w2'], 'L1_ffn_b2': _L1_ffn_in['b2'], 'L1_ffn_ln_g': _L1_ffn_in['ln_g'], 'L1_ffn_ln_b': _L1_ffn_in['ln_b']}

def reference(x, L0_tok_glove_tab, L0_tok_fast_tab, L0_tok_levy_tab, L0_tok_W_glove, L0_tok_b_glove, L0_tok_W_fast, L0_tok_b_fast, L0_tok_W_levy, L0_tok_b_levy, L0_tok_gW1_glove, L0_tok_gb1_glove, L0_tok_gW2_glove, L0_tok_gb2_glove, L0_tok_gW1_fast, L0_tok_gb1_fast, L0_tok_gW2_fast, L0_tok_gb2_fast, L0_tok_gW1_levy, L0_tok_gb1_levy, L0_tok_gW2_levy, L0_tok_gb2_levy, L0_attn_qkv_w, L0_attn_qkv_b, L0_attn_ln_g, L0_attn_ln_b, L0_attn_out_w, L0_attn_out_b, L0_ffn_gfc1_w, L0_ffn_gfc1_b, L0_ffn_gfc2_w, L0_ffn_gfc2_b, L0_ffn_W1, L0_ffn_b1, L0_ffn_W2, L0_ffn_b2, L0_ffn_ln_g, L0_ffn_ln_b, L0_ffn_tv_W1, L0_ffn_tv_b1, L0_ffn_tv_W2, L0_ffn_tv_b2, L0_ffn_tv_ln_g, L0_ffn_tv_ln_b, L1_attn_gamma, L1_attn_w_qkv, L1_attn_b_qkv, L1_attn_w_a, L1_attn_b_a, L1_attn_w_out, L1_attn_b_out, L1_ffn_gate_w, L1_ffn_w1, L1_ffn_b1, L1_ffn_w2, L1_ffn_b2, L1_ffn_ln_g, L1_ffn_ln_b):
    import jax
    import jax.numpy as jnp

    def _L0_tok_ref(word, glove_tab, fast_tab, levy_tab, W_glove, b_glove, W_fast, b_fast, W_levy, b_levy, gW1_glove, gb1_glove, gW2_glove, gb2_glove, gW1_fast, gb1_fast, gW2_fast, gb2_fast, gW1_levy, gb1_levy, gW2_levy, gb2_levy):
        import jax, jax.numpy as jnp
        import numpy as np
        V, DIM, EMB, H = (25000, 75, 128, 10)
        B, S = (8, 512)

        def _gate(e, W1, b1, W2, b2):
            h = jnp.einsum('bsd,hd->bsh', e, W1) + b1
            return jnp.einsum('bsh,oh->bso', h, W2) + b2
        ge = glove_tab[word]
        fe = fast_tab[word]
        le = levy_tab[word]
        go = jnp.einsum('bsd,ed->bse', ge, W_glove) + b_glove
        fo = jnp.einsum('bsd,ed->bse', fe, W_fast) + b_fast
        lo = jnp.einsum('bsd,ed->bse', le, W_levy) + b_levy
        ga = _gate(ge, gW1_glove, gb1_glove, gW2_glove, gb2_glove)
        fa = _gate(fe, gW1_fast, gb1_fast, gW2_fast, gb2_fast)
        la = _gate(le, gW1_levy, gb1_levy, gW2_levy, gb2_levy)
        embed = jnp.stack([go, fo, lo], axis=2)
        alpha = jnp.concatenate([ga, fa, la], axis=2)
        alpha = jax.nn.softmax(alpha, axis=2)[..., None]
        return jnp.sum(alpha * embed, axis=2)

    def _L0_attn_ref(x, qkv_w, qkv_b, ln_g, ln_b, out_w, out_b):
        import math
        import jax, jax.numpy as jnp
        import numpy as np
        NUM_HEADS = 8
        ALPHA = 20.0
        LN_EPS = 1e-05

        def _forward(x, qkv_w, qkv_b, ln_g, ln_b, out_w, out_b):
            B, N, C = x.shape
            H = NUM_HEADS
            D = C // H
            qkv = x @ qkv_w + qkv_b
            q, k, v = jnp.split(qkv, 3, axis=-1)

            def to_heads(t):
                return t.reshape(B, N, H, D).transpose(0, 2, 1, 3)
            q, k, v = (to_heads(q), to_heads(k), to_heads(v))
            q_norm = jnp.linalg.norm(q, axis=-1, keepdims=True)
            k_norm = jnp.linalg.norm(k, axis=-1, keepdims=True)
            q_t = q / q_norm
            dq = jnp.tanh(q / q_norm * ALPHA) * (math.pi / 4)
            dk = jnp.tanh(k / k_norm * ALPHA) * (math.pi / 4)
            k3 = jnp.abs(k) ** 3
            kf = jnp.concatenate([k3 * jnp.cos(dk), k3 * jnp.sin(dk)], axis=-1)
            power = 1.5 * (0.5 + jnp.tanh(q_norm))
            q_t = (q_t ** 2) ** power
            qf = jnp.concatenate([q_t * jnp.cos(dq), q_t * jnp.sin(dq)], axis=-1)
            k_mean = jnp.mean(kf, axis=2, keepdims=True)
            z = 1.0 / (jnp.einsum('bhnf,bhmf->bhnm', qf, k_mean) + 1e-06)
            scale = N ** (-0.5)
            kv = jnp.einsum('bhnf,bhnd->bhfd', kf * scale, v * scale)
            out = jnp.einsum('bhnf,bhfd->bhnd', qf, kv) * z
            out = out.transpose(0, 2, 1, 3).reshape(B, N, C)
            mu = jnp.mean(out, axis=-1, keepdims=True)
            var = jnp.var(out, axis=-1, keepdims=True)
            out = (out - mu) * jax.lax.rsqrt(var + LN_EPS) * ln_g + ln_b
            return out @ out_w + out_b
        return _forward(x, qkv_w, qkv_b, ln_g, ln_b, out_w, out_b)

    def _L0_ffn_ref(hidden_states, gfc1_w, gfc1_b, gfc2_w, gfc2_b, W1, b1, W2, b2, ln_g, ln_b, tv_W1, tv_b1, tv_W2, tv_b2, tv_ln_g, tv_ln_b):
        import jax, jax.numpy as jnp
        import numpy as np
        B, S, D, F, E = (8, 1024, 128, 512, 8)
        INIT_LAMBDA = 0.2
        LN_EPS = 1e-05
        LN_MERGE = 0.03
        x = hidden_states
        gh = jax.nn.relu(jnp.einsum('bsd,hd->bsh', x, gfc1_w) + gfc1_b)
        g = (jnp.einsum('bsh,eh->bse', gh, gfc2_w) + gfc2_b).mean(axis=1)
        W1m = W1 + jnp.einsum('be,efd->bfd', g, tv_W1)
        b1m = b1 + g @ tv_b1
        W2m = W2 + jnp.einsum('be,edf->bdf', g, tv_W2)
        b2m = b2 + g @ tv_b2
        lng = ln_g + LN_MERGE * (tv_ln_g - ln_g).sum(axis=0)
        lnb = ln_b + LN_MERGE * (tv_ln_b - ln_b).sum(axis=0)
        h = jax.nn.relu(jnp.einsum('bsd,bfd->bsf', x, W1m) + b1m[:, None, :])
        out = jnp.einsum('bsf,bdf->bsd', h, W2m) + b2m[:, None, :]
        res = x + out
        mu = res.mean(axis=-1, keepdims=True)
        var = res.var(axis=-1, keepdims=True)
        return (res - mu) * jax.lax.rsqrt(var + LN_EPS) * lng + lnb

    def _L1_attn_ref(x, gamma, w_qkv, b_qkv, w_a, b_a, w_out, b_out):
        import jax, jax.numpy as jnp
        import numpy as np
        DIM = 128
        HEADS = 8
        DIM_HEAD = 64
        DIM_INNER = HEADS * DIM_HEAD
        FRAC_GRAD = 0.5
        SCALE = DIM_HEAD ** (-0.5)
        EPS_CUMPROD = 1e-10
        EPS_INV = 1e-08

        def _rms_norm(x, gamma):
            nrm = jnp.linalg.norm(x, axis=-1, keepdims=True)
            return x / jnp.maximum(nrm, 1e-12) * DIM ** 0.5 * gamma

        def _safe_cumprod(t, axis):
            t = jnp.clip(t, EPS_CUMPROD, 1.0)
            return jnp.exp(jnp.cumsum(jnp.log(t), axis=axis))
        b, n, _ = x.shape
        x = _rms_norm(x, gamma)
        qkv = x @ w_qkv + b_qkv
        qkv = qkv.reshape(b, n, 3, HEADS, DIM_HEAD).transpose(2, 0, 3, 1, 4)
        q, k, v = (qkv[0], qkv[1], qkv[2])
        q = q * SCALE
        a = (x @ w_a + b_a).reshape(b, n, HEADS, DIM_HEAD).transpose(0, 2, 1, 3)
        a = a * FRAC_GRAD + jax.lax.stop_gradient(a) * (1.0 - FRAC_GRAD)
        a = jax.nn.sigmoid(a)
        a_cum = _safe_cumprod(a, axis=-2)
        a_cum_inv = 1.0 / jnp.maximum(a_cum, EPS_INV)
        q = q * a_cum
        k = k * a_cum_inv
        sim = jnp.einsum('bhid,bhjd->bhij', q, k)
        causal_mask = jnp.triu(jnp.ones((n, n), dtype=bool), k=1)
        attn = jnp.where(causal_mask, 0.0, sim)
        out = jnp.einsum('bhij,bhjd->bhid', attn, v)
        out = out.transpose(0, 2, 1, 3).reshape(b, n, DIM_INNER)
        return out @ w_out + b_out

    def _L1_ffn_ref(x, gate_w, w1, b1, w2, b2, ln_g, ln_b):
        import jax, jax.numpy as jnp
        import numpy as np
        NUM_EXPERTS = 8
        TOP_K = 2
        LN_EPS = 1e-05

        def _layernorm(x, g, b):
            mu = jnp.mean(x, axis=-1, keepdims=True)
            var = jnp.mean(jnp.square(x - mu), axis=-1, keepdims=True)
            return (x - mu) * jax.lax.rsqrt(var + LN_EPS) * g + b
        B, S, D = x.shape
        E = gate_w.shape[1]
        x_norm = _layernorm(x, ln_g, ln_b)
        xf = x_norm.reshape(B * S, D)
        logits = xf @ gate_w
        probs = jax.nn.softmax(logits, axis=-1)
        dispatch_w, expert_idx = jax.lax.top_k(probs, TOP_K)
        combine = jnp.sum(jax.nn.one_hot(expert_idx, E, dtype=xf.dtype) * dispatch_w[..., None], axis=1)
        out = jnp.zeros_like(xf)
        for e in range(E):
            h = jax.nn.gelu(xf @ w1[e] + b1[e], approximate=False)
            y = h @ w2[e] + b2[e]
            out = out + combine[:, e:e + 1] * y
        return x + out.reshape(B, S, D)
    h = _L0_tok_ref(x, L0_tok_glove_tab, L0_tok_fast_tab, L0_tok_levy_tab, L0_tok_W_glove, L0_tok_b_glove, L0_tok_W_fast, L0_tok_b_fast, L0_tok_W_levy, L0_tok_b_levy, L0_tok_gW1_glove, L0_tok_gb1_glove, L0_tok_gW2_glove, L0_tok_gb2_glove, L0_tok_gW1_fast, L0_tok_gb1_fast, L0_tok_gW2_fast, L0_tok_gb2_fast, L0_tok_gW1_levy, L0_tok_gb1_levy, L0_tok_gW2_levy, L0_tok_gb2_levy)
    h = h + _L0_attn_ref(_layernorm(h, axis=-1), L0_attn_qkv_w, L0_attn_qkv_b, L0_attn_ln_g, L0_attn_ln_b, L0_attn_out_w, L0_attn_out_b)
    h = h + _L0_ffn_ref(_layernorm(h, axis=-1), L0_ffn_gfc1_w, L0_ffn_gfc1_b, L0_ffn_gfc2_w, L0_ffn_gfc2_b, L0_ffn_W1, L0_ffn_b1, L0_ffn_W2, L0_ffn_b2, L0_ffn_ln_g, L0_ffn_ln_b, L0_ffn_tv_W1, L0_ffn_tv_b1, L0_ffn_tv_W2, L0_ffn_tv_b2, L0_ffn_tv_ln_g, L0_ffn_tv_ln_b)
    h = h + _L1_attn_ref(_layernorm(h, axis=-1), L1_attn_gamma, L1_attn_w_qkv, L1_attn_b_qkv, L1_attn_w_a, L1_attn_b_a, L1_attn_w_out, L1_attn_b_out)
    h = h + _L1_ffn_ref(_layernorm(h, axis=-1), L1_ffn_gate_w, L1_ffn_w1, L1_ffn_b1, L1_ffn_w2, L1_ffn_b2, L1_ffn_ln_g, L1_ffn_ln_b)
    return h

_drawn_inputs = setup_inputs


def setup_inputs(seed=0):
    import zlib

    import numpy as np

    out = dict(_drawn_inputs(seed))
    spreads = {'L0_tok_b_glove': (0.0, 0.1),
     'L0_tok_b_fast': (0.0, 0.1),
     'L0_tok_b_levy': (0.0, 0.1),
     'L0_tok_gb1_glove': (0.0, 0.1),
     'L0_tok_gb1_fast': (0.0, 0.1),
     'L0_tok_gb1_levy': (0.0, 0.616),
     'L0_attn_qkv_b': (0.0, 0.1),
     'L0_attn_ln_g': (1.0, 0.2),
     'L0_attn_ln_b': (0.0, 0.1),
     'L0_attn_out_b': (0.0, 0.1),
     'L0_ffn_gfc1_b': (0.0, 0.8),
     'L0_ffn_gfc2_b': (0.20000000298023224, 0.6),
     'L0_ffn_b1': (0.0, 0.446),
     'L0_ffn_b2': (0.0, 0.289),
     'L0_ffn_ln_g': (1.0, 0.2),
     'L0_ffn_ln_b': (0.0, 0.1),
     'L1_attn_gamma': (1.0, 0.6),
     'L1_attn_b_qkv': (0.0, 0.382),
     'L1_attn_b_a': (2.0, 0.6),
     'L1_attn_b_out': (0.0, 0.1),
     'L1_ffn_b1': (0.0, 0.8),
     'L1_ffn_b2': (0.0, 0.8),
     'L1_ffn_ln_g': (1.0, 0.6),
     'L1_ffn_ln_b': (0.0, 0.8)}
    factors = {'L0_tok_gW1_glove': 8.0,
     'L0_tok_gW1_fast': 8.0,
     'L0_tok_gW2_fast': 5.443,
     'L0_tok_gW1_levy': 8.0,
     'L0_ffn_gfc1_w': 8.0,
     'L0_ffn_gfc2_w': 8.0,
     'L0_ffn_tv_W1': 3.121,
     'L0_ffn_tv_b1': 8.0,
     'L0_ffn_tv_b2': 8.0,
     'L0_ffn_tv_ln_g': 43.697,
     'L0_ffn_tv_ln_b': 42.631,
     'L1_attn_w_a': 5.15,
     'L1_ffn_gate_w': 8.0,
     'L1_ffn_w1': 8.0,
     'L1_ffn_w2': 8.0}
    for name, (base, spread) in spreads.items():
        noise = np.random.default_rng([zlib.crc32(name.encode()), seed]).standard_normal(out[name].shape)
        drawn = base * np.exp(spread * noise) if base else spread * noise
        out[name] = jnp.asarray(drawn.astype(out[name].dtype))
    for name, factor in factors.items():
        out[name] = (out[name] * factor).astype(out[name].dtype)
    return out
```

```python
from contextlib import ExitStack

import concourse.bass as bass
from concourse import mybir

ALU = mybir.AluOpType
ACT = mybir.ActivationFunctionType
F32 = mybir.dt.float32
I32 = mybir.dt.int32
X = mybir.AxisListType.X
HALF_PI = 1.5707963267948966

P = 128
B, S, D = 4, 512, 128
T = S // P
DIM, TABLES = 75, 3
GATE_H = 10
HEADS0 = 8
HD0 = D // HEADS0
E, FF = 8, 512
FC = FF // P
J = P // E
HEADS1, HD1 = 8, 64
PAIRS = HEADS1 * HD1 // P
EPS = 1e-5
LN_MERGE = 0.03
LN_INV_MAX = 18.420680743952367

STEPS = {
    "T.dve": ["prod", "sum", "bias", "max", "sub", "den", "rden", "alpha", "scaled", "h"],
    "T.act": ["exp", "eT1", "eT2"],
    "T.pe": ["tr1", "tr2", "h"],
    "A.dve": ["st%d" % t for t in range(T)] + ["mv%d" % t for t in range(T)] + ["x%d" % t for t in range(T)]
    + ["qkv%d" % t for t in range(T)],
    "A.pool": ["eps", "rstd", "hb"],
    "A.pe": ["tr"] + ["qkv%d" % t for t in range(T)],
    "A.act": ["xT"],
    "B.act": ["sq", "ln", "rn", "qn", "uu", "lnu", "kabs", "tq", "tanh", "qt", "sin", "cos"],
    "B.dve": ["n2", "u", "pw", "pl", "fs", "fc"],
    "B.pool": ["k3"],
    "C.pe": ["trc", "trs", "kv", "o0", "o1", "trn", "out"],
    "C.act": ["qc", "qs", "oT"],
    "C.dve": ["kv0", "kv1", "km0", "km1", "den0", "den1", "z", "o0", "o1"]
    + ["st%d" % t for t in range(T)] + ["mv%d" % t for t in range(T)] + ["x%d" % t for t in range(T)] + ["h"],
    "C.pool": ["eps", "rstd"],
    "D.dve": ["st%d" % t for t in range(T)] + ["mv%d" % t for t in range(T)] + ["x%d" % t for t in range(T)]
    + ["g", "sel", "gb", "w1", "w2", "b1", "b2"],
    "D.pool": ["eps", "rstd", "hb", "xb"],
    "D.pe": ["tr", "gh", "g", "w1", "w2", "b"],
    "D.act": ["xT", "gh"],
    "E.pe": ["up%d" % c for c in range(FC)] + ["down"],
    "E.act": ["ht%d" % c for c in range(FC)],
    "E.dve": ["res"] + ["st%d" % t for t in range(T)] + ["mv%d" % t for t in range(T)]
    + ["x%d" % t for t in range(T)] + ["g", "h"],
    "E.pool": ["eps", "rstd"],
    "F.dve": ["st%d" % t for t in range(T)] + ["mv%d" % t for t in range(T)] + ["lo", "var"]
    + ["x%d" % t for t in range(T)] + ["e"] + ["v%d" % t for t in range(T)] + ["sum%d" % p for p in range(PAIRS)]
    + ["cut"] + [x % p for p in range(PAIRS) for x in ("qa%d", "qb%d", "k%d")],
    "F.pool": ["rstd", "hb"],
    "F.pe": ["tr"] + ["a%d" % p for p in range(PAIRS)] + ["v%d" % t for t in range(T)]
    + [x % p for p in range(PAIRS) for x in ("q%d", "k%d")],
    "F.act": ["xT"] + ["e%d" % p for p in range(PAIRS)] + ["l", "cum", "inv"],
    "G.pe": ["tr", "qk0", "qk1", "av", "kv", "out"],
    "G.act": ["kt", "o", "s"],
    "G.dve": ["m0", "m1", "h"],
    "I.dve": ["st%d" % t for t in range(T)] + ["mv%d" % t for t in range(T)] + ["x%d" % t for t in range(T)]
    + ["y%d" % t for t in range(T)] + ["h", "max", "sub", "den", "rden", "p"] + ["top%d" % t for t in range(T)]
    + ["at%d" % t for t in range(T)] + ["is0", "is1", "c0", "c1", "c"],
    "I.pool": ["ve", "vv", "rstd"],
    "I.pe": ["tr", "lg", "cT", "b2"],
    "I.act": ["xT", "exp", "cT"],
    "I.dve2": ["h"],
    "J.pe": ["up%d" % c for c in range(FC)] + ["down"],
    "J.act": ["ht%d" % c for c in range(FC)],
    "J.dve": ["y%d" % t for t in range(T)],
}


def lm_tower(nc, a, out, dbg=None):
    ctx = ExitStack()
    with ctx:
        def sb(name, shape, dt=F32):
            return ctx.enter_context(nc.sbuf_tensor(name, shape, dt))

        sem = {name: ctx.enter_context(nc.semaphore(name.replace(".", "_"))) for name in STEPS}

        def count(step, b):
            section, engine, what = step.split(".")
            steps = STEPS[section + "." + engine]
            return b * len(steps) + steps.index(what) + 1

        def wait(eng, step, b):
            if b >= 0:
                eng.wait_ge(sem[step.rsplit(".", 1)[0]], count(step, b))

        emitted = {}

        def did(ins, step, b):
            name = step.rsplit(".", 1)[0]
            emitted[name] = emitted.get(name, 0) + 1
            assert emitted[name] == count(step, b), (step, b, emitted[name])
            ins.then_inc(sem[name], 1)

        def carve(arena, size):
            used = [0]

            def take(shape):
                n = 1
                for k in shape[1:]:
                    n *= k
                view = arena[0:shape[0], used[0]:used[0] + n]
                used[0] += n
                assert used[0] <= size, used[0]
                if len(shape) == 3:
                    view = view.rearrange("p (a b) -> p a b", a=shape[1])
                elif len(shape) == 4:
                    view = view.rearrange("p (a b c) -> p a b c", a=shape[1], b=shape[2])
                return view
            return take

        h = sb("h", [P, B * T, D])
        ident = sb("ident", [P, P])
        idx = sb("idx", [P, B * T], I32)
        ES = TABLES * DIM + TABLES

        SIZE1 = 8448
        arena1 = sb("arena1", [P, SIZE1])
        take = carve(arena1, SIZE1)
        e_in = [take([P, T, TABLES * DIM]) for i in range(B)]
        e_sc = [take([P, T, ES]) for i in range(2)]
        e_pr = take([P, T, TABLES * DIM])
        eT1 = [take([P, S]) for i in range(2)]
        eT2 = [take([ES - P, S]) for i in range(2)]
        take = carve(arena1, SIZE1)
        ht = [take([P, FC, S]) for i in range(2)]
        w1m = [take([P, FF]) for i in range(2)]
        w2m = [take([P, FF]) for i in range(2)]
        res = take([P, T, D])
        rn = take([P, T, D])
        wide = take([P, D])
        junk = take([P, S])
        gb = take([P, P])

        take = carve(arena1, SIZE1)
        kt = [take([P, PAIRS, P]) for i in range(2)]
        sim = [take([P, PAIRS, 2, P]) for i in range(2)]
        oc = [take([P, PAIRS, P]) for i in range(2)]
        ss = [take([P, PAIRS, P]) for i in range(2)]

        gatev = sb("gatev", [P, TABLES, DIM + 1])
        gw1 = sb("gw1", [GATE_H, TABLES, DIM + 1])
        gw2 = sb("gw2", [GATE_H, TABLES])
        gw2b = sb("gw2b", [GATE_H, TABLES, P])
        gb2 = sb("gb2", [P, TABLES])
        lg = [sb("lg%d" % i, [P, 5, T, TABLES]) for i in range(2)]
        wtok1 = sb("wtok1", [P, D])
        wtok2 = sb("wtok2", [ES - P, D])
        stat = [sb("stat%d" % i, [P, T, 6]) for i in range(2)]
        mv = [sb("mv%d" % i, [P, T, 2]) for i in range(2)]
        rstd = [sb("rstd%d" % i, [P, 2, T]) for i in range(2)]
        ve = [sb("ve%d" % i, [P, 2, T]) for i in range(2)]
        stat_o = sb("stat_o", [P, T, 6])
        mv_o = sb("mv_o", [P, T, 2])
        ve_o = sb("ve_o", [P, T])
        rstd_o = sb("rstd_o", [P, T])
        mhalf = sb("mhalf", [P, 2, T])
        xn = [sb("xn%d" % i, [P, T, D]) for i in range(2)]
        xT = [sb("xT%d" % i, [P, S]) for i in range(2)]
        half_pi = sb("half_pi", [P, 1])
        tiny = sb("tiny", [P, 1])
        wqkv0 = sb("wqkv0", [P, 3 * D])
        bqkv0 = sb("bqkv0", [P, 3 * D])
        wo0 = sb("wo0", [P, D])
        bo0 = sb("bo0", [P, D])
        lngb0 = sb("lngb0", [P, 2])
        blk = sb("blk", [P, D + HEADS0])

        SIZE2 = 20 * 1024 + 512
        arena2 = sb("arena2", [P, SIZE2])
        take = carve(arena2, SIZE2)
        qkv = [take([P, T, 3 * D + 1]) for i in range(2)]
        sq = [take([P, T, 2 * D]) for i in range(2)]
        n2 = [take([P, 4, T * 16]) for i in range(2)]
        u = take([P, T, 2 * D])
        pw = take([P, T * HEADS0])
        lnu = take([P, T, D])
        kab = take([P, T, D])
        tq = take([P, T, HEADS0])
        th = take([P, T, 2 * D])
        amp = take([P, T, 2 * D])
        fs = [take([P, T, 2 * D]) for i in range(2)]
        fc = [take([P, T, 2 * D]) for i in range(2)]
        sn = take([P, T, 2 * D])
        cs = take([P, T, 2 * D])
        qc = take([P, S])
        qs = take([P, S])
        kvm = take([P, 2, D + HEADS0])
        den = take([P, T * HEADS0])
        rden = take([P, T * HEADS0])
        o = take([P, T, D])
        on = take([P, T, D])
        oT = take([P, S])
        take = carve(arena2, SIZE2)
        qz = [take([P, PAIRS, 2, S]) for i in range(2)]
        kk = [take([P, PAIRS, S]) for i in range(2)]
        vv = [take([P, T, HEADS1 * HD1]) for i in range(2)]
        la = take([P, PAIRS, S])
        lb = take([P, PAIRS, S])
        xf = [la[:, i, :] for i in range(B)]

        big = sb("big", [P, 2 * E * FF])
        tv1 = big[:, 0:E * FF].rearrange("p (i f) -> p i f", i=E)
        tv2 = big[:, E * FF:].rearrange("p (i f) -> p i f", i=E)
        ew1 = tv1
        ew2 = tv2
        w1t = sb("w1t", [P, FF])
        w2t = sb("w2t", [P, FF])
        g1t = sb("g1t", [P, D])
        g2r = sb("g2r", [P, P])
        gcol = sb("gcol", [P, 2])
        tvb1 = sb("tvb1", [P, FF])
        tvb2 = sb("tvb2", [P, D])
        b1t = sb("b1t", [P, FC])
        b2w = sb("b2w", [P, D])
        sel = sb("sel", [P, 2, 2 * J])
        lnr = sb("lnr", [E + 1, 2 * D])
        lnco = sb("lnco", [E + 1, P])
        lnw = sb("lnw", [P, 2, D])
        gs = [sb("gs%d" % i, [P, 1]) for i in range(2)]
        grow = [sb("grow%d" % i, [P, 1]) for i in range(2)]
        selg = [sb("selg%d" % i, [P, 2, 2 * J]) for i in range(2)]
        b1m = [sb("b1m%d" % i, [P, FC]) for i in range(2)]
        xb = sb("xb", [P, T, D])

        wq = sb("wq", [P, 4 * 512])
        wo1 = sb("wo1", [P, PAIRS, D])
        bq1 = sb("bq1", [P, 3, PAIRS])
        nba = sb("nba", [P, PAIRS])
        bv1 = sb("bv1", [P, HEADS1 * HD1])
        bo1 = sb("bo1", [P, D])
        gam = sb("gam", [P, 1])
        gam2 = sb("gam2", [P, 1])
        causal = sb("causal", [P, 4 * P])
        low = sb("low", [P, T])

        gate = sb("gate", [P, E])
        lngb1 = sb("lngb1", [P, 2])
        eb1 = sb("eb1", [P, E, FC])
        eb2 = sb("eb2", [E, D])
        iota = sb("iota", [P, E])
        rt = sb("rt", [P, 8, T, E])
        rix = sb("rix", [P, T, E], mybir.dt.uint32)
        r1 = sb("r1", [P, 4, T])
        cmb = [sb("cmb%d" % i, [P, T, E]) for i in range(B)]
        cT = sb("cT", [E, S])
        one = sb("one", [P, 1])

        bank = [ctx.enter_context(nc.psum_tensor("bank%d" % i, [P, S], F32)) for i in range(8)]
        READ = {"T.tr1": "T.act.eT1", "T.tr2": "T.act.eT2", "T.h": "T.dve.h", "A.tr": "A.act.xT",
                "C.trc": "C.act.qc", "C.trs": "C.act.qs", "C.kv": "C.dve.km1", "C.o0": "C.dve.o0",
                "C.o1": "C.dve.o1", "C.trn": "C.act.oT", "C.out": "C.dve.h",
                "D.tr": "D.act.xT", "D.gh": "D.act.gh", "D.g": "D.dve.g", "D.w1": "D.dve.w1", "D.w2": "D.dve.w2",
                "D.b": "D.dve.b2", "E.down": "E.dve.res", "F.tr": "F.act.xT", "G.tr": "G.act.kt",
                "G.qk0": "G.dve.m0", "G.qk1": "G.dve.m1", "G.av": "G.act.o", "G.out": "G.dve.h",
                "I.tr": "I.act.xT", "I.lg": "I.dve.sub", "I.cT": "I.act.cT", "I.b2": "I.dve2.h",
                "J.down": "J.dve.y3"}
        READ.update({"E.up%d" % c: "E.act.ht%d" % c for c in range(FC)})
        READ.update({"J.up%d" % c: "J.act.ht%d" % c for c in range(FC)})
        READ.update({"F.a%d" % p: "F.act.e%d" % p for p in range(PAIRS)})
        READ.update({"F.v%d" % t: "F.dve.v%d" % t for t in range(T)})
        READ.update({"F.q%d" % p: "F.dve.qb%d" % p for p in range(PAIRS)})
        READ.update({"F.k%d" % p: "F.dve.k%d" % p for p in range(PAIRS)})
        READ.update({"A.qkv%d" % t: "A.dve.qkv%d" % t for t in range(T)})
        GROUPS = {("T", 3): ["tr1", "tr2"], ("T", 5): ["h"], ("A", 3): ["tr"],
                  ("A", 5): ["qkv%d" % t for t in range(T)],
                  ("C", 0): ["trc", "trs", "kv"], ("C", 2): ["o0", "o1"], ("C", 6): ["trn"], ("C", 8): ["out"],
                  ("D", 3): ["tr"], ("D", 5): ["gh"], ("D", 7): ["g"], ("D", 9): ["w1", "w2", "b"],
                  ("E", 0): ["up0", "up1"], ("E", 1): ["up2", "up3"], ("E", 3): ["down"],
                  ("F", 3): ["tr"], ("F", 5): ["a%d" % p for p in range(PAIRS)], ("F", 6): ["v%d" % t for t in range(T)],
                  ("F", 12): ["q0", "k0"], ("F", 13): ["q1", "k1"], ("F", 14): ["q2", "k2"], ("F", 15): ["q3", "k3"],
                  ("G", 0): ["tr", "qk0", "qk1"], ("G", 2): ["av"], ("G", 4): ["out"],
                  ("I", 3): ["tr"], ("I", 5): ["lg"], ("I", 9): ["cT"], ("I", 11): ["b2"],
                  ("J", 0): ["up%d" % c for c in range(FC)], ("J", 2): ["down"]}
        PHASES = {"T": 7, "A": 7, "B": 8, "C": 10, "D": 12, "E": 8, "F": 17, "G": 6, "I": 13, "J": 4}
        starts = []
        for b in range(B):
            for s, at in (("T", 0), ("A", 7), ("B", 14), ("C", 22)):
                starts.append((at + 8 * b, 1, s, b))
        at = 32 + 8 * (B - 1)
        for b in range(B):
            starts.append((at + 10 * b, 1, "D", b))
            starts.append((at + 10 * b + 12, 1, "E", b))
        at += 10 * (B - 1) + 12 + 8
        for b in range(B):
            starts.append((at + 18 * b, 1, "F", b))
            for c in range(T):
                starts.append((at + 18 * b + 17 + 4 * c, 1, "G", b * T + c))
        at += 18 * (B - 1) + 17 + 18
        for b in range(B):
            starts.append((at + 8 * b, 1, "I", b))
        at += 8 * (B - 1) + 13
        for n in range(B * E):
            starts.append((at + 2 * n, 1, "J", n))
        order = sorted((at + k * ph, n, s, b, ph) for n, (at, k, s, b) in enumerate(starts) for ph in range(PHASES[s]))
        order = [x[2:] for x in order]
        RING = 7
        place = {}
        ring = [g for s, b, ph in order for g in [(s + "." + x, b) for x in GROUPS.get((s, ph), [])]]
        for i, (g, b) in enumerate(ring):
            place[g, b] = (bank[i % RING], ring[i - RING] if i >= RING else None)

        def room(pe, g, b):
            at, last = place[g, b]
            if last:
                wait(pe, READ[last[0]], last[1])
            else:
                pe.wait_ge(s_banks, 1)
            return at

        def of(g, b):
            return place[g, b][0]

        s_const = ctx.enter_context(nc.semaphore("s_const"))
        s_ident = ctx.enter_context(nc.semaphore("s_ident"))
        s_banks = ctx.enter_context(nc.semaphore("s_banks"))
        s_gather = [ctx.enter_context(nc.semaphore("s_gather%d" % b)) for b in range(B)]
        s_idx = ctx.enter_context(nc.semaphore("s_idx"))
        s_wtok = ctx.enter_context(nc.semaphore("s_wtok"))
        s_w0 = ctx.enter_context(nc.semaphore("s_w0"))
        s_w1 = ctx.enter_context(nc.semaphore("s_w1"))
        s_w2 = ctx.enter_context(nc.semaphore("s_w2"))
        s_w3 = ctx.enter_context(nc.semaphore("s_w3"))
        s_lnw = ctx.enter_context(nc.semaphore("s_lnw"))
        s_lnb = ctx.enter_context(nc.semaphore("s_lnb"))
        s_qz = ctx.enter_context(nc.semaphore("s_qz"))
        s_gam = ctx.enter_context(nc.semaphore("s_gam"))
        s_gw2b = ctx.enter_context(nc.semaphore("s_gw2b"))
        s_gv = ctx.enter_context(nc.semaphore("s_gv"))
        s_gatev = ctx.enter_context(nc.semaphore("s_gatev"))
        s_out = ctx.enter_context(nc.semaphore("s_out"))
        block = ctx.enter_context(nc.Block())

        def row(name, n):
            return a[name].rearrange("(o n) -> o n", o=1).to_broadcast([P, n])

        @block.sync
        def _(sp):
            sp.dma_start(idx[:], a["idx"]).then_inc(s_idx, 16)
            for dst, src in ((gw1, a["gw1"]), (gw2, a["gw2"]), (gb2, row("gb2", TABLES)),
                             (wtok1, a["wtok"][0:P, :]), (wtok2, a["wtok"][P:ES, :]), (lnr, a["lnr"])):
                sp.dma_start(dst[:], src).then_inc(s_wtok, 16)
            for dst, src in ((wqkv0, a["wqkv0"]), (bqkv0, row("bqkv0", 3 * D)), (wo0, a["wo0"]),
                             (bo0, row("bo0", D)), (lngb0, a["lngb0"])):
                sp.dma_start(dst[:], src).then_inc(s_w0, 16)
            for dst, src in ((g1t, a["g1t"]), (g2r, a["g2r"]), (gcol, a["gcol"]), (w1t, a["w1t"]), (w2t, a["w2t"]),
                             (tvb2[0:P:J, :], a["tvb2"]), (tvb1[0:P:J, :], a["tvb1"]), (b1t, a["b1t"]),
                             (b2w, row("b2", D)), (sel, a["sel"]), (tv1, a["tv1"]), (tv2, a["tv2"])):
                if src is a["tvb2"]:
                    sp.wait_ge(s_const, 2)
                sp.dma_start(dst[:], src).then_inc(s_w1, 16)
            for dst, src in ((wq, a["wq"]), (wo1, a["wo1"]), (bq1, a["bq1"]), (bv1, row("bv1", HEADS1 * HD1)),
                             (bo1, row("bo1", D)), (gam, a["gam"]), (causal, a["causal"])):
                sp.dma_start(dst[:], src).then_inc(s_w2, 16)
            for dst, src in ((gate, a["gate"]), (lngb1, a["lngb1"]), (eb1, a["eb1"]), (eb2, a["eb2"]), (iota, a["iota"])):
                sp.dma_start(dst[:], src).then_inc(s_w3, 16)
            wait(sp, "D.pe.w2", B - 1)
            sp.dma_start(ew1, a["ew1"]).then_inc(s_w3, 16)
            sp.dma_start(ew2, a["ew2"]).then_inc(s_w3, 16)
            for b in range(B):
                wait(sp, "J.dve.y3", E * b + E - 1)
                sp.dma_start(out[b * S:(b + 1) * S, :].rearrange("(t p) d -> p t d", p=P),
                             h[:, b * T:(b + 1) * T, :]).then_inc(s_out, 16)
            sp.wait_ge(s_out, 16 * B)

        def each(order, programs):
            for section, b, ph in order:
                if section in programs:
                    programs[section](b, ph)

        @block.gpsimd
        def _(pool):
            pool.memset(ident[:], 0.0).then_inc(s_ident, 1)
            pool.memset(tvb1[:], 0.0).then_inc(s_const, 1)
            pool.memset(tvb2[:], 0.0).then_inc(s_const, 1)
            pool.memset(lnco[:], 1.0 - E * LN_MERGE).then_inc(s_const, 1)
            pool.wait_ge(s_const, 3)
            pool.memset(lnco[0:E, :], LN_MERGE).then_inc(s_const, 1)
            pool.memset(blk[:], 1.0 / S).then_inc(s_const, 1)
            pool.memset(mhalf[:], -0.5).then_inc(s_const, 1)
            pool.memset(half_pi[:], HALF_PI).then_inc(s_const, 1)
            pool.memset(tiny[:], 1e-19).then_inc(s_const, 1)
            pool.memset(one[:], 1.0).then_inc(s_const, 1)
            for i in range(2):
                pool.memset(qkv[i][:, :, 3 * D:3 * D + 1], 1.0).then_inc(s_const, 1)
            pool.wait_ge(s_ident, 1)
            pool.affine_select(out=ident[:], in_=ident[:], compare_op=ALU.not_equal, fill=1.0, base=0,
                               pattern=[[-1, P]], channel_multiplier=1).then_inc(s_ident, 1)
            pool.wait_ge(s_const, 11)
            for cols, step in ((blk[:, 0:D].rearrange("p (g c) -> p g c", c=HD0), 1), (blk[:, D:].unsqueeze(2), 1)):
                w = cols.shape[2]
                pool.affine_select(out=cols, in_=cols, compare_op=ALU.is_ge, fill=0.0, base=0,
                                   pattern=[[-HD0, HEADS0], [0, w]], channel_multiplier=1).then_inc(s_const, 1)
            pool.wait_ge(s_const, 13)
            for cols in (blk[:, 0:D].rearrange("p (g c) -> p g c", c=HD0), blk[:, D:].unsqueeze(2)):
                w = cols.shape[2]
                pool.affine_select(out=cols, in_=cols, compare_op=ALU.is_ge, fill=0.0, base=HD0 - 1,
                                   pattern=[[HD0, HEADS0], [0, w]], channel_multiplier=-1).then_inc(s_const, 1)
            pool.wait_ge(s_idx, 16)
            for b in range(B):
                for t in range(T):
                    pool.indirect_dma_start(
                        e_in[b][:, t, :], None, a["tables"],
                        bass.IndirectOffsetOnAxis(ap=idx[:, b * T + t:b * T + t + 1], axis=0)).then_inc(s_gather[b], 16)

            def section_A(b, ph):
                i = b % 2
                if ph == 1:
                    wait(pool, "A.dve.mv3", b)
                    did(pool.tensor_scalar(ve[i][:, 0], mv[i][:, :, 1], EPS, None, ALU.add), "A.pool.eps", b)
                    wait(pool, "A.pool.eps", b)
                    did(pool.tensor_tensor(rstd[i][:, 0], ve[i][:, 0], mhalf[:, 0], ALU.pow), "A.pool.rstd", b)
                if ph == 3:
                    if b == 0:
                        pool.wait_ge(s_w0, 16 * 5)
                    wait(pool, "A.dve.x3", b)
                    hb = h[:, b * T:(b + 1) * T, :]
                    did(pool.tensor_tensor(hb, hb, bo0[:].unsqueeze(1).to_broadcast([P, T, D]), ALU.add), "A.pool.hb", b)

            def section_B(b, ph):
                i = b % 2
                if ph == 5:
                    wait(pool, "B.act.kabs", b)
                    wait(pool, "B.act.sq", b)
                    wait(pool, "B.dve.fc", b - 1)
                    did(pool.tensor_tensor(amp[:, :, D:], kab[:], sq[i][:, :, D:], ALU.mult), "B.pool.k3", b)

            def section_C(b, ph):
                if ph == 4:
                    wait(pool, "C.dve.mv3", b)
                    did(pool.tensor_scalar(ve_o[:], mv_o[:, :, 1], EPS, None, ALU.add), "C.pool.eps", b)
                    wait(pool, "C.pool.eps", b)
                    did(pool.tensor_tensor(rstd_o[:], ve_o[:], mhalf[:, 0], ALU.pow), "C.pool.rstd", b)

            def section_D(b, ph):
                i = b % 2
                hb = h[:, b * T:(b + 1) * T, :]
                if ph == 1:
                    wait(pool, "D.dve.mv3", b)
                    did(pool.tensor_scalar(ve[i][:, 0], mv[i][:, :, 1], EPS, None, ALU.add), "D.pool.eps", b)
                    wait(pool, "D.pool.eps", b)
                    did(pool.tensor_tensor(rstd[i][:, 0], ve[i][:, 0], mhalf[:, 0], ALU.pow), "D.pool.rstd", b)
                if ph == 3:
                    pool.wait_ge(s_lnb, 1)
                    wait(pool, "D.dve.x3", b)
                    did(pool.tensor_tensor(hb, hb, lnw[:, 1, :].unsqueeze(1).to_broadcast([P, T, D]), ALU.add),
                        "D.pool.hb", b)
                if ph == 11:
                    wait(pool, "D.dve.b2", b)
                    wait(pool, "E.dve.res", b - 1)
                    did(pool.tensor_tensor(xb[:], xn[i][:], wide[:].unsqueeze(1).to_broadcast([P, T, D]), ALU.add),
                        "D.pool.xb", b)

            def section_E(b, ph):
                if ph == 5:
                    wait(pool, "E.dve.mv3", b)
                    did(pool.tensor_scalar(ve_o[:], mv_o[:, :, 1], EPS, None, ALU.add), "E.pool.eps", b)
                    wait(pool, "E.pool.eps", b)
                    did(pool.tensor_tensor(rstd_o[:], ve_o[:], mhalf[:, 0], ALU.pow), "E.pool.rstd", b)

            def section_F(b, ph):
                i = b % 2
                hb = h[:, b * T:(b + 1) * T, :]
                if ph == 0:
                    if b == 0:
                        wait(pool, "C.dve.h", B - 1)
                        for j in range(2):
                            pool.memset(qz[j], 0.0).then_inc(s_qz, 1)
                if ph == 1:
                    wait(pool, "F.dve.var", b)
                    did(pool.tensor_tensor(rstd[i][:, 0], ve[i][:, 1], mhalf[:, 0], ALU.pow), "F.pool.rstd", b)
                if ph == 3:
                    if b == 0:
                        pool.wait_ge(s_w2, 16 * 7)
                    wait(pool, "F.dve.x3", b)
                    did(pool.tensor_tensor(hb, hb, bo1[:].unsqueeze(1).to_broadcast([P, T, D]), ALU.add), "F.pool.hb", b)

            def section_I(b, ph):
                i = b % 2
                if ph == 1:
                    wait(pool, "I.dve.mv3", b)
                    did(pool.tensor_scalar(ve[i][:, 0], mv[i][:, :, 1], EPS, None, ALU.add), "I.pool.ve", b)
                    did(pool.tensor_scalar(ve[i][:, 1], mv[i][:, :, 1], 1.0 + EPS, EPS * EPS, ALU.mult, ALU.add),
                        "I.pool.vv", b)
                    wait(pool, "I.pool.vv", b)
                    did(pool.tensor_tensor(rstd[i][:], ve[i][:], mhalf[:], ALU.pow), "I.pool.rstd", b)

            each(order, {"A": section_A, "B": section_B, "C": section_C, "D": section_D, "E": section_E,
                         "F": section_F, "I": section_I})

        @block.tensor
        def _(pe):
            pe.wait_ge(s_gw2b, 1)
            for t in range(TABLES):
                last = pe.matmul(bank[7][:, t * (DIM + 1):(t + 1) * (DIM + 1)], gw2b[:, t, :], gw1[:, t, :],
                                 start=True, stop=True)
            last.then_inc(s_gv, 1)
            pe.wait_ge(s_ident, 2)
            pe.wait_ge(s_wtok, 16 * 6)
            pe.wait_ge(s_const, 4)
            pe.matmul(bank[6][:, 0:2 * D], lnco[:], lnr[:], start=True, stop=True).then_inc(s_lnw, 1)

            def section_T(b, ph):
                i = b % 2
                if ph == 3:
                    p1 = room(pe, "T.tr1", b)
                    wait(pe, "T.dve.scaled", b)
                    for t in range(T):
                        last = pe.transpose(p1[:, t * P:(t + 1) * P], e_sc[i][:, t, 0:P], ident[:])
                    did(last, "T.pe.tr1", b)
                    p2 = room(pe, "T.tr2", b)
                    for t in range(T):
                        last = pe.transpose(p2[0:ES - P, t * P:(t + 1) * P], e_sc[i][:, t, P:ES], ident[:])
                    did(last, "T.pe.tr2", b)
                if ph == 5:
                    p3 = room(pe, "T.h", b)
                    if b == 0:
                        pe.wait_ge(s_wtok, 16 * 6)
                    wait(pe, "T.act.eT1", b)
                    wait(pe, "T.act.eT2", b)
                    for t in range(T):
                        tk = slice(t * P, (t + 1) * P)
                        pe.matmul(p3[:, tk], eT1[i][:, tk], wtok1[:], start=True, stop=False)
                        last = pe.matmul(p3[:, tk], eT2[i][:, tk], wtok2[:], start=False, stop=True)
                    did(last, "T.pe.h", b)

            def section_A(b, ph):
                i = b % 2
                if ph == 3:
                    p = room(pe, "A.tr", b)
                    wait(pe, "A.dve.x3", b)
                    for t in range(T):
                        last = pe.transpose(p[:, t * P:(t + 1) * P], xn[i][:, t, :], ident[:])
                    did(last, "A.pe.tr", b)
                if ph == 5:
                    if b == 0:
                        pe.wait_ge(s_w0, 16 * 5)
                    for t in range(T):
                        p = room(pe, "A.qkv%d" % t, b)
                        wait(pe, "A.act.xT", b)
                        did(pe.matmul(p[:, 0:3 * D], xT[i][:, t * P:(t + 1) * P], wqkv0[:], start=True, stop=True),
                            "A.pe.qkv%d" % t, b)

            def section_C(b, ph):
                i = b % 2
                if ph == 0:
                    p = room(pe, "C.trc", b)
                    wait(pe, "B.dve.fc", b)
                    for t in range(T):
                        last = pe.transpose(p[:, t * P:(t + 1) * P], fc[i][:, t, 0:D], ident[:])
                    did(last, "C.pe.trc", b)
                    p = room(pe, "C.trs", b)
                    for t in range(T):
                        last = pe.transpose(p[:, t * P:(t + 1) * P], fs[i][:, t, 0:D], ident[:])
                    did(last, "C.pe.trs", b)
                    p = room(pe, "C.kv", b)
                    for half, f in enumerate((fc, fs)):
                        for t in range(T):
                            last = pe.matmul(p[:, half * (D + 1):(half + 1) * (D + 1)], f[i][:, t, D:2 * D],
                                             qkv[i][:, t, 2 * D:3 * D + 1], start=(t == 0), stop=(t == T - 1))
                    did(last, "C.pe.kv", b)
                if ph == 2:
                    for n in range(2):
                        p = room(pe, "C.o%d" % n, b)
                        wait(pe, "C.act.qs", b)
                        wait(pe, "C.dve.km1", b)
                        for j in range(2):
                            t = 2 * n + j
                            at = p[:, j * (D + HEADS0):(j + 1) * (D + HEADS0)]
                            pe.matmul(at, qc[:, t * P:(t + 1) * P], kvm[:, 0, :], start=True, stop=False)
                            last = pe.matmul(at, qs[:, t * P:(t + 1) * P], kvm[:, 1, :], start=False, stop=True)
                        did(last, "C.pe.o%d" % n, b)
                if ph == 6:
                    p = room(pe, "C.trn", b)
                    wait(pe, "C.dve.x3", b)
                    for t in range(T):
                        last = pe.transpose(p[:, t * P:(t + 1) * P], on[:, t, :], ident[:])
                    did(last, "C.pe.trn", b)
                if ph == 8:
                    p = room(pe, "C.out", b)
                    wait(pe, "C.act.oT", b)
                    for t in range(T):
                        last = pe.matmul(p[:, t * P:(t + 1) * P], oT[:, t * P:(t + 1) * P], wo0[:], start=True, stop=True)
                    did(last, "C.pe.out", b)

            def section_D(b, ph):
                i = b % 2
                if ph == 3:
                    p = room(pe, "D.tr", b)
                    wait(pe, "D.dve.x3", b)
                    for t in range(T):
                        last = pe.transpose(p[:, t * P:(t + 1) * P], xn[i][:, t, :], ident[:])
                    did(last, "D.pe.tr", b)
                if ph == 5:
                    p = room(pe, "D.gh", b)
                    if b == 0:
                        pe.wait_ge(s_w1, 16 * 12)
                    wait(pe, "D.act.xT", b)
                    did(pe.matmul(p[:], g1t[:], xT[i][:], start=True, stop=True), "D.pe.gh", b)
                if ph == 7:
                    p = room(pe, "D.g", b)
                    wait(pe, "D.act.gh", b)
                    did(pe.matmul(p[:, 0:1], g2r[:], gs[i][:], start=True, stop=True), "D.pe.g", b)
                if ph == 9:
                    for name, w in (("w1", tv1), ("w2", tv2)):
                        p = room(pe, "D." + name, b)
                        wait(pe, "D.dve.sel", b)
                        for r in range(2):
                            for c in range(4):
                                last = pe.matmul(p[2 * J * c:2 * J * (c + 1), :], selg[i][:, r, :], w[:, 2 * c + r, :],
                                                 start=(r == 0), stop=(r == 1), skip_group_check=True)
                        did(last, "D.pe." + name, b)
                    p = room(pe, "D.b", b)
                    wait(pe, "D.dve.gb", b)
                    for c in range(FC):
                        pe.matmul(p[:, c:c + 1], tvb1[:, c * P:(c + 1) * P], grow[i][:], start=True, stop=True)
                    did(pe.matmul(p[:, P:2 * P], gb[:], tvb2[:], start=True, stop=True), "D.pe.b", b)

            def feed(name, n, x, w1, w2, hid, ph, last_x):
                if ph < 2:
                    for c in (range(FC) if name == "J" else range(2 * ph, 2 * ph + 2)):
                        p = room(pe, "%s.up%d" % (name, c), n)
                        if last_x:
                            wait(pe, *last_x)
                        did(pe.matmul(p[:], w1[:, c * P:(c + 1) * P], x, start=True, stop=True),
                            "%s.pe.up%d" % (name, c), n)
                else:
                    p = room(pe, name + ".down", n)
                    wait(pe, "%s.act.ht3" % name, n)
                    for t in range(T):
                        for c in range(FC):
                            last = pe.matmul(p[:, t * P:(t + 1) * P], hid[:, c, t * P:(t + 1) * P],
                                             w2[:, c * D:(c + 1) * D], start=(c == 0), stop=(c == FC - 1))
                    did(last, name + ".pe.down", n)

            def section_E(b, ph):
                i = b % 2
                if ph in (0, 1, 3):
                    feed("E", b, xT[i][:], w1m[i], w2m[i], ht[i], ph, ("D.dve.b1", b))

            def section_F(b, ph):
                i = b % 2
                if ph == 3:
                    p = room(pe, "F.tr", b)
                    wait(pe, "F.dve.x3", b)
                    for t in range(T):
                        last = pe.transpose(p[:, t * P:(t + 1) * P], xn[i][:, t, :], ident[:])
                    did(last, "F.pe.tr", b)
                if ph == 5:
                    if b == 0:
                        pe.wait_ge(s_w2, 16 * 7)
                    for j in range(PAIRS):
                        p = room(pe, "F.a%d" % j, b)
                        wait(pe, "F.act.xT", b)
                        did(pe.matmul(p[:], wq[:, 3 * 512 + j * P:3 * 512 + (j + 1) * P], xT[i][:], start=True, stop=True),
                            "F.pe.a%d" % j, b)
                if ph == 6:
                    for t in range(T):
                        p = room(pe, "F.v%d" % t, b)
                        did(pe.matmul(p[:], xT[i][:, t * P:(t + 1) * P], wq[:, 2 * 512:3 * 512], start=True, stop=True),
                            "F.pe.v%d" % t, b)
                if 12 <= ph < 16:
                    j = ph - 12
                    for at, name in enumerate("qk"):
                        p = room(pe, "F.%s%d" % (name, j), b)
                        did(pe.matmul(p[:], wq[:, at * 512 + j * P:at * 512 + (j + 1) * P], xT[i][:], start=True, stop=True),
                            "F.pe.%s%d" % (name, j), b)

            def section_G(n, ph):
                b, c = n // T, n % T
                i, k = b % 2, n % 2
                tk = slice(c * P, (c + 1) * P)
                if ph == 0:
                    p = room(pe, "G.tr", n)
                    wait(pe, "F.dve.k3", b)
                    for j in range(PAIRS):
                        last = pe.transpose(p[:, j * P:(j + 1) * P], kk[i][:, j, tk], ident[:])
                    did(last, "G.pe.tr", n)
                    for m in range(2):
                        p = room(pe, "G.qk%d" % m, n)
                        for j in (2 * m, 2 * m + 1):
                            at = p[:, (j % 2) * 2 * P:(j % 2 + 1) * 2 * P].rearrange("p (g s) -> p g s", g=2)
                            last = pe.matmul(at, kk[i][:, j, tk], qz[i][:, j, :, tk], start=True, stop=True)
                        did(last, "G.pe.qk%d" % m, n)
                if ph == 2:
                    p = room(pe, "G.av", n)
                    wait(pe, "G.dve.m1", n)
                    if c:
                        wait(pe, "G.act.s", n - 1)
                    for j in range(PAIRS):
                        for m in range(2):
                            last = pe.matmul(p[m * HD1:(m + 1) * HD1, j * P:(j + 1) * P],
                                             vv[i][:, c, (2 * j + m) * HD1:(2 * j + m + 1) * HD1], sim[k][:, j, m, :],
                                             start=True, stop=(c == 0), skip_group_check=True)
                        if c:
                            for m in range(2):
                                last = pe.matmul(p[m * HD1:(m + 1) * HD1, j * P:(j + 1) * P],
                                                 ss[(n - 1) % 2][:, j, m * HD1:(m + 1) * HD1], qz[i][:, j, m, tk],
                                                 start=False, stop=True, skip_group_check=True)
                    did(last, "G.pe.av", n)
                    wait(pe, "G.act.kt", n)
                    wait(pe, "G.act.s", n - 1)
                    for j in range(PAIRS):
                        last = pe.matmul(bank[7][:, j * P:(j + 1) * P], kt[k][:, j, :], vv[i][:, c, j * P:(j + 1) * P],
                                         start=(c == 0 and j == 0), stop=True, skip_group_check=True)
                    did(last, "G.pe.kv", n)
                if ph == 4:
                    p = room(pe, "G.out", n)
                    wait(pe, "G.act.o", n)
                    for j in range(PAIRS):
                        last = pe.matmul(p[:, 0:D], oc[k][:, j, :], wo1[:, j, :], start=(j == 0), stop=(j == PAIRS - 1))
                    did(last, "G.pe.out", n)

            def section_I(b, ph):
                if ph == 3:
                    p = room(pe, "I.tr", b)
                    wait(pe, "I.dve.y3", b)
                    for t in range(T):
                        last = pe.transpose(p[:, t * P:(t + 1) * P], xn[b % 2][:, t, :], ident[:])
                    did(last, "I.pe.tr", b)
                if ph == 5:
                    p = room(pe, "I.lg", b)
                    wait(pe, "I.act.xT", b)
                    for t in range(T):
                        last = pe.matmul(p[:, t * E:(t + 1) * E], xf[b][:, t * P:(t + 1) * P], gate[:], start=True, stop=True)
                    did(last, "I.pe.lg", b)
                if ph == 9:
                    p = room(pe, "I.cT", b)
                    wait(pe, "I.dve.c", b)
                    for t in range(T):
                        last = pe.transpose(p[0:E, t * P:(t + 1) * P], cmb[b][:, t, :], ident[:])
                    did(last, "I.pe.cT", b)
                if ph == 11:
                    p = room(pe, "I.b2", b)
                    wait(pe, "I.act.cT", b)
                    for t in range(T):
                        last = pe.matmul(p[:, t * P:(t + 1) * P], cT[:, t * P:(t + 1) * P], eb2[:], start=True, stop=True)
                    did(last, "I.pe.b2", b)

            def section_J(n, ph):
                b, e = n // E, n % E
                if n == 0 and ph == 0:
                    pe.wait_ge(s_w3, 16 * 7)
                if ph in (0, 2):
                    feed("J", n, xf[b], ew1[:, e, :], ew2[:, e, :], ht[n % 2], ph, None)

            each(order, {"T": section_T, "A": section_A, "C": section_C, "D": section_D, "E": section_E,
                         "F": section_F, "G": section_G, "I": section_I, "J": section_J})

        @block.scalar
        def _(act):
            act.wait_ge(s_const, 15)

            def section_T(b, ph):
                i = b % 2
                if ph == 1:
                    wait(act, "T.dve.sub", b)
                    did(act.activation(lg[i][:, 3], lg[i][:, 2], ACT.Exp), "T.act.exp", b)
                if ph == 4:
                    wait(act, "T.pe.tr1", b)
                    wait(act, "T.pe.h", b - 2)
                    did(act.activation(eT1[i][:], of("T.tr1", b)[:], ACT.Copy), "T.act.eT1", b)
                    wait(act, "T.pe.tr2", b)
                    did(act.activation(eT2[i][:], of("T.tr2", b)[0:ES - P, :], ACT.Copy), "T.act.eT2", b)

            def section_A(b, ph):
                if ph == 4:
                    wait(act, "A.pe.tr", b)
                    wait(act, "A.pe.qkv3", b - 2)
                    did(act.activation(xT[b % 2][:], of("A.tr", b)[:], ACT.Copy), "A.act.xT", b)

            def section_B(b, ph):
                i = b % 2
                qk = qkv[i][:, :, 0:2 * D]
                if ph == 0:
                    wait(act, "A.dve.qkv3", b)
                    wait(act, "B.pool.k3", b - 2)
                    did(act.activation(sq[i][:], qk, ACT.Square), "B.act.sq", b)
                if ph == 2:
                    wait(act, "B.dve.n2", b)
                    did(act.activation(n2[i][:, 1], n2[i][:, 0], ACT.Ln), "B.act.ln", b)
                    wait(act, "B.act.ln", b)
                    did(act.activation(n2[i][:, 2], n2[i][:, 1], ACT.Exp, scale=-0.5), "B.act.rn", b)
                    did(act.activation(n2[i][:, 3], n2[i][:, 1], ACT.Exp, scale=0.5), "B.act.qn", b)
                if ph == 4:
                    wait(act, "B.dve.u", b)
                    did(act.activation(lnu[:], u[:, :, 0:D], ACT.Square), "B.act.uu", b)
                    wait(act, "B.act.uu", b)
                    did(act.activation(lnu[:], lnu[:], ACT.Ln, bias=tiny[:]), "B.act.lnu", b)
                    wait(act, "B.pool.k3", b - 1)
                    did(act.activation(kab[:], qk[:, :, D:], ACT.Abs), "B.act.kabs", b)
                    did(act.activation(tq[:], n2[i][:, 3].rearrange("p (t g) -> p t g", g=16)[:, :, 0:HEADS0], ACT.Tanh),
                        "B.act.tq", b)
                    wait(act, "B.act.cos", b - 1)
                    did(act.activation(th[:], u[:], ACT.Tanh, scale=20.0), "B.act.tanh", b)
                if ph == 6:
                    wait(act, "B.dve.pl", b)
                    wait(act, "B.dve.fc", b - 1)
                    did(act.activation(amp[:, :, 0:D], lnu[:], ACT.Exp, scale=1.5), "B.act.qt", b)
                    wait(act, "B.act.tanh", b)
                    did(act.activation(sn[:], th[:], ACT.Sin, scale=HALF_PI / 2), "B.act.sin", b)
                    did(act.activation(cs[:], th[:], ACT.Sin, scale=HALF_PI / 2, bias=half_pi[:]), "B.act.cos", b)

            def section_C(b, ph):
                if ph == 1:
                    wait(act, "C.pe.trc", b)
                    wait(act, "C.pe.o1", b - 1)
                    did(act.activation(qc[:], of("C.trc", b)[:], ACT.Copy), "C.act.qc", b)
                    wait(act, "C.pe.trs", b)
                    did(act.activation(qs[:], of("C.trs", b)[:], ACT.Copy), "C.act.qs", b)
                if ph == 7:
                    wait(act, "C.pe.trn", b)
                    wait(act, "C.pe.out", b - 1)
                    did(act.activation(oT[:], of("C.trn", b)[:], ACT.Identity, bias=lngb0[:, 1:2], scale=lngb0[:, 0:1]),
                        "C.act.oT", b)

            act.wait_ge(s_w0, 16 * 5)
            def section_D(b, ph):
                i = b % 2
                if ph == 4:
                    wait(act, "D.pe.tr", b)
                    wait(act, "E.pe.up3", b - 2)
                    did(act.activation(xT[i][:], of("D.tr", b)[:], ACT.Copy), "D.act.xT", b)
                if ph == 6:
                    wait(act, "D.pe.gh", b)
                    wait(act, "D.act.gh", b - 1)
                    did(act.activation(junk, of("D.gh", b)[:], ACT.Relu, bias=gcol[:, 0:1], accum_out=gs[i][:]), "D.act.gh", b)

            def section_E(b, ph):
                i = b % 2
                if ph in (1, 2):
                    for c in (2 * ph - 2, 2 * ph - 1):
                        wait(act, "E.pe.up%d" % c, b)
                        wait(act, "E.pe.down", b - 2)
                        did(act.activation(ht[i][:, c, :], of("E.up%d" % c, b)[:], ACT.Relu, bias=b1m[i][:, c:c + 1]),
                            "E.act.ht%d" % c, b)

            def section_F(b, ph):
                i = b % 2
                if ph == 4:
                    if b == 0:
                        act.wait_ge(s_w2, 16 * 7)
                        act.activation(gam2[:], gam[:], ACT.Copy, scale=float(D) ** 0.5).then_inc(s_gam, 1)
                        act.activation(nba[:], bq1[:, 2, :], ACT.Copy, scale=-1.0).then_inc(s_gam, 1)
                        act.wait_ge(s_gam, 2)
                    wait(act, "F.pe.tr", b)
                    wait(act, "F.pe.k3", b - 2)
                    did(act.activation(xT[i][:], of("F.tr", b)[:], ACT.Copy, scale=gam2[:]), "F.act.xT", b)
                if ph == 6:
                    for j in range(PAIRS):
                        wait(act, "F.pe.a%d" % j, b)
                        wait(act, "F.dve.k3", b - 1)
                        did(act.activation(la[:, j, :], of("F.a%d" % j, b)[:], ACT.Exp, scale=-1.0, bias=nba[:, j:j + 1]),
                            "F.act.e%d" % j, b)
                if ph == 8:
                    wait(act, "F.dve.e", b)
                    did(act.activation(la[:], la[:], ACT.Ln, bias=one[:]), "F.act.l", b)
                if ph == 11:
                    wait(act, "F.dve.cut", b)
                    did(act.activation(lb[:], lb[:], ACT.Exp, scale=-1.0), "F.act.cum", b)
                    did(act.activation(la[:], la[:], ACT.Exp), "F.act.inv", b)

            def section_G(n, ph):
                k = n % 2
                if ph == 1:
                    wait(act, "G.pe.tr", n)
                    wait(act, "G.pe.kv", n - 2)
                    did(act.activation(kt[k][:].rearrange("p a b -> p (a b)"), of("G.tr", n)[:], ACT.Copy), "G.act.kt", n)
                if ph == 3:
                    wait(act, "G.pe.av", n)
                    wait(act, "G.pe.out", n - 2)
                    did(act.activation(oc[k][:].rearrange("p a b -> p (a b)"), of("G.av", n)[:], ACT.Copy), "G.act.o", n)
                    wait(act, "G.pe.kv", n)
                    did(act.activation(ss[k][:].rearrange("p a b -> p (a b)"), bank[7][:], ACT.Copy, scale=HD1 ** -0.5),
                        "G.act.s", n)

            def section_I(b, ph):
                if ph == 4:
                    if b == 0:
                        act.wait_ge(s_w3, 16 * 7)
                    wait(act, "I.pe.tr", b)
                    did(act.activation(xf[b], of("I.tr", b)[:], ACT.Identity, bias=lngb1[:, 1:2], scale=lngb1[:, 0:1]),
                        "I.act.xT", b)
                if ph == 7:
                    wait(act, "I.dve.sub", b)
                    did(act.activation(rt[:, 1], rt[:, 0], ACT.Exp), "I.act.exp", b)
                if ph == 10:
                    wait(act, "I.pe.cT", b)
                    wait(act, "I.pe.b2", b - 1)
                    did(act.activation(cT[:], of("I.cT", b)[0:E, :], ACT.Copy), "I.act.cT", b)

            def section_J(n, ph):
                e = n % E
                if ph == 1:
                    for c in range(FC):
                        wait(act, "J.pe.up%d" % c, n)
                        wait(act, "J.pe.down", n - 2)
                        did(act.activation(ht[n % 2][:, c, :], of("J.up%d" % c, n)[:], ACT.Gelu, bias=eb1[:, e, c:c + 1]),
                            "J.act.ht%d" % c, n)

            each(order, {"T": section_T, "A": section_A, "B": section_B, "C": section_C, "D": section_D,
                         "E": section_E, "F": section_F, "G": section_G, "I": section_I, "J": section_J})

        @block.vector
        def _(dve):
            dve.wait_ge(s_wtok, 16 * 6)
            dve.tensor_copy(gw2b[:], gw2[:].unsqueeze(2).to_broadcast([GATE_H, TABLES, P])).then_inc(s_gw2b, 1)
            dve.wait_ge(s_gv, 1)
            dve.tensor_copy(gatev[:], bank[7][:, 0:TABLES * (DIM + 1)].rearrange("p (t c) -> p t c", t=TABLES))\
               .then_inc(s_gatev, 1)
            dve.wait_ge(s_gatev, 1)
            dve.tensor_tensor(gb2[:], gb2[:], gatev[:, :, DIM], ALU.add).then_inc(s_banks, 1)
            dve.wait_ge(s_banks, 1)

            def statistics(name, b, src, stats, means):
                for t in range(T):
                    did(dve.bn_stats(stats[:, t, :], src[:, t, :]), "%s.dve.st%d" % (name, t), b)
                for t in range(T):
                    wait(dve, "%s.dve.st%d" % (name, t), b)
                    did(dve.bn_aggr(means[:, t, :], stats[:, t, :]), "%s.dve.mv%d" % (name, t), b)

            def normalise(name, b, src, means, scale, dst):
                wait(dve, "%s.pool.rstd" % name, b)
                for t in range(T):
                    did(dve.tensor_scalar(dst[:, t, :], src[:, t, :], means[:, t, 0:1], scale[:, t:t + 1],
                                          ALU.subtract, ALU.mult), "%s.dve.x%d" % (name, t), b)

            dve.wait_ge(s_lnw, 1)
            dve.tensor_copy(lnw[:], bank[6][:, 0:2 * D].rearrange("p (a c) -> p a c", a=2)).then_inc(s_lnb, 1)
            dve.wait_ge(s_lnb, 1)

            def section_T(b, ph):
                i = b % 2
                ein = e_in[b][:].rearrange("p t (a c) -> p t a c", a=TABLES)
                epr = e_pr[:].rearrange("p t (a c) -> p t a c", a=TABLES)
                esc = e_sc[i][:, :, 0:TABLES * DIM].rearrange("p t (a c) -> p t a c", a=TABLES)
                alpha = e_sc[i][:, :, TABLES * DIM:]
                if ph == 0:
                    dve.wait_ge(s_gather[b], 16 * T)
                    did(dve.tensor_tensor(epr, ein, gatev[:, :, 0:DIM].unsqueeze(1).to_broadcast([P, T, TABLES, DIM]),
                                          ALU.mult), "T.dve.prod", b)
                    wait(dve, "T.dve.prod", b)
                    did(dve.tensor_reduce(lg[i][:, 0], epr, X, ALU.add), "T.dve.sum", b)
                    wait(dve, "T.dve.sum", b)
                    did(dve.tensor_tensor(lg[i][:, 1], lg[i][:, 0], gb2[:].unsqueeze(1).to_broadcast([P, T, TABLES]),
                                          ALU.add), "T.dve.bias", b)
                    wait(dve, "T.dve.bias", b)
                    did(dve.tensor_reduce(lg[i][:, 4, :, 0], lg[i][:, 1], X, ALU.max), "T.dve.max", b)
                    wait(dve, "T.dve.max", b)
                    did(dve.tensor_tensor(lg[i][:, 2], lg[i][:, 1], lg[i][:, 4, :, 0:1].to_broadcast([P, T, TABLES]),
                                          ALU.subtract), "T.dve.sub", b)
                if ph == 2:
                    wait(dve, "T.act.exp", b)
                    did(dve.tensor_reduce(lg[i][:, 4, :, 1], lg[i][:, 3], X, ALU.add), "T.dve.den", b)
                    wait(dve, "T.dve.den", b)
                    did(dve.reciprocal(lg[i][:, 4, :, 2], lg[i][:, 4, :, 1]), "T.dve.rden", b)
                    wait(dve, "T.dve.rden", b)
                    wait(dve, "T.pe.tr2", b - 2)
                    did(dve.tensor_tensor(alpha, lg[i][:, 3], lg[i][:, 4, :, 2:3].to_broadcast([P, T, TABLES]),
                                          ALU.mult), "T.dve.alpha", b)
                    wait(dve, "T.dve.alpha", b)
                    did(dve.tensor_tensor(esc, ein, alpha.unsqueeze(3).to_broadcast([P, T, TABLES, DIM]),
                                          ALU.mult), "T.dve.scaled", b)
                if ph == 6:
                    wait(dve, "T.pe.h", b)
                    did(dve.tensor_copy(h[:, b * T:(b + 1) * T, :], of("T.h", b)[:].rearrange("p (t c) -> p t c", t=T)), "T.dve.h", b)

            def section_A(b, ph):
                i = b % 2
                if ph == 0:
                    wait(dve, "T.dve.h", b)
                    statistics("A", b, h[:, b * T:(b + 1) * T, :], stat[i], mv[i])
                if ph == 2:
                    wait(dve, "A.pe.tr", b - 2)
                    normalise("A", b, h[:, b * T:(b + 1) * T, :], mv[i], rstd[i][:, 0], xn[i])
                if ph == 6:
                    if b == 0:
                        dve.wait_ge(s_w0, 16 * 5)
                    for t in range(T):
                        wait(dve, "A.pe.qkv%d" % t, b)
                        wait(dve, "C.pe.kv", b - 2)
                        did(dve.tensor_tensor(qkv[i][:, t, 0:3 * D], of("A.qkv%d" % t, b)[:, 0:3 * D], bqkv0[:], ALU.add),
                            "A.dve.qkv%d" % t, b)

            def section_B(b, ph):
                i = b % 2
                qk = qkv[i][:, :, 0:2 * D].rearrange("p t (g c) -> p t g c", c=HD0)
                if ph == 1:
                    wait(dve, "B.act.sq", b)
                    did(dve.tensor_reduce(n2[i][:, 0].rearrange("p (t g) -> p t g", t=T),
                                          sq[i][:].rearrange("p t (g c) -> p t g c", c=HD0), X, ALU.add), "B.dve.n2", b)
                if ph == 3:
                    wait(dve, "B.act.rn", b)
                    wait(dve, "B.act.tanh", b - 1)
                    rn = n2[i][:, 2].rearrange("p (t g) -> p t g", t=T)
                    did(dve.tensor_tensor(u[:].rearrange("p t (g c) -> p t g c", c=HD0), qk,
                                          rn.unsqueeze(3).to_broadcast([P, T, 16, HD0]), ALU.mult), "B.dve.u", b)
                if ph == 5:
                    wait(dve, "B.act.tq", b)
                    did(dve.tensor_scalar(pw[:], tq[:].rearrange("p t g -> p (t g)"), 0.5, None, ALU.add), "B.dve.pw", b)
                    wait(dve, "B.dve.pw", b)
                    l = lnu[:].rearrange("p t (g c) -> p (t g) c", c=HD0)
                    did(dve.tensor_tensor(l, l, pw[:].unsqueeze(2).to_broadcast([P, T * HEADS0, HD0]), ALU.mult), "B.dve.pl", b)
                if ph == 7:
                    wait(dve, "B.act.sin", b)
                    wait(dve, "B.pool.k3", b)
                    wait(dve, "C.pe.kv", b - 2)
                    did(dve.tensor_tensor(fs[i][:], amp[:], sn[:], ALU.mult), "B.dve.fs", b)
                    wait(dve, "B.act.cos", b)
                    did(dve.tensor_tensor(fc[i][:], amp[:], cs[:], ALU.mult), "B.dve.fc", b)

            def section_C(b, ph):
                i = b % 2
                if ph == 1:
                    wait(dve, "C.pe.kv", b)
                    wait(dve, "C.pe.o1", b - 1)
                    p = of("C.kv", b)
                    for n in range(2):
                        did(dve.tensor_tensor(kvm[:, n, 0:D], p[:, n * (D + 1):n * (D + 1) + D], blk[:, 0:D], ALU.mult),
                            "C.dve.kv%d" % n, b)
                    for n in range(2):
                        did(dve.tensor_scalar(kvm[:, n, D:], blk[:, D:], p[:, n * (D + 1) + D:(n + 1) * (D + 1)], None, ALU.mult),
                            "C.dve.km%d" % n, b)
                if ph == 3:
                    part = [of("C.o%d" % n, b)[:, 0:2 * (D + HEADS0)].rearrange("p (t c) -> p t c", t=2) for n in range(2)]
                    for n in range(2):
                        wait(dve, "C.pe.o%d" % n, b)
                        did(dve.tensor_scalar(den[:, n * 16:(n + 1) * 16].rearrange("p (t g) -> p t g", t=2),
                                              part[n][:, :, D:], 1e-6, None, ALU.add), "C.dve.den%d" % n, b)
                    wait(dve, "C.dve.den1", b)
                    did(dve.reciprocal(rden[:], den[:]), "C.dve.z", b)
                    wait(dve, "C.dve.z", b)
                    for n in range(2):
                        z = rden[:, n * 16:(n + 1) * 16].rearrange("p (t g) -> p t g", t=2).unsqueeze(3).to_broadcast([P, 2, HEADS0, HD0])
                        did(dve.tensor_tensor(o[:, 2 * n:2 * n + 2, :].rearrange("p t (g c) -> p t g c", c=HD0),
                                              part[n][:, :, 0:D].rearrange("p t (g c) -> p t g c", c=HD0), z, ALU.mult),
                            "C.dve.o%d" % n, b)
                    wait(dve, "C.dve.o1", b)
                    statistics("C", b, o, stat_o, mv_o)
                if ph == 5:
                    normalise("C", b, o, mv_o, rstd_o, on)
                if ph == 9:
                    hb = h[:, b * T:(b + 1) * T, :]
                    wait(dve, "C.pe.out", b)
                    wait(dve, "A.pool.hb", b)
                    did(dve.tensor_tensor(hb, hb, of("C.out", b)[:].rearrange("p (t c) -> p t c", t=T), ALU.add), "C.dve.h", b)

            def section_D(b, ph):
                i = b % 2
                hb = h[:, b * T:(b + 1) * T, :]
                if ph == 0:
                    wait(dve, "C.dve.h", b)
                    statistics("D", b, hb, stat[i], mv[i])
                if ph == 2:
                    wait(dve, "D.pool.xb", b - 2)
                    normalise("D", b, hb, mv[i], rstd[i][:, 0], xn[i])
                if ph == 8:
                    wait(dve, "D.pe.g", b)
                    did(dve.tensor_scalar(grow[i][:], of("D.g", b)[:, 0:1], 1.0 / S, gcol[:, 1:2], ALU.mult, ALU.add),
                        "D.dve.g", b)
                    wait(dve, "D.dve.g", b)
                    did(dve.tensor_scalar(selg[i][:], sel[:], grow[i][:], None, ALU.mult), "D.dve.sel", b)
                    wait(dve, "D.pe.b", b - 1)
                    did(dve.tensor_copy(gb[:], grow[i][:].to_broadcast([P, P])), "D.dve.gb", b)
                if ph == 10:
                    wait(dve, "D.pe.w1", b)
                    wait(dve, "E.pe.down", b - 2)
                    did(dve.tensor_tensor(w1m[i][:], of("D.w1", b)[:], w1t[:], ALU.add), "D.dve.w1", b)
                    wait(dve, "D.pe.w2", b)
                    did(dve.tensor_tensor(w2m[i][:], of("D.w2", b)[:], w2t[:], ALU.add), "D.dve.w2", b)
                    wait(dve, "D.pe.b", b)
                    did(dve.tensor_tensor(b1m[i][:], of("D.b", b)[:, 0:FC], b1t[:], ALU.add), "D.dve.b1", b)
                    wait(dve, "D.pool.xb", b - 1)
                    did(dve.tensor_tensor(wide[:], of("D.b", b)[:, P:2 * P], b2w[:], ALU.add), "D.dve.b2", b)

            def section_E(b, ph):
                hb = h[:, b * T:(b + 1) * T, :]
                if ph == 4:
                    wait(dve, "E.pe.down", b)
                    wait(dve, "D.pool.xb", b)
                    did(dve.tensor_tensor(res[:], of("E.down", b)[:].rearrange("p (t c) -> p t c", t=T), xb[:], ALU.add),
                        "E.dve.res", b)
                    wait(dve, "E.dve.res", b)
                    statistics("E", b, res, stat_o, mv_o)
                if ph == 6:
                    normalise("E", b, res, mv_o, rstd_o, rn)
                    wait(dve, "E.dve.x3", b)
                    did(dve.tensor_tensor(rn[:], rn[:], lnw[:, 0, :].unsqueeze(1).to_broadcast([P, T, D]), ALU.mult),
                        "E.dve.g", b)
                    wait(dve, "E.dve.g", b)
                    wait(dve, "D.pool.hb", b)
                    did(dve.tensor_tensor(hb, hb, rn[:], ALU.add), "E.dve.h", b)

            def section_F(b, ph):
                i = b % 2
                hb = h[:, b * T:(b + 1) * T, :]
                if ph == 0:
                    wait(dve, "E.dve.h", b)
                    statistics("F", b, hb, stat[i], mv[i])
                    wait(dve, "F.dve.mv3", b)
                    did(dve.tensor_scalar(low[:], mv[i][:, :, 1], EPS, 1e-24, ALU.add, ALU.mult), "F.dve.lo", b)
                    wait(dve, "F.dve.lo", b)
                    did(dve.scalar_tensor_tensor(ve[i][:, 1], mv[i][:, :, 1], float(D), low[:], ALU.mult, ALU.max),
                        "F.dve.var", b)
                if ph == 2:
                    wait(dve, "F.pe.tr", b - 2)
                    normalise("F", b, hb, mv[i], rstd[i][:, 0], xn[i])
                if ph == 7:
                    wait(dve, "F.act.e3", b)
                    la2 = la[:].rearrange("p a b -> p (a b)")
                    did(dve.tensor_scalar(la2, la2, 1e10, None, ALU.min), "F.dve.e", b)
                    if b == 0:
                        dve.wait_ge(s_w2, 16 * 7)
                    for t in range(T):
                        wait(dve, "F.pe.v%d" % t, b)
                        wait(dve, "G.pe.kv", (b - 2) * T + 3)
                        did(dve.tensor_tensor(vv[i][:, t, :], of("F.v%d" % t, b)[:], bv1[:], ALU.add), "F.dve.v%d" % t, b)
                if ph == 9:
                    wait(dve, "F.act.l", b)
                    for j in range(PAIRS):
                        did(dve.tensor_tensor_scan(lb[:, j, :], la[:, j, :], la[:, j, :], 0.0, ALU.add, ALU.bypass),
                            "F.dve.sum%d" % j, b)
                if ph == 10:
                    wait(dve, "F.dve.sum3", b)
                    did(dve.tensor_scalar(la[:].rearrange("p a b -> p (a b)"), lb[:].rearrange("p a b -> p (a b)"),
                                          LN_INV_MAX, None, ALU.min), "F.dve.cut", b)
                if 13 <= ph < 17:
                    j = ph - 13
                    wait(dve, "F.act.inv", b)
                    wait(dve, "G.pe.av", (b - 2) * T + 3)
                    dve.wait_ge(s_qz, min(b + 1, 2))
                    wait(dve, "F.pe.q%d" % j, b)
                    for m, name in enumerate(("qa", "qb")):
                        rows = slice(m * HD1, (m + 1) * HD1)
                        did(dve.scalar_tensor_tensor(qz[i][rows, j, m, :], of("F.q%d" % j, b)[rows, :], bq1[rows, 0, j:j + 1],
                                                     lb[rows, j, :], ALU.add, ALU.mult), "F.dve.%s%d" % (name, j), b)
                    wait(dve, "F.pe.k%d" % j, b)
                    did(dve.scalar_tensor_tensor(kk[i][:, j, :], of("F.k%d" % j, b)[:], bq1[:, 1, j:j + 1], la[:, j, :],
                                                 ALU.add, ALU.mult), "F.dve.k%d" % j, b)

            def section_G(n, ph):
                if ph == 1:
                    for m in range(2):
                        wait(dve, "G.pe.qk%d" % m, n)
                        wait(dve, "G.pe.av", n - 2)
                        did(dve.tensor_tensor(sim[n % 2][:, 2 * m:2 * m + 2].rearrange("p a b c -> p (a b c)"),
                                              of("G.qk%d" % m, n)[:], causal[:], ALU.mult), "G.dve.m%d" % m, n)
                if ph == 5:
                    wait(dve, "G.pe.out", n)
                    wait(dve, "F.pool.hb", n // T)
                    did(dve.tensor_tensor(h[:, n, :], h[:, n, :], of("G.out", n)[:, 0:D], ALU.add), "G.dve.h", n)

            def section_I(b, ph):
                i = b % 2
                hb = h[:, b * T:(b + 1) * T, :]
                if ph == 0:
                    wait(dve, "G.dve.h", b * T + 3)
                    statistics("I", b, hb, stat[i], mv[i])
                if ph == 2:
                    normalise("I", b, hb, mv[i], rstd[i][:, 0], rn)
                    wait(dve, "I.pe.tr", b - 2)
                    for t in range(T):
                        did(dve.tensor_scalar(xn[i][:, t, :], hb[:, t, :], mv[i][:, t, 0:1], rstd[i][:, 1, t:t + 1],
                                              ALU.subtract, ALU.mult), "I.dve.y%d" % t, b)
                if ph == 3:
                    wait(dve, "I.dve.y3", b)
                    did(dve.tensor_tensor(hb, hb, rn[:], ALU.add), "I.dve.h", b)
                if ph == 6:
                    wait(dve, "I.pe.lg", b)
                    lgt = of("I.lg", b)[:, 0:T * E].rearrange("p (t e) -> p t e", t=T)
                    did(dve.tensor_reduce(r1[:, 0], lgt, X, ALU.max), "I.dve.max", b)
                    wait(dve, "I.dve.max", b)
                    did(dve.tensor_tensor(rt[:, 0], lgt, r1[:, 0].unsqueeze(2).to_broadcast([P, T, E]), ALU.subtract),
                        "I.dve.sub", b)
                if ph == 8:
                    wait(dve, "I.act.exp", b)
                    did(dve.tensor_reduce(r1[:, 1], rt[:, 1], X, ALU.add), "I.dve.den", b)
                    wait(dve, "I.dve.den", b)
                    did(dve.reciprocal(r1[:, 2], r1[:, 1]), "I.dve.rden", b)
                    wait(dve, "I.dve.rden", b)
                    did(dve.tensor_tensor(rt[:, 2], rt[:, 1], r1[:, 2].unsqueeze(2).to_broadcast([P, T, E]), ALU.mult),
                        "I.dve.p", b)
                    wait(dve, "I.dve.p", b)
                    for t in range(T):
                        did(dve.max(rt[:, 3, t, :], rt[:, 2, t, :]), "I.dve.top%d" % t, b)
                    wait(dve, "I.dve.top3", b)
                    for t in range(T):
                        did(dve.max_index(rix[:, t, :], rt[:, 3, t, :], rt[:, 2, t, :]), "I.dve.at%d" % t, b)
                    wait(dve, "I.dve.at3", b)
                    for n in range(2):
                        did(dve.tensor_tensor(rt[:, 4 + n], rix[:, :, n:n + 1].to_broadcast([P, T, E]),
                                              iota[:].unsqueeze(1).to_broadcast([P, T, E]), ALU.is_equal), "I.dve.is%d" % n, b)
                    wait(dve, "I.dve.is1", b)
                    for n in range(2):
                        did(dve.tensor_tensor(rt[:, 6 + n], rt[:, 4 + n], rt[:, 3, :, n:n + 1].to_broadcast([P, T, E]),
                                              ALU.mult), "I.dve.c%d" % n, b)
                    wait(dve, "I.dve.c1", b)
                    did(dve.tensor_tensor(cmb[b][:], rt[:, 6], rt[:, 7], ALU.add), "I.dve.c", b)
                if ph == 12:
                    wait(dve, "I.pe.b2", b)
                    did(dve.tensor_tensor(hb, hb, of("I.b2", b)[:].rearrange("p (t c) -> p t c", t=T), ALU.add),
                        "I.dve2.h", b)

            def section_J(n, ph):
                b, e = n // E, n % E
                if ph == 3:
                    wait(dve, "J.pe.down", n)
                    wait(dve, "I.dve2.h", b)
                    wait(dve, "J.dve.y3", n - 1)
                    for t in range(T):
                        ht_ = h[:, b * T + t, :]
                        did(dve.scalar_tensor_tensor(ht_, of("J.down", n)[:, t * P:(t + 1) * P], cmb[b][:, t, e:e + 1], ht_,
                                                     ALU.mult, ALU.add), "J.dve.y%d" % t, n)

            each(order, {"T": section_T, "A": section_A, "B": section_B, "C": section_C, "D": section_D,
                         "E": section_E, "F": section_F, "G": section_G, "I": section_I, "J": section_J})


def lay(i):
    import numpy as np

    def col(x):
        return np.asarray(x).reshape(-1, P).T

    a = {}
    a["idx"] = np.asarray(i["x"]).reshape(B * T, P).T
    names = ("glove", "fast", "levy")
    a["tables"] = np.concatenate([np.asarray(i["L0_tok_%s_tab" % n]) for n in names], axis=1)
    a["gw1"] = np.stack([np.concatenate([i["L0_tok_gW1_" + n], np.asarray(i["L0_tok_gb1_" + n])[:, None]], axis=1)
                         for n in names], axis=1)
    a["gw2"] = np.stack([np.asarray(i["L0_tok_gW2_" + n])[0] for n in names], axis=1)
    a["gb2"] = np.concatenate([i["L0_tok_gb2_" + n] for n in names])
    a["wtok"] = np.concatenate([np.asarray(i["L0_tok_W_" + n]).T for n in names]
                               + [np.asarray(i["L0_tok_b_" + n])[None] for n in names])
    a["wqkv0"] = i["L0_attn_qkv_w"]
    a["bqkv0"] = i["L0_attn_qkv_b"]
    a["wo0"] = i["L0_attn_out_w"]
    a["bo0"] = i["L0_attn_out_b"]
    a["lngb0"] = np.stack([i["L0_attn_ln_g"], i["L0_attn_ln_b"]], axis=1)
    f = {k[7:]: np.asarray(v) for k, v in i.items() if k.startswith("L0_ffn_")}
    a["g1t"] = f["gfc1_w"].T
    a["g2r"] = np.repeat(f["gfc2_w"].T, J, axis=1)
    a["gcol"] = np.stack([f["gfc1_b"], np.repeat(f["gfc2_b"], J)], axis=1)
    a["w1t"] = f["W1"].T
    a["w2t"] = f["W2"].T.reshape(FC, P, D).transpose(1, 0, 2).reshape(P, FC * D)
    a["tv1"] = f["tv_W1"].transpose(0, 2, 1).reshape(E, D // J, J, FF).transpose(0, 2, 1, 3).reshape(P, D // J, FF)
    a["tv2"] = f["tv_W2"].transpose(0, 2, 1).reshape(E, FC, P // J, J, D).transpose(0, 3, 2, 1, 4).reshape(P, P // J, FC * D)
    a["tvb1"] = f["tv_b1"]
    a["tvb2"] = f["tv_b2"]
    a["b1t"] = col(f["b1"])
    a["b2"] = f["b2"]
    sel = np.zeros((P, 2, 2 * J), np.float32)
    for p in range(P):
        for r in range(2):
            sel[p, r, J * r + p % J] = 1
    a["sel"] = sel
    a["lnr"] = np.concatenate([np.concatenate([f["tv_ln_g"], f["tv_ln_b"]], axis=1),
                               np.concatenate([f["ln_g"], f["ln_b"]])[None]])
    g = {k[8:]: np.asarray(v) for k, v in i.items() if k.startswith("L1_attn_")}
    inner = HEADS1 * HD1
    a["wq"] = np.concatenate([g["w_qkv"], g["w_a"]], axis=1)
    a["wo1"] = g["w_out"].reshape(PAIRS, P, D).transpose(1, 0, 2)
    a["bq1"] = np.stack([col(g["b_qkv"][0:inner]), col(g["b_qkv"][inner:2 * inner]), col(g["b_a"])], axis=1)
    a["bv1"] = g["b_qkv"][2 * inner:]
    a["bo1"] = g["b_out"]
    a["gam"] = g["gamma"].reshape(P, 1)
    a["causal"] = np.tile(np.triu(np.full((P, P), HD1 ** -0.5, np.float32)), (1, 4))
    m = {k[7:]: np.asarray(v) for k, v in i.items() if k.startswith("L1_ffn_")}
    a["gate"] = m["gate_w"]
    a["lngb1"] = np.stack([m["ln_g"], m["ln_b"]], axis=1)
    a["eb1"] = m["b1"].reshape(E, FC, P).transpose(2, 0, 1)
    a["eb2"] = m["b2"]
    a["iota"] = np.tile(np.arange(E, dtype=np.float32), (P, 1))
    a["ew1"] = m["w1"].transpose(1, 0, 2)
    a["ew2"] = m["w2"].reshape(E, FC, P, D).transpose(2, 0, 1, 3).reshape(P, E, FC * D)
    return {k: np.ascontiguousarray(v) for k, v in a.items()}


def kernel(**inputs):
    import numpy as np
    import concourse.bacc as bacc
    from concourse.bass_utils import run_bass_kernel_spmd

    nc = bacc.Bacc("TRN2", target_bir_lowering=False, num_devices=1)
    arrays = lay(inputs)
    a = {name: nc.dram_tensor("in_" + name, x.shape, mybir.dt.from_np(x.dtype), kind="ExternalInput").ap()
         for name, x in arrays.items()}
    out = nc.dram_tensor("out", (B * S, D), F32, kind="ExternalOutput").ap()
    lm_tower(nc, a, out)
    got = run_bass_kernel_spmd(nc, [{"in_" + name: x for name, x in arrays.items()}], core_ids=[0])
    return np.asarray(got.results[0]["out"]).reshape(B, S, D)
```

```python
from contextlib import ExitStack

import concourse.bass as bass
from concourse import mybir

ALU = mybir.AluOpType
ACT = mybir.ActivationFunctionType
F32 = mybir.dt.float32
I32 = mybir.dt.int32
X = mybir.AxisListType.X
HALF_PI = 1.5707963267948966

P = 128
B, S, D = 4, 512, 128
T = S // P
DIM, TABLES = 75, 3
GATE_H = 10
HEADS0 = 8
HD0 = D // HEADS0
E, FF = 8, 512
FC = FF // P
J = P // E
HEADS1, HD1 = 8, 64
PAIRS = HEADS1 * HD1 // P
EPS = 1e-5
LN_MERGE = 0.03
LN_INV_MAX = 18.420680743952367

STEPS = {
    "T.dve": ["prod", "sum", "bias", "max", "sub", "den", "rden", "alpha", "scaled", "h"],
    "T.act": ["exp", "eT1", "eT2"],
    "T.pe": ["tr1", "tr2", "h"],
    "A.dve": ["st%d" % t for t in range(T)] + ["mv%d" % t for t in range(T)] + ["eps"] + ["x%d" % t for t in range(T)]
    + ["qkv%d" % t for t in range(T)],
    "A.pool": ["rstd", "hb"],
    "A.pe": ["tr"] + ["qkv%d" % t for t in range(T)],
    "A.act": ["xT"],
    "B.act": ["sq", "ln", "rn", "qn", "uu", "lnu", "kabs", "tq", "tanh", "qt", "sin", "cos"],
    "B.dve": ["n2", "u", "pw", "pl", "fs", "fc"],
    "B.pool": ["k3"],
    "C.pe": ["trc", "trs", "kv", "o0", "o1"],
    "C.act": ["qc", "qs"],
    "C.dve": ["kv0", "kv1", "km0", "km1", "den0", "den1", "z", "o0", "o1"],
    "O.pe": ["tr", "out"],
    "O.act": ["oT"],
    "O.dve": ["st%d" % t for t in range(T)] + ["mv%d" % t for t in range(T)] + ["eps"] + ["x%d" % t for t in range(T)] + ["h"],
    "O.pool": ["rstd"],
    "D.dve": ["st%d" % t for t in range(T)] + ["mv%d" % t for t in range(T)] + ["eps"] + ["x%d" % t for t in range(T)],
    "D.pool": ["rstd", "hb"],
    "D.pe": ["tr"],
    "D.act": ["xT"],
    "H.pe": ["gh", "g", "w1", "w2", "b"],
    "H.act": ["gh"],
    "H.dve": ["g", "sel", "gb", "w1", "w2", "b1", "b2"],
    "H.pool": ["xb"],
    "E.pe": ["up%d" % c for c in range(FC)] + ["down"],
    "E.act": ["ht%d" % c for c in range(FC)],
    "E.dve": ["res"] + ["st%d" % t for t in range(T)] + ["mv%d" % t for t in range(T)] + ["eps"]
    + ["x%d" % t for t in range(T)] + ["g", "h"],
    "E.pool": ["rstd"],
    "F.dve": ["st%d" % t for t in range(T)] + ["mv%d" % t for t in range(T)] + ["lo", "var"]
    + ["x%d" % t for t in range(T)] + ["e"] + ["v%d" % t for t in range(T)] + ["sum%d" % p for p in range(PAIRS)]
    + ["cut"] + [x % p for p in range(PAIRS) for x in ("qa%d", "qb%d", "k%d")],
    "F.pool": ["rstd", "hb"],
    "F.pe": ["tr"] + ["a%d" % p for p in range(PAIRS)] + ["v%d" % t for t in range(T)]
    + [x % p for p in range(PAIRS) for x in ("q%d", "k%d")],
    "F.act": ["xT"] + ["e%d" % p for p in range(PAIRS)] + ["l", "cum", "inv"],
    "G.pe": ["tr", "qk0", "qk1", "av", "kv", "out"],
    "G.act": ["kt", "o", "s"],
    "G.dve": ["m0", "m1", "h"],
    "I.dve": ["st%d" % t for t in range(T)] + ["mv%d" % t for t in range(T)] + ["ve", "vv"] + ["x%d" % t for t in range(T)]
    + ["y%d" % t for t in range(T)] + ["h", "max", "sub", "den", "rden", "p"] + ["top%d" % t for t in range(T)]
    + ["at%d" % t for t in range(T)] + ["is0", "is1", "c0", "c1", "c"],
    "I.pool": ["rstd"],
    "I.pe": ["tr", "lg", "cT", "b2"],
    "I.act": ["xT", "exp", "cT"],
    "I.dve2": ["h"],
    "J.pe": ["up%d" % c for c in range(FC)] + ["down"],
    "J.act": ["ht%d" % c for c in range(FC)],
    "J.dve": ["y%d" % t for t in range(T)],
}



def lm_tower(nc, a, out, dbg=None):
    ctx = ExitStack()
    with ctx:
        def sb(name, shape, dt=F32):
            return ctx.enter_context(nc.sbuf_tensor(name, shape, dt))

        sem = {name: ctx.enter_context(nc.semaphore(name.replace(".", "_"))) for name in STEPS}

        def count(step, b):
            section, engine, what = step.split(".")
            steps = STEPS[section + "." + engine]
            return b * len(steps) + steps.index(what) + 1

        def wait(eng, step, b):
            if b >= 0:
                eng.wait_ge(sem[step.rsplit(".", 1)[0]], count(step, b))

        emitted = {}

        def did(ins, step, b):
            name = step.rsplit(".", 1)[0]
            emitted[name] = emitted.get(name, 0) + 1
            assert emitted[name] == count(step, b), (step, b, emitted[name])
            ins.then_inc(sem[name], 1)

        def carve(arena, size):
            used = [0]

            def take(shape):
                n = 1
                for k in shape[1:]:
                    n *= k
                view = arena[0:shape[0], used[0]:used[0] + n]
                used[0] += n
                assert used[0] <= size, used[0]
                if len(shape) == 3:
                    view = view.rearrange("p (a b) -> p a b", a=shape[1])
                elif len(shape) == 4:
                    view = view.rearrange("p (a b c) -> p a b c", a=shape[1], b=shape[2])
                return view
            return take

        h = sb("h", [P, B * T, D])
        ident = sb("ident", [P, P])
        idx = sb("idx", [P, B * T], I32)
        ES = TABLES * DIM + TABLES

        SIZE1 = 8448
        arena1 = sb("arena1", [P, SIZE1])
        arena3 = sb("arena3", [P, FC * S])
        take = carve(arena1, SIZE1)
        e_in = [take([P, T, TABLES * DIM]) for i in range(B)]
        e_sc = [take([P, T, ES]) for i in range(2)]
        e_pr = take([P, T, TABLES * DIM])
        eT1 = [take([P, S]) for i in range(2)]
        eT2 = [take([ES - P, S]) for i in range(2)]
        take = carve(arena1, SIZE1)
        ht = [take([P, FC, S]) for i in range(2)]
        w1m = [take([P, FF]) for i in range(2)]
        w2m = [take([P, FF]) for i in range(2)]
        res = take([P, T, D])
        rn = take([P, T, D])
        wide = take([P, D])
        junk = take([P, S])
        gb = take([P, P])

        take = carve(arena1, SIZE1)
        kt = [take([P, PAIRS, P]) for i in range(2)]
        sim = [take([P, PAIRS, 2, P]) for i in range(2)]
        oc = [take([P, PAIRS, P]) for i in range(2)]
        ss = [take([P, PAIRS, P]) for i in range(2)]
        hj = [take([P, FC, S]), arena3[:].rearrange("p (a b) -> p a b", a=FC)]
        rt = take([P, 8, T, E])
        cmb = [take([P, T, E]) for i in range(B)]
        cT = take([E, S])

        gatev = sb("gatev", [P, TABLES, DIM + 1])
        gw1 = sb("gw1", [GATE_H, TABLES, DIM + 1])
        gw2 = sb("gw2", [GATE_H, TABLES])
        gw2b = sb("gw2b", [GATE_H, TABLES, P])
        gb2 = sb("gb2", [P, TABLES])
        lg = [sb("lg%d" % i, [P, 5, T, TABLES]) for i in range(2)]
        wtok1 = sb("wtok1", [P, D])
        wtok2 = sb("wtok2", [ES - P, D])
        stat = [sb("stat%d" % i, [P, T, 6]) for i in range(2)]
        mv = [sb("mv%d" % i, [P, T, 2]) for i in range(2)]
        rstd = [sb("rstd%d" % i, [P, 2, T]) for i in range(2)]
        ve = [sb("ve%d" % i, [P, 2, T]) for i in range(2)]
        stat_o = sb("stat_o", [P, T, 6])
        mv_o = sb("mv_o", [P, T, 2])
        ve_o = sb("ve_o", [P, T])
        rstd_o = sb("rstd_o", [P, T])
        stat_e = sb("stat_e", [P, T, 6])
        mv_e = sb("mv_e", [P, T, 2])
        ve_e = sb("ve_e", [P, T])
        rstd_e = sb("rstd_e", [P, T])
        mhalf = sb("mhalf", [P, 2, T])
        xn = [sb("xn%d" % i, [P, T, D]) for i in range(2)]
        xT = [sb("xT%d" % i, [P, S]) for i in range(2)]
        stat_f = sb("stat_f", [P, T, 6])
        mv_f = sb("mv_f", [P, T, 2])
        ve_f = sb("ve_f", [P, T])
        rstd_f = sb("rstd_f", [P, T])
        xn_f = sb("xn_f", [P, T, D])
        xT_f = sb("xT_f", [P, S])
        take = carve(arena3, FC * S)
        w1t, w2t, tvb1, bqkv0, wo0 = (take([P, n]) for n in (FF, FF, FF, 3 * D, D))
        half_pi = sb("half_pi", [P, 1])
        tiny = sb("tiny", [P, 1])
        wqkv0 = sb("wqkv0", [P, 3 * D])
        bo0 = sb("bo0", [P, D])
        lngb0 = sb("lngb0", [P, 2])
        blk = sb("blk", [P, D + HEADS0])

        SIZE2 = 20 * 1024 + 512
        arena2 = sb("arena2", [P, SIZE2])
        take = carve(arena2, SIZE2)
        qkv = [take([P, T, 3 * D + 1]) for i in range(2)]
        sq = [take([P, T, 2 * D]) for i in range(2)]
        n2 = [take([P, 4, T * 16]) for i in range(2)]
        u = take([P, T, 2 * D])
        pw = take([P, T * HEADS0])
        lnu = take([P, T, D])
        kab = take([P, T, D])
        tq = take([P, T, HEADS0])
        th = take([P, T, 2 * D])
        amp = take([P, T, 2 * D])
        fs = [take([P, T, 2 * D]) for i in range(2)]
        fc = [take([P, T, 2 * D]) for i in range(2)]
        sn = take([P, T, 2 * D])
        cs = take([P, T, 2 * D])
        qc = take([P, S])
        qs = take([P, S])
        kvm = take([P, 2, D + HEADS0])
        den = take([P, T * HEADS0])
        rden = take([P, T * HEADS0])
        o = take([P, T, D])
        on = take([P, T, D])
        oT = take([P, S])
        take = carve(arena2, SIZE2)
        qz = [take([P, PAIRS, 2, S]) for i in range(2)]
        kk = [take([P, PAIRS, S]) for i in range(2)]
        vv = [take([P, T, HEADS1 * HD1]) for i in range(2)]
        la = take([P, PAIRS, S])
        lb = take([P, PAIRS, S])

        big = sb("big", [P, 2 * E * FF])
        tv1 = big[:, 0:E * FF].rearrange("p (i f) -> p i f", i=E)
        tv2 = big[:, E * FF:].rearrange("p (i f) -> p i f", i=E)
        ew1 = tv1
        ew2 = tv2
        g1t = sb("g1t", [P, D])
        g2r = sb("g2r", [P, P])
        gcol = sb("gcol", [P, 2])
        tvb2 = sb("tvb2", [P, D])
        b1t = sb("b1t", [P, FC])
        b2w = sb("b2w", [P, D])
        sel = sb("sel", [P, 2, 2 * J])
        lnr = sb("lnr", [E + 1, 2 * D])
        lnco = sb("lnco", [E + 1, P])
        lnw = sb("lnw", [P, 2, D])
        gs = [sb("gs%d" % i, [P, 1]) for i in range(2)]
        grow = [sb("grow%d" % i, [P, 1]) for i in range(2)]
        selg = [sb("selg%d" % i, [P, 2, 2 * J]) for i in range(2)]
        b1m = [sb("b1m%d" % i, [P, FC]) for i in range(2)]
        xb = sb("xb", [P, T, D])

        wq = sb("wq", [P, 4 * 512])
        wo1 = sb("wo1", [P, PAIRS, D])
        bq1 = sb("bq1", [P, 3, PAIRS])
        nba = sb("nba", [P, PAIRS])
        bv1 = sb("bv1", [P, HEADS1 * HD1])
        bo1 = sb("bo1", [P, D])
        gam = sb("gam", [P, 1])
        gam2 = sb("gam2", [P, 1])
        causal = sb("causal", [P, 4 * P])
        low = sb("low", [P, T])

        gate = sb("gate", [P, E])
        lngb1 = sb("lngb1", [P, 2])
        eb1 = sb("eb1", [P, E, FC])
        eb2 = sb("eb2", [E, D])
        iota = sb("iota", [P, E])
        rix = sb("rix", [P, T, E], mybir.dt.uint32)
        r1 = sb("r1", [P, 4, T])
        one = sb("one", [P, 1])

        bank = [ctx.enter_context(nc.psum_tensor("bank%d" % i, [P, S], F32)) for i in range(8)]
        READ = {"T.tr1": "T.act.eT1", "T.tr2": "T.act.eT2", "T.h": "T.dve.h", "A.tr": "A.act.xT",
                "C.trc": "C.act.qc", "C.trs": "C.act.qs", "C.kv": "C.dve.km1", "C.o0": "C.dve.o0",
                "C.o1": "C.dve.o1", "O.tr": "O.act.oT", "O.out": "O.dve.h",
                "D.tr": "D.act.xT", "H.gh": "H.act.gh", "H.g": "H.dve.g", "H.w1": "H.dve.w1", "H.w2": "H.dve.w2",
                "H.b": "H.dve.b2", "E.down": "E.dve.res", "F.tr": "F.act.xT", "G.tr": "G.act.kt",
                "G.qk0": "G.dve.m0", "G.qk1": "G.dve.m1", "G.av": "G.act.o", "G.out": "G.dve.h",
                "I.tr": "I.act.xT", "I.lg": "I.dve.sub", "I.cT": "I.act.cT", "I.b2": "I.dve2.h",
                "J.down": "J.dve.y3"}
        READ.update({"E.up%d" % c: "E.act.ht%d" % c for c in range(FC)})
        READ.update({"J.up%d" % c: "J.act.ht%d" % c for c in range(FC)})
        READ.update({"F.a%d" % p: "F.act.e%d" % p for p in range(PAIRS)})
        READ.update({"F.v%d" % t: "F.dve.v%d" % t for t in range(T)})
        READ.update({"F.q%d" % p: "F.dve.qb%d" % p for p in range(PAIRS)})
        READ.update({"F.k%d" % p: "F.dve.k%d" % p for p in range(PAIRS)})
        READ.update({"A.qkv%d" % t: "A.dve.qkv%d" % t for t in range(T)})
        GROUPS = {("T", 3): ["tr1", "tr2"], ("T", 5): ["h"], ("A", 3): ["tr"],
                  ("A", 5): ["qkv%d" % t for t in range(T)],
                  ("C", 0): ["trc", "trs", "kv"], ("C", 2): ["o0", "o1"], ("O", 3): ["tr"], ("O", 5): ["out"],
                  ("D", 3): ["tr"], ("H", 0): ["gh"], ("H", 2): ["g"], ("H", 4): ["w1", "w2", "b"],
                  ("E", 0): ["up0", "up1"], ("E", 1): ["up2", "up3"], ("E", 3): ["down"],
                  ("F", 3): ["tr"], ("F", 5): ["a%d" % p for p in range(PAIRS)], ("F", 6): ["v%d" % t for t in range(T)],
                  ("F", 12): ["q0", "k0"], ("F", 13): ["q1", "k1"], ("F", 14): ["q2", "k2"], ("F", 15): ["q3", "k3"],
                  ("G", 0): ["tr", "qk0", "qk1"], ("G", 2): ["av"], ("G", 4): ["out"],
                  ("I", 3): ["tr"], ("I", 5): ["lg"], ("I", 9): ["cT"], ("I", 11): ["b2"],
                  ("J", 0): ["up%d" % c for c in range(FC)], ("J", 2): ["down"]}
        PHASES = {"T": 7, "A": 7, "B": 8, "C": 4, "O": 7, "D": 5, "H": 7, "E": 8, "F": 17, "G": 6, "I": 13, "J": 4}
        starts = []
        for b in range(B):
            for s, at in (("T", 0), ("A", 7.5), ("B", 14), ("C", 22.5), ("O", 25.5)):
                starts.append((at + 8 * b, 1, s, b))
        for b in range(B):
            for s, at in (("D", 34.5), ("H", 40), ("E", 47)):
                starts.append((at + 7.5 * b, 1, s, b))
        for b in range(B):
            at = 57.5 + 20.5 * b
            starts.append((at, 1, "F", b))
            for c in range(T):
                starts.append((at + 17 + 4.75 * c, 1, "G", b * T + c))
            at += 36.75
            starts.append((at, 1, "I", b))
            for e in range(E):
                starts.append((at + 9.5 + 2.375 * e, 1, "J", b * E + e))
        order = sorted((at + k * ph, n, s, b, ph) for n, (at, k, s, b) in enumerate(starts) for ph in range(PHASES[s]))
        order = [x[2:] for x in order]
        RING = 7
        place = {}
        ring = [g for s, b, ph in order for g in [(s + "." + x, b) for x in GROUPS.get((s, ph), [])]]
        for i, (g, b) in enumerate(ring):
            place[g, b] = (bank[i % RING], ring[i - RING] if i >= RING else None)

        def room(pe, g, b):
            at, last = place[g, b]
            if last:
                wait(pe, READ[last[0]], last[1])
            else:
                pe.wait_ge(s_banks, 1)
            return at

        def of(g, b):
            return place[g, b][0]

        s_const = ctx.enter_context(nc.semaphore("s_const"))
        s_ident = ctx.enter_context(nc.semaphore("s_ident"))
        s_banks = ctx.enter_context(nc.semaphore("s_banks"))
        s_gather = [ctx.enter_context(nc.semaphore("s_gather%d" % b)) for b in range(B)]
        s_idx = ctx.enter_context(nc.semaphore("s_idx"))
        s_wtok = ctx.enter_context(nc.semaphore("s_wtok"))
        s_w0 = ctx.enter_context(nc.semaphore("s_w0"))
        s_w1 = ctx.enter_context(nc.semaphore("s_w1"))
        s_w2 = ctx.enter_context(nc.semaphore("s_w2"))
        s_w3 = ctx.enter_context(nc.semaphore("s_w3"))
        s_lnw = ctx.enter_context(nc.semaphore("s_lnw"))
        s_lnb = ctx.enter_context(nc.semaphore("s_lnb"))
        s_qz = ctx.enter_context(nc.semaphore("s_qz"))
        s_gam = ctx.enter_context(nc.semaphore("s_gam"))
        s_gw2b = ctx.enter_context(nc.semaphore("s_gw2b"))
        s_gv = ctx.enter_context(nc.semaphore("s_gv"))
        s_gatev = ctx.enter_context(nc.semaphore("s_gatev"))
        s_out = ctx.enter_context(nc.semaphore("s_out"))
        block = ctx.enter_context(nc.Block())

        def row(name, n):
            return a[name].rearrange("(o n) -> o n", o=1).to_broadcast([P, n])

        @block.sync
        def _(sp):
            sp.dma_start(idx[:], a["idx"]).then_inc(s_idx, 16)
            for dst, src in ((gw1, a["gw1"]), (gw2, a["gw2"]), (gb2, row("gb2", TABLES)),
                             (wtok1, a["wtok"][0:P, :]), (wtok2, a["wtok"][P:ES, :]), (lnr, a["lnr"])):
                sp.dma_start(dst[:], src).then_inc(s_wtok, 16)
            for dst, src in ((wqkv0, a["wqkv0"]), (bqkv0, row("bqkv0", 3 * D)), (wo0, a["wo0"]),
                             (bo0, row("bo0", D)), (lngb0, a["lngb0"])):
                sp.dma_start(dst[:], src).then_inc(s_w0, 16)
            for dst, src in ((g1t, a["g1t"]), (g2r, a["g2r"]), (gcol, a["gcol"]), (w1t, a["w1t"]), (w2t, a["w2t"]),
                             (tvb2[0:P:J, :], a["tvb2"]), (tvb1[0:P:J, :], a["tvb1"]), (b1t, a["b1t"]),
                             (b2w, row("b2", D)), (sel, a["sel"]), (tv1, a["tv1"]), (tv2, a["tv2"])):
                if src is a["tvb2"]:
                    sp.wait_ge(s_const, 2)
                sp.dma_start(dst[:], src).then_inc(s_w1, 16)
            for dst, src in ((wq, a["wq"]), (wo1, a["wo1"]), (bq1, a["bq1"]), (bv1, row("bv1", HEADS1 * HD1)),
                             (bo1, row("bo1", D)), (gam, a["gam"]), (causal, a["causal"])):
                sp.dma_start(dst[:], src).then_inc(s_w2, 16)
            for dst, src in ((gate, a["gate"]), (lngb1, a["lngb1"]), (eb1, a["eb1"]), (eb2, a["eb2"]), (iota, a["iota"])):
                sp.dma_start(dst[:], src).then_inc(s_w3, 16)
            wait(sp, "H.pe.w2", B - 1)
            sp.dma_start(ew1, a["ew1"]).then_inc(s_w3, 16)
            sp.dma_start(ew2, a["ew2"]).then_inc(s_w3, 16)
            for b in range(B):
                wait(sp, "J.dve.y3", E * b + E - 1)
                sp.dma_start(out[b * S:(b + 1) * S, :].rearrange("(t p) d -> p t d", p=P),
                             h[:, b * T:(b + 1) * T, :]).then_inc(s_out, 16)
            sp.wait_ge(s_out, 16 * B)

        def each(order, programs):
            for section, b, ph in order:
                if section in programs:
                    programs[section](b, ph)

        @block.gpsimd
        def _(pool):
            pool.memset(ident[:], 0.0).then_inc(s_ident, 1)
            pool.memset(tvb1[:], 0.0).then_inc(s_const, 1)
            pool.memset(tvb2[:], 0.0).then_inc(s_const, 1)
            pool.memset(lnco[:], 1.0 - E * LN_MERGE).then_inc(s_const, 1)
            pool.wait_ge(s_const, 3)
            pool.memset(lnco[0:E, :], LN_MERGE).then_inc(s_const, 1)
            pool.memset(blk[:], 1.0 / S).then_inc(s_const, 1)
            pool.memset(mhalf[:], -0.5).then_inc(s_const, 1)
            pool.memset(half_pi[:], HALF_PI).then_inc(s_const, 1)
            pool.memset(tiny[:], 1e-19).then_inc(s_const, 1)
            pool.memset(one[:], 1.0).then_inc(s_const, 1)
            for i in range(2):
                pool.memset(qkv[i][:, :, 3 * D:3 * D + 1], 1.0).then_inc(s_const, 1)
            pool.wait_ge(s_ident, 1)
            pool.affine_select(out=ident[:], in_=ident[:], compare_op=ALU.not_equal, fill=1.0, base=0,
                               pattern=[[-1, P]], channel_multiplier=1).then_inc(s_ident, 1)
            pool.wait_ge(s_const, 11)
            for cols, step in ((blk[:, 0:D].rearrange("p (g c) -> p g c", c=HD0), 1), (blk[:, D:].unsqueeze(2), 1)):
                w = cols.shape[2]
                pool.affine_select(out=cols, in_=cols, compare_op=ALU.is_ge, fill=0.0, base=0,
                                   pattern=[[-HD0, HEADS0], [0, w]], channel_multiplier=1).then_inc(s_const, 1)
            pool.wait_ge(s_const, 13)
            for cols in (blk[:, 0:D].rearrange("p (g c) -> p g c", c=HD0), blk[:, D:].unsqueeze(2)):
                w = cols.shape[2]
                pool.affine_select(out=cols, in_=cols, compare_op=ALU.is_ge, fill=0.0, base=HD0 - 1,
                                   pattern=[[HD0, HEADS0], [0, w]], channel_multiplier=-1).then_inc(s_const, 1)
            pool.wait_ge(s_idx, 16)
            for b in range(B):
                for t in range(T):
                    pool.indirect_dma_start(
                        e_in[b][:, t, :], None, a["tables"],
                        bass.IndirectOffsetOnAxis(ap=idx[:, b * T + t:b * T + t + 1], axis=0)).then_inc(s_gather[b], 16)

            def section_A(b, ph):
                i = b % 2
                if ph == 1:
                    wait(pool, "A.dve.eps", b)
                    did(pool.tensor_tensor(rstd[i][:, 0], ve[i][:, 0], mhalf[:, 0], ALU.pow), "A.pool.rstd", b)
                if ph == 3:
                    if b == 0:
                        pool.wait_ge(s_w0, 16 * 5)
                    wait(pool, "A.dve.x3", b)
                    hb = h[:, b * T:(b + 1) * T, :]
                    did(pool.tensor_tensor(hb, hb, bo0[:].unsqueeze(1).to_broadcast([P, T, D]), ALU.add), "A.pool.hb", b)

            def section_B(b, ph):
                i = b % 2
                if ph == 5:
                    wait(pool, "B.act.kabs", b)
                    wait(pool, "B.act.sq", b)
                    wait(pool, "B.dve.fc", b - 1)
                    did(pool.tensor_tensor(amp[:, :, D:], kab[:], sq[i][:, :, D:], ALU.mult), "B.pool.k3", b)

            def section_O(b, ph):
                if ph == 1:
                    wait(pool, "O.dve.eps", b)
                    did(pool.tensor_tensor(rstd_o[:], ve_o[:], mhalf[:, 0], ALU.pow), "O.pool.rstd", b)

            def section_D(b, ph):
                i = b % 2
                hb = h[:, b * T:(b + 1) * T, :]
                if ph == 1:
                    wait(pool, "D.dve.eps", b)
                    did(pool.tensor_tensor(rstd[i][:, 0], ve[i][:, 0], mhalf[:, 0], ALU.pow), "D.pool.rstd", b)
                if ph == 3:
                    pool.wait_ge(s_lnb, 1)
                    wait(pool, "D.dve.x3", b)
                    did(pool.tensor_tensor(hb, hb, lnw[:, 1, :].unsqueeze(1).to_broadcast([P, T, D]), ALU.add),
                        "D.pool.hb", b)

            def section_H(b, ph):
                i = b % 2
                hb = h[:, b * T:(b + 1) * T, :]
                if ph == 6:
                    wait(pool, "H.dve.b2", b)
                    wait(pool, "E.dve.res", b - 1)
                    did(pool.tensor_tensor(xb[:], xn[i][:], wide[:].unsqueeze(1).to_broadcast([P, T, D]), ALU.add),
                        "H.pool.xb", b)

            def section_E(b, ph):
                if ph == 5:
                    wait(pool, "E.dve.eps", b)
                    did(pool.tensor_tensor(rstd_e[:], ve_e[:], mhalf[:, 0], ALU.pow), "E.pool.rstd", b)

            def section_F(b, ph):
                i = b % 2
                hb = h[:, b * T:(b + 1) * T, :]
                if ph == 0:
                    if b == 0:
                        wait(pool, "O.dve.h", B - 1)
                        for j in range(2):
                            pool.memset(qz[j], 0.0).then_inc(s_qz, 1)
                if ph == 1:
                    wait(pool, "F.dve.var", b)
                    did(pool.tensor_tensor(rstd_f[:], ve_f[:], mhalf[:, 0], ALU.pow), "F.pool.rstd", b)
                if ph == 3:
                    if b == 0:
                        pool.wait_ge(s_w2, 16 * 7)
                    wait(pool, "F.dve.x3", b)
                    did(pool.tensor_tensor(hb, hb, bo1[:].unsqueeze(1).to_broadcast([P, T, D]), ALU.add), "F.pool.hb", b)

            def section_I(b, ph):
                i = b % 2
                if ph == 1:
                    wait(pool, "I.dve.vv", b)
                    did(pool.tensor_tensor(rstd[i][:], ve[i][:], mhalf[:], ALU.pow), "I.pool.rstd", b)

            each(order, {"A": section_A, "B": section_B, "O": section_O, "D": section_D, "H": section_H,
                         "E": section_E, "F": section_F, "I": section_I})

        @block.tensor
        def _(pe):
            pe.wait_ge(s_gw2b, 1)
            for t in range(TABLES):
                last = pe.matmul(bank[7][:, t * (DIM + 1):(t + 1) * (DIM + 1)], gw2b[:, t, :], gw1[:, t, :],
                                 start=True, stop=True)
            last.then_inc(s_gv, 1)
            pe.wait_ge(s_ident, 2)
            pe.wait_ge(s_wtok, 16 * 6)
            pe.wait_ge(s_const, 4)
            pe.matmul(bank[6][:, 0:2 * D], lnco[:], lnr[:], start=True, stop=True).then_inc(s_lnw, 1)

            def section_T(b, ph):
                i = b % 2
                if ph == 3:
                    p1 = room(pe, "T.tr1", b)
                    wait(pe, "T.dve.scaled", b)
                    for t in range(T):
                        last = pe.transpose(p1[:, t * P:(t + 1) * P], e_sc[i][:, t, 0:P], ident[:])
                    did(last, "T.pe.tr1", b)
                    p2 = room(pe, "T.tr2", b)
                    for t in range(T):
                        last = pe.transpose(p2[0:ES - P, t * P:(t + 1) * P], e_sc[i][:, t, P:ES], ident[:])
                    did(last, "T.pe.tr2", b)
                if ph == 5:
                    p3 = room(pe, "T.h", b)
                    if b == 0:
                        pe.wait_ge(s_wtok, 16 * 6)
                    wait(pe, "T.act.eT1", b)
                    wait(pe, "T.act.eT2", b)
                    for t in range(T):
                        tk = slice(t * P, (t + 1) * P)
                        pe.matmul(p3[:, tk], eT1[i][:, tk], wtok1[:], start=True, stop=False)
                        last = pe.matmul(p3[:, tk], eT2[i][:, tk], wtok2[:], start=False, stop=True)
                    did(last, "T.pe.h", b)

            def section_A(b, ph):
                i = b % 2
                if ph == 3:
                    p = room(pe, "A.tr", b)
                    wait(pe, "A.dve.x3", b)
                    for t in range(T):
                        last = pe.transpose(p[:, t * P:(t + 1) * P], xn[i][:, t, :], ident[:])
                    did(last, "A.pe.tr", b)
                if ph == 5:
                    if b == 0:
                        pe.wait_ge(s_w0, 16 * 5)
                    for t in range(T):
                        p = room(pe, "A.qkv%d" % t, b)
                        wait(pe, "A.act.xT", b)
                        did(pe.matmul(p[:, 0:3 * D], xT[i][:, t * P:(t + 1) * P], wqkv0[:], start=True, stop=True),
                            "A.pe.qkv%d" % t, b)

            def section_C(b, ph):
                i = b % 2
                if ph == 0:
                    p = room(pe, "C.trc", b)
                    wait(pe, "B.dve.fc", b)
                    for t in range(T):
                        last = pe.transpose(p[:, t * P:(t + 1) * P], fc[i][:, t, 0:D], ident[:])
                    did(last, "C.pe.trc", b)
                    p = room(pe, "C.trs", b)
                    for t in range(T):
                        last = pe.transpose(p[:, t * P:(t + 1) * P], fs[i][:, t, 0:D], ident[:])
                    did(last, "C.pe.trs", b)
                    p = room(pe, "C.kv", b)
                    for half, f in enumerate((fc, fs)):
                        for t in range(T):
                            last = pe.matmul(p[:, half * (D + 1):(half + 1) * (D + 1)], f[i][:, t, D:2 * D],
                                             qkv[i][:, t, 2 * D:3 * D + 1], start=(t == 0), stop=(t == T - 1))
                    did(last, "C.pe.kv", b)
                if ph == 2:
                    for n in range(2):
                        p = room(pe, "C.o%d" % n, b)
                        wait(pe, "C.act.qs", b)
                        wait(pe, "C.dve.km1", b)
                        for j in range(2):
                            t = 2 * n + j
                            at = p[:, j * (D + HEADS0):(j + 1) * (D + HEADS0)]
                            pe.matmul(at, qc[:, t * P:(t + 1) * P], kvm[:, 0, :], start=True, stop=False)
                            last = pe.matmul(at, qs[:, t * P:(t + 1) * P], kvm[:, 1, :], start=False, stop=True)
                        did(last, "C.pe.o%d" % n, b)

            def section_O(b, ph):
                i = b % 2
                if ph == 3:
                    p = room(pe, "O.tr", b)
                    wait(pe, "O.dve.x3", b)
                    for t in range(T):
                        last = pe.transpose(p[:, t * P:(t + 1) * P], on[:, t, :], ident[:])
                    did(last, "O.pe.tr", b)
                if ph == 5:
                    p = room(pe, "O.out", b)
                    wait(pe, "O.act.oT", b)
                    for t in range(T):
                        last = pe.matmul(p[:, t * P:(t + 1) * P], oT[:, t * P:(t + 1) * P], wo0[:], start=True, stop=True)
                    did(last, "O.pe.out", b)

            def section_D(b, ph):
                i = b % 2
                if ph == 3:
                    p = room(pe, "D.tr", b)
                    wait(pe, "D.dve.x3", b)
                    for t in range(T):
                        last = pe.transpose(p[:, t * P:(t + 1) * P], xn[i][:, t, :], ident[:])
                    did(last, "D.pe.tr", b)

            def section_H(b, ph):
                i = b % 2
                if ph == 0:
                    p = room(pe, "H.gh", b)
                    if b == 0:
                        pe.wait_ge(s_w1, 16 * 12)
                    wait(pe, "D.act.xT", b)
                    did(pe.matmul(p[:], g1t[:], xT[i][:], start=True, stop=True), "H.pe.gh", b)
                if ph == 2:
                    p = room(pe, "H.g", b)
                    wait(pe, "H.act.gh", b)
                    did(pe.matmul(p[:, 0:1], g2r[:], gs[i][:], start=True, stop=True), "H.pe.g", b)
                if ph == 4:
                    for name, w in (("w1", tv1), ("w2", tv2)):
                        p = room(pe, "H." + name, b)
                        wait(pe, "H.dve.sel", b)
                        for r in range(2):
                            for c in range(4):
                                last = pe.matmul(p[2 * J * c:2 * J * (c + 1), :], selg[i][:, r, :], w[:, 2 * c + r, :],
                                                 start=(r == 0), stop=(r == 1), skip_group_check=True)
                        did(last, "H.pe." + name, b)
                    p = room(pe, "H.b", b)
                    wait(pe, "H.dve.gb", b)
                    for c in range(FC):
                        pe.matmul(p[:, c:c + 1], tvb1[:, c * P:(c + 1) * P], grow[i][:], start=True, stop=True)
                    did(pe.matmul(p[:, P:2 * P], gb[:], tvb2[:], start=True, stop=True), "H.pe.b", b)

            def feed(name, n, x, w1, w2, hid, ph, last_x):
                if ph < 2:
                    for c in (range(FC) if name == "J" else range(2 * ph, 2 * ph + 2)):
                        p = room(pe, "%s.up%d" % (name, c), n)
                        if last_x:
                            wait(pe, *last_x)
                        did(pe.matmul(p[:], w1[:, c * P:(c + 1) * P], x, start=True, stop=True),
                            "%s.pe.up%d" % (name, c), n)
                else:
                    p = room(pe, name + ".down", n)
                    wait(pe, "%s.act.ht3" % name, n)
                    for t in range(T):
                        for c in range(FC):
                            last = pe.matmul(p[:, t * P:(t + 1) * P], hid[:, c, t * P:(t + 1) * P],
                                             w2[:, c * D:(c + 1) * D], start=(c == 0), stop=(c == FC - 1))
                    did(last, name + ".pe.down", n)

            def section_E(b, ph):
                i = b % 2
                if ph in (0, 1, 3):
                    feed("E", b, xT[i][:], w1m[i], w2m[i], ht[i], ph, ("H.dve.b1", b))

            def section_F(b, ph):
                i = b % 2
                if ph == 3:
                    p = room(pe, "F.tr", b)
                    wait(pe, "F.dve.x3", b)
                    for t in range(T):
                        last = pe.transpose(p[:, t * P:(t + 1) * P], xn_f[:, t, :], ident[:])
                    did(last, "F.pe.tr", b)
                if ph == 5:
                    if b == 0:
                        pe.wait_ge(s_w2, 16 * 7)
                    for j in range(PAIRS):
                        p = room(pe, "F.a%d" % j, b)
                        wait(pe, "F.act.xT", b)
                        did(pe.matmul(p[:], wq[:, 3 * 512 + j * P:3 * 512 + (j + 1) * P], xT_f[:], start=True, stop=True),
                            "F.pe.a%d" % j, b)
                if ph == 6:
                    for t in range(T):
                        p = room(pe, "F.v%d" % t, b)
                        did(pe.matmul(p[:], xT_f[:, t * P:(t + 1) * P], wq[:, 2 * 512:3 * 512], start=True, stop=True),
                            "F.pe.v%d" % t, b)
                if 12 <= ph < 16:
                    j = ph - 12
                    for at, name in enumerate("qk"):
                        p = room(pe, "F.%s%d" % (name, j), b)
                        did(pe.matmul(p[:], wq[:, at * 512 + j * P:at * 512 + (j + 1) * P], xT_f[:], start=True, stop=True),
                            "F.pe.%s%d" % (name, j), b)

            def section_G(n, ph):
                b, c = n // T, n % T
                i, k = b % 2, n % 2
                tk = slice(c * P, (c + 1) * P)
                if ph == 0:
                    p = room(pe, "G.tr", n)
                    wait(pe, "F.dve.k3", b)
                    for j in range(PAIRS):
                        last = pe.transpose(p[:, j * P:(j + 1) * P], kk[i][:, j, tk], ident[:])
                    did(last, "G.pe.tr", n)
                    for m in range(2):
                        p = room(pe, "G.qk%d" % m, n)
                        for j in (2 * m, 2 * m + 1):
                            at = p[:, (j % 2) * 2 * P:(j % 2 + 1) * 2 * P].rearrange("p (g s) -> p g s", g=2)
                            last = pe.matmul(at, kk[i][:, j, tk], qz[i][:, j, :, tk], start=True, stop=True)
                        did(last, "G.pe.qk%d" % m, n)
                if ph == 2:
                    p = room(pe, "G.av", n)
                    wait(pe, "G.dve.m1", n)
                    if c:
                        wait(pe, "G.act.s", n - 1)
                    for j in range(PAIRS):
                        for m in range(2):
                            last = pe.matmul(p[m * HD1:(m + 1) * HD1, j * P:(j + 1) * P],
                                             vv[i][:, c, (2 * j + m) * HD1:(2 * j + m + 1) * HD1], sim[k][:, j, m, :],
                                             start=True, stop=(c == 0), skip_group_check=True)
                        if c:
                            for m in range(2):
                                last = pe.matmul(p[m * HD1:(m + 1) * HD1, j * P:(j + 1) * P],
                                                 ss[(n - 1) % 2][:, j, m * HD1:(m + 1) * HD1], qz[i][:, j, m, tk],
                                                 start=False, stop=True, skip_group_check=True)
                    did(last, "G.pe.av", n)
                    wait(pe, "G.act.kt", n)
                    wait(pe, "G.act.s", n - 1)
                    for j in range(PAIRS):
                        last = pe.matmul(bank[7][:, j * P:(j + 1) * P], kt[k][:, j, :], vv[i][:, c, j * P:(j + 1) * P],
                                         start=(c == 0 and j == 0), stop=True, skip_group_check=True)
                    did(last, "G.pe.kv", n)
                if ph == 4:
                    p = room(pe, "G.out", n)
                    wait(pe, "G.act.o", n)
                    for j in range(PAIRS):
                        last = pe.matmul(p[:, 0:D], oc[k][:, j, :], wo1[:, j, :], start=(j == 0), stop=(j == PAIRS - 1))
                    did(last, "G.pe.out", n)

            def section_I(b, ph):
                if ph == 3:
                    p = room(pe, "I.tr", b)
                    wait(pe, "I.dve.y3", b)
                    for t in range(T):
                        last = pe.transpose(p[:, t * P:(t + 1) * P], xn[0][:, t, :], ident[:])
                    did(last, "I.pe.tr", b)
                if ph == 5:
                    p = room(pe, "I.lg", b)
                    wait(pe, "I.act.xT", b)
                    for t in range(T):
                        last = pe.matmul(p[:, t * E:(t + 1) * E], xT[b % 2][:, t * P:(t + 1) * P], gate[:], start=True, stop=True)
                    did(last, "I.pe.lg", b)
                if ph == 9:
                    p = room(pe, "I.cT", b)
                    wait(pe, "I.dve.c", b)
                    for t in range(T):
                        last = pe.transpose(p[0:E, t * P:(t + 1) * P], cmb[b][:, t, :], ident[:])
                    did(last, "I.pe.cT", b)
                if ph == 11:
                    p = room(pe, "I.b2", b)
                    wait(pe, "I.act.cT", b)
                    for t in range(T):
                        last = pe.matmul(p[:, t * P:(t + 1) * P], cT[:, t * P:(t + 1) * P], eb2[:], start=True, stop=True)
                    did(last, "I.pe.b2", b)

            def section_J(n, ph):
                b, e = n // E, n % E
                if n == 0 and ph == 0:
                    pe.wait_ge(s_w3, 16 * 7)
                if ph in (0, 2):
                    feed("J", n, xT[b % 2][:], ew1[:, e, :], ew2[:, e, :], hj[n % 2], ph, None)

            each(order, {"T": section_T, "A": section_A, "C": section_C, "O": section_O, "D": section_D,
                         "H": section_H, "E": section_E, "F": section_F, "G": section_G, "I": section_I,
                         "J": section_J})

        @block.scalar
        def _(act):
            act.wait_ge(s_const, 15)

            def section_T(b, ph):
                i = b % 2
                if ph == 1:
                    wait(act, "T.dve.sub", b)
                    did(act.activation(lg[i][:, 3], lg[i][:, 2], ACT.Exp), "T.act.exp", b)
                if ph == 4:
                    wait(act, "T.pe.tr1", b)
                    wait(act, "T.pe.h", b - 2)
                    did(act.activation(eT1[i][:], of("T.tr1", b)[:], ACT.Copy), "T.act.eT1", b)
                    wait(act, "T.pe.tr2", b)
                    did(act.activation(eT2[i][:], of("T.tr2", b)[0:ES - P, :], ACT.Copy), "T.act.eT2", b)

            def section_A(b, ph):
                if ph == 4:
                    wait(act, "A.pe.tr", b)
                    wait(act, "A.pe.qkv3", b - 2)
                    did(act.activation(xT[b % 2][:], of("A.tr", b)[:], ACT.Copy), "A.act.xT", b)

            def section_B(b, ph):
                i = b % 2
                qk = qkv[i][:, :, 0:2 * D]
                if ph == 0:
                    wait(act, "A.dve.qkv3", b)
                    wait(act, "B.pool.k3", b - 2)
                    did(act.activation(sq[i][:], qk, ACT.Square), "B.act.sq", b)
                if ph == 2:
                    wait(act, "B.dve.n2", b)
                    did(act.activation(n2[i][:, 1], n2[i][:, 0], ACT.Ln), "B.act.ln", b)
                    wait(act, "B.act.ln", b)
                    did(act.activation(n2[i][:, 2], n2[i][:, 1], ACT.Exp, scale=-0.5), "B.act.rn", b)
                    did(act.activation(n2[i][:, 3], n2[i][:, 1], ACT.Exp, scale=0.5), "B.act.qn", b)
                if ph == 4:
                    wait(act, "B.dve.u", b)
                    did(act.activation(lnu[:], u[:, :, 0:D], ACT.Square), "B.act.uu", b)
                    wait(act, "B.act.uu", b)
                    did(act.activation(lnu[:], lnu[:], ACT.Ln, bias=tiny[:]), "B.act.lnu", b)
                    wait(act, "B.pool.k3", b - 1)
                    did(act.activation(kab[:], qk[:, :, D:], ACT.Abs), "B.act.kabs", b)
                    did(act.activation(tq[:], n2[i][:, 3].rearrange("p (t g) -> p t g", g=16)[:, :, 0:HEADS0], ACT.Tanh),
                        "B.act.tq", b)
                    wait(act, "B.act.cos", b - 1)
                    did(act.activation(th[:], u[:], ACT.Tanh, scale=20.0), "B.act.tanh", b)
                if ph == 6:
                    wait(act, "B.dve.pl", b)
                    wait(act, "B.dve.fc", b - 1)
                    did(act.activation(amp[:, :, 0:D], lnu[:], ACT.Exp, scale=1.5), "B.act.qt", b)
                    wait(act, "B.act.tanh", b)
                    did(act.activation(sn[:], th[:], ACT.Sin, scale=HALF_PI / 2), "B.act.sin", b)
                    did(act.activation(cs[:], th[:], ACT.Sin, scale=HALF_PI / 2, bias=half_pi[:]), "B.act.cos", b)

            def section_C(b, ph):
                if ph == 1:
                    wait(act, "C.pe.trc", b)
                    wait(act, "C.pe.o1", b - 1)
                    did(act.activation(qc[:], of("C.trc", b)[:], ACT.Copy), "C.act.qc", b)
                    wait(act, "C.pe.trs", b)
                    did(act.activation(qs[:], of("C.trs", b)[:], ACT.Copy), "C.act.qs", b)

            def section_O(b, ph):
                if ph == 4:
                    wait(act, "O.pe.tr", b)
                    wait(act, "O.pe.out", b - 1)
                    did(act.activation(oT[:], of("O.tr", b)[:], ACT.Identity, bias=lngb0[:, 1:2], scale=lngb0[:, 0:1]),
                        "O.act.oT", b)

            act.wait_ge(s_w0, 16 * 5)
            def section_D(b, ph):
                i = b % 2
                if ph == 4:
                    wait(act, "D.pe.tr", b)
                    wait(act, "E.pe.up3", b - 2)
                    wait(act, "A.pe.qkv3", B - 1 - (b + 1) % 2)
                    did(act.activation(xT[i][:], of("D.tr", b)[:], ACT.Copy), "D.act.xT", b)

            def section_H(b, ph):
                i = b % 2
                if ph == 1:
                    wait(act, "H.pe.gh", b)
                    wait(act, "H.act.gh", b - 1)
                    did(act.activation(junk, of("H.gh", b)[:], ACT.Relu, bias=gcol[:, 0:1], accum_out=gs[i][:]), "H.act.gh", b)

            def section_E(b, ph):
                i = b % 2
                if ph in (1, 2):
                    for c in (2 * ph - 2, 2 * ph - 1):
                        wait(act, "E.pe.up%d" % c, b)
                        wait(act, "E.pe.down", b - 2)
                        did(act.activation(ht[i][:, c, :], of("E.up%d" % c, b)[:], ACT.Relu, bias=b1m[i][:, c:c + 1]),
                            "E.act.ht%d" % c, b)

            def section_F(b, ph):
                i = b % 2
                if ph == 4:
                    if b == 0:
                        act.wait_ge(s_w2, 16 * 7)
                        act.activation(gam2[:], gam[:], ACT.Copy, scale=float(D) ** 0.5).then_inc(s_gam, 1)
                        act.activation(nba[:], bq1[:, 2, :], ACT.Copy, scale=-1.0).then_inc(s_gam, 1)
                        act.wait_ge(s_gam, 2)
                    wait(act, "F.pe.tr", b)
                    wait(act, "F.pe.k3", b - 1)
                    did(act.activation(xT_f[:], of("F.tr", b)[:], ACT.Copy, scale=gam2[:]), "F.act.xT", b)
                if ph == 6:
                    if b == 0:
                        wait(act, "O.dve.h", B - 1)
                    for j in range(PAIRS):
                        wait(act, "F.pe.a%d" % j, b)
                        wait(act, "F.dve.k3", b - 1)
                        did(act.activation(la[:, j, :], of("F.a%d" % j, b)[:], ACT.Exp, scale=-1.0, bias=nba[:, j:j + 1]),
                            "F.act.e%d" % j, b)
                if ph == 8:
                    wait(act, "F.dve.e", b)
                    did(act.activation(la[:], la[:], ACT.Ln, bias=one[:]), "F.act.l", b)
                if ph == 11:
                    wait(act, "F.dve.cut", b)
                    did(act.activation(lb[:], lb[:], ACT.Exp, scale=-1.0), "F.act.cum", b)
                    did(act.activation(la[:], la[:], ACT.Exp), "F.act.inv", b)

            def section_G(n, ph):
                k = n % 2
                if ph == 1:
                    if n == 0:
                        wait(act, "E.dve.h", B - 1)
                    wait(act, "G.pe.tr", n)
                    wait(act, "G.pe.kv", n - 2)
                    did(act.activation(kt[k][:].rearrange("p a b -> p (a b)"), of("G.tr", n)[:], ACT.Copy), "G.act.kt", n)
                if ph == 3:
                    wait(act, "G.pe.av", n)
                    wait(act, "G.pe.out", n - 2)
                    did(act.activation(oc[k][:].rearrange("p a b -> p (a b)"), of("G.av", n)[:], ACT.Copy), "G.act.o", n)
                    wait(act, "G.pe.kv", n)
                    did(act.activation(ss[k][:].rearrange("p a b -> p (a b)"), bank[7][:], ACT.Copy, scale=HD1 ** -0.5),
                        "G.act.s", n)

            def section_I(b, ph):
                if ph == 4:
                    if b == 0:
                        act.wait_ge(s_w3, 16 * 7)
                    wait(act, "I.pe.tr", b)
                    wait(act, "J.pe.up3", E * (b - 1) - 1)
                    did(act.activation(xT[b % 2][:], of("I.tr", b)[:], ACT.Identity, bias=lngb1[:, 1:2], scale=lngb1[:, 0:1]),
                        "I.act.xT", b)
                if ph == 7:
                    wait(act, "I.dve.sub", b)
                    did(act.activation(rt[:, 1], rt[:, 0], ACT.Exp), "I.act.exp", b)
                if ph == 10:
                    wait(act, "I.pe.cT", b)
                    wait(act, "I.pe.b2", b - 1)
                    did(act.activation(cT[:], of("I.cT", b)[0:E, :], ACT.Copy), "I.act.cT", b)

            def section_J(n, ph):
                e = n % E
                if ph == 1:
                    for c in range(FC):
                        wait(act, "J.pe.up%d" % c, n)
                        wait(act, "J.pe.down", n - 2)
                        did(act.activation(hj[n % 2][:, c, :], of("J.up%d" % c, n)[:], ACT.Gelu, bias=eb1[:, e, c:c + 1]),
                            "J.act.ht%d" % c, n)

            each(order, {"T": section_T, "A": section_A, "B": section_B, "C": section_C, "O": section_O,
                         "D": section_D, "H": section_H, "E": section_E, "F": section_F, "G": section_G,
                         "I": section_I, "J": section_J})

        @block.vector
        def _(dve):
            dve.wait_ge(s_wtok, 16 * 6)
            dve.tensor_copy(gw2b[:], gw2[:].unsqueeze(2).to_broadcast([GATE_H, TABLES, P])).then_inc(s_gw2b, 1)
            dve.wait_ge(s_gv, 1)
            dve.tensor_copy(gatev[:], bank[7][:, 0:TABLES * (DIM + 1)].rearrange("p (t c) -> p t c", t=TABLES))\
               .then_inc(s_gatev, 1)
            dve.wait_ge(s_gatev, 1)
            dve.tensor_tensor(gb2[:], gb2[:], gatev[:, :, DIM], ALU.add).then_inc(s_banks, 1)
            dve.wait_ge(s_banks, 1)

            def statistics(name, b, src, stats, means, v_eps=None):
                for t in range(T):
                    did(dve.bn_stats(stats[:, t, :], src[:, t, :]), "%s.dve.st%d" % (name, t), b)
                for t in range(T):
                    wait(dve, "%s.dve.st%d" % (name, t), b)
                    did(dve.bn_aggr(means[:, t, :], stats[:, t, :]), "%s.dve.mv%d" % (name, t), b)
                wait(dve, "%s.dve.mv3" % name, b)
                if name in "AODE":
                    did(dve.tensor_scalar(v_eps, means[:, :, 1], EPS, None, ALU.add), name + ".dve.eps", b)

            def normalise(name, b, src, means, scale, dst):
                wait(dve, "%s.pool.rstd" % name, b)
                for t in range(T):
                    did(dve.tensor_scalar(dst[:, t, :], src[:, t, :], means[:, t, 0:1], scale[:, t:t + 1],
                                          ALU.subtract, ALU.mult), "%s.dve.x%d" % (name, t), b)

            dve.wait_ge(s_lnw, 1)
            dve.tensor_copy(lnw[:], bank[6][:, 0:2 * D].rearrange("p (a c) -> p a c", a=2)).then_inc(s_lnb, 1)
            dve.wait_ge(s_lnb, 1)

            def section_T(b, ph):
                i = b % 2
                ein = e_in[b][:].rearrange("p t (a c) -> p t a c", a=TABLES)
                epr = e_pr[:].rearrange("p t (a c) -> p t a c", a=TABLES)
                esc = e_sc[i][:, :, 0:TABLES * DIM].rearrange("p t (a c) -> p t a c", a=TABLES)
                alpha = e_sc[i][:, :, TABLES * DIM:]
                if ph == 0:
                    dve.wait_ge(s_gather[b], 16 * T)
                    did(dve.tensor_tensor(epr, ein, gatev[:, :, 0:DIM].unsqueeze(1).to_broadcast([P, T, TABLES, DIM]),
                                          ALU.mult), "T.dve.prod", b)
                    wait(dve, "T.dve.prod", b)
                    did(dve.tensor_reduce(lg[i][:, 0], epr, X, ALU.add), "T.dve.sum", b)
                    wait(dve, "T.dve.sum", b)
                    did(dve.tensor_tensor(lg[i][:, 1], lg[i][:, 0], gb2[:].unsqueeze(1).to_broadcast([P, T, TABLES]),
                                          ALU.add), "T.dve.bias", b)
                    wait(dve, "T.dve.bias", b)
                    did(dve.tensor_reduce(lg[i][:, 4, :, 0], lg[i][:, 1], X, ALU.max), "T.dve.max", b)
                    wait(dve, "T.dve.max", b)
                    did(dve.tensor_tensor(lg[i][:, 2], lg[i][:, 1], lg[i][:, 4, :, 0:1].to_broadcast([P, T, TABLES]),
                                          ALU.subtract), "T.dve.sub", b)
                if ph == 2:
                    wait(dve, "T.act.exp", b)
                    did(dve.tensor_reduce(lg[i][:, 4, :, 1], lg[i][:, 3], X, ALU.add), "T.dve.den", b)
                    wait(dve, "T.dve.den", b)
                    did(dve.reciprocal(lg[i][:, 4, :, 2], lg[i][:, 4, :, 1]), "T.dve.rden", b)
                    wait(dve, "T.dve.rden", b)
                    wait(dve, "T.pe.tr2", b - 2)
                    did(dve.tensor_tensor(alpha, lg[i][:, 3], lg[i][:, 4, :, 2:3].to_broadcast([P, T, TABLES]),
                                          ALU.mult), "T.dve.alpha", b)
                    wait(dve, "T.dve.alpha", b)
                    did(dve.tensor_tensor(esc, ein, alpha.unsqueeze(3).to_broadcast([P, T, TABLES, DIM]),
                                          ALU.mult), "T.dve.scaled", b)
                if ph == 6:
                    wait(dve, "T.pe.h", b)
                    did(dve.tensor_copy(h[:, b * T:(b + 1) * T, :], of("T.h", b)[:].rearrange("p (t c) -> p t c", t=T)), "T.dve.h", b)

            def section_A(b, ph):
                i = b % 2
                if ph == 0:
                    wait(dve, "T.dve.h", b)
                    statistics("A", b, h[:, b * T:(b + 1) * T, :], stat[i], mv[i], ve[i][:, 0])
                if ph == 2:
                    wait(dve, "A.pe.tr", b - 2)
                    normalise("A", b, h[:, b * T:(b + 1) * T, :], mv[i], rstd[i][:, 0], xn[i])
                if ph == 6:
                    if b == 0:
                        dve.wait_ge(s_w0, 16 * 5)
                    for t in range(T):
                        wait(dve, "A.pe.qkv%d" % t, b)
                        wait(dve, "C.pe.kv", b - 2)
                        did(dve.tensor_tensor(qkv[i][:, t, 0:3 * D], of("A.qkv%d" % t, b)[:, 0:3 * D], bqkv0[:], ALU.add),
                            "A.dve.qkv%d" % t, b)

            def section_B(b, ph):
                i = b % 2
                qk = qkv[i][:, :, 0:2 * D].rearrange("p t (g c) -> p t g c", c=HD0)
                if ph == 1:
                    wait(dve, "B.act.sq", b)
                    did(dve.tensor_reduce(n2[i][:, 0].rearrange("p (t g) -> p t g", t=T),
                                          sq[i][:].rearrange("p t (g c) -> p t g c", c=HD0), X, ALU.add), "B.dve.n2", b)
                if ph == 3:
                    wait(dve, "B.act.rn", b)
                    wait(dve, "B.act.tanh", b - 1)
                    rn = n2[i][:, 2].rearrange("p (t g) -> p t g", t=T)
                    did(dve.tensor_tensor(u[:].rearrange("p t (g c) -> p t g c", c=HD0), qk,
                                          rn.unsqueeze(3).to_broadcast([P, T, 16, HD0]), ALU.mult), "B.dve.u", b)
                if ph == 5:
                    wait(dve, "B.act.tq", b)
                    did(dve.tensor_scalar(pw[:], tq[:].rearrange("p t g -> p (t g)"), 0.5, None, ALU.add), "B.dve.pw", b)
                    wait(dve, "B.dve.pw", b)
                    l = lnu[:].rearrange("p t (g c) -> p (t g) c", c=HD0)
                    did(dve.tensor_tensor(l, l, pw[:].unsqueeze(2).to_broadcast([P, T * HEADS0, HD0]), ALU.mult), "B.dve.pl", b)
                if ph == 7:
                    wait(dve, "B.act.sin", b)
                    wait(dve, "B.pool.k3", b)
                    wait(dve, "C.pe.kv", b - 2)
                    did(dve.tensor_tensor(fs[i][:], amp[:], sn[:], ALU.mult), "B.dve.fs", b)
                    wait(dve, "B.act.cos", b)
                    did(dve.tensor_tensor(fc[i][:], amp[:], cs[:], ALU.mult), "B.dve.fc", b)

            def section_C(b, ph):
                i = b % 2
                if ph == 1:
                    wait(dve, "C.pe.kv", b)
                    wait(dve, "C.pe.o1", b - 1)
                    p = of("C.kv", b)
                    for n in range(2):
                        did(dve.tensor_tensor(kvm[:, n, 0:D], p[:, n * (D + 1):n * (D + 1) + D], blk[:, 0:D], ALU.mult),
                            "C.dve.kv%d" % n, b)
                    for n in range(2):
                        did(dve.tensor_scalar(kvm[:, n, D:], blk[:, D:], p[:, n * (D + 1) + D:(n + 1) * (D + 1)], None, ALU.mult),
                            "C.dve.km%d" % n, b)
                if ph == 3:
                    part = [of("C.o%d" % n, b)[:, 0:2 * (D + HEADS0)].rearrange("p (t c) -> p t c", t=2) for n in range(2)]
                    for n in range(2):
                        wait(dve, "C.pe.o%d" % n, b)
                        did(dve.tensor_scalar(den[:, n * 16:(n + 1) * 16].rearrange("p (t g) -> p t g", t=2),
                                              part[n][:, :, D:], 1e-6, None, ALU.add), "C.dve.den%d" % n, b)
                    wait(dve, "C.dve.den1", b)
                    did(dve.reciprocal(rden[:], den[:]), "C.dve.z", b)
                    wait(dve, "C.dve.z", b)
                    for n in range(2):
                        z = rden[:, n * 16:(n + 1) * 16].rearrange("p (t g) -> p t g", t=2).unsqueeze(3).to_broadcast([P, 2, HEADS0, HD0])
                        did(dve.tensor_tensor(o[:, 2 * n:2 * n + 2, :].rearrange("p t (g c) -> p t g c", c=HD0),
                                              part[n][:, :, 0:D].rearrange("p t (g c) -> p t g c", c=HD0), z, ALU.mult),
                            "C.dve.o%d" % n, b)

            def section_O(b, ph):
                i = b % 2
                if ph == 0:
                    wait(dve, "C.dve.o1", b)
                    statistics("O", b, o, stat_o, mv_o, ve_o[:])
                if ph == 2:
                    normalise("O", b, o, mv_o, rstd_o, on)
                if ph == 6:
                    hb = h[:, b * T:(b + 1) * T, :]
                    wait(dve, "O.pe.out", b)
                    wait(dve, "A.pool.hb", b)
                    did(dve.tensor_tensor(hb, hb, of("O.out", b)[:].rearrange("p (t c) -> p t c", t=T), ALU.add), "O.dve.h", b)

            def section_D(b, ph):
                i = b % 2
                hb = h[:, b * T:(b + 1) * T, :]
                if ph == 0:
                    wait(dve, "O.dve.h", b)
                    statistics("D", b, hb, stat[i], mv[i], ve[i][:, 0])
                if ph == 2:
                    wait(dve, "H.pool.xb", b - 2)
                    wait(dve, "A.pe.tr", B - 1 - (b + 1) % 2)
                    normalise("D", b, hb, mv[i], rstd[i][:, 0], xn[i])

            def section_H(b, ph):
                i = b % 2
                hb = h[:, b * T:(b + 1) * T, :]
                if ph == 3:
                    wait(dve, "H.pe.g", b)
                    did(dve.tensor_scalar(grow[i][:], of("H.g", b)[:, 0:1], 1.0 / S, gcol[:, 1:2], ALU.mult, ALU.add),
                        "H.dve.g", b)
                    wait(dve, "H.dve.g", b)
                    did(dve.tensor_scalar(selg[i][:], sel[:], grow[i][:], None, ALU.mult), "H.dve.sel", b)
                    wait(dve, "H.pe.b", b - 1)
                    did(dve.tensor_copy(gb[:], grow[i][:].to_broadcast([P, P])), "H.dve.gb", b)
                if ph == 5:
                    if b == 0:
                        wait(dve, "T.pe.h", B - 1)
                    wait(dve, "H.pe.w1", b)
                    wait(dve, "E.pe.down", b - 2)
                    did(dve.tensor_tensor(w1m[i][:], of("H.w1", b)[:], w1t[:], ALU.add), "H.dve.w1", b)
                    wait(dve, "H.pe.w2", b)
                    did(dve.tensor_tensor(w2m[i][:], of("H.w2", b)[:], w2t[:], ALU.add), "H.dve.w2", b)
                    wait(dve, "H.pe.b", b)
                    did(dve.tensor_tensor(b1m[i][:], of("H.b", b)[:, 0:FC], b1t[:], ALU.add), "H.dve.b1", b)
                    wait(dve, "H.pool.xb", b - 1)
                    did(dve.tensor_tensor(wide[:], of("H.b", b)[:, P:2 * P], b2w[:], ALU.add), "H.dve.b2", b)

            def section_E(b, ph):
                hb = h[:, b * T:(b + 1) * T, :]
                if ph == 4:
                    wait(dve, "E.pe.down", b)
                    wait(dve, "H.pool.xb", b)
                    did(dve.tensor_tensor(res[:], of("E.down", b)[:].rearrange("p (t c) -> p t c", t=T), xb[:], ALU.add),
                        "E.dve.res", b)
                    wait(dve, "E.dve.res", b)
                    statistics("E", b, res, stat_e, mv_e, ve_e[:])
                if ph == 6:
                    normalise("E", b, res, mv_e, rstd_e, rn)
                    wait(dve, "E.dve.x3", b)
                    did(dve.tensor_tensor(rn[:], rn[:], lnw[:, 0, :].unsqueeze(1).to_broadcast([P, T, D]), ALU.mult),
                        "E.dve.g", b)
                    wait(dve, "E.dve.g", b)
                    wait(dve, "D.pool.hb", b)
                    did(dve.tensor_tensor(hb, hb, rn[:], ALU.add), "E.dve.h", b)

            def section_F(b, ph):
                i = b % 2
                hb = h[:, b * T:(b + 1) * T, :]
                if ph == 0:
                    wait(dve, "E.dve.h", b)
                    statistics("F", b, hb, stat_f, mv_f)
                    did(dve.tensor_scalar(low[:], mv_f[:, :, 1], EPS, 1e-24, ALU.add, ALU.mult), "F.dve.lo", b)
                    wait(dve, "F.dve.lo", b)
                    did(dve.scalar_tensor_tensor(ve_f[:], mv_f[:, :, 1], float(D), low[:], ALU.mult, ALU.max),
                        "F.dve.var", b)
                if ph == 2:
                    wait(dve, "F.pe.tr", b - 1)
                    normalise("F", b, hb, mv_f, rstd_f[:], xn_f)
                if ph == 7:
                    wait(dve, "F.act.e3", b)
                    la2 = la[:].rearrange("p a b -> p (a b)")
                    did(dve.tensor_scalar(la2, la2, 1e10, None, ALU.min), "F.dve.e", b)
                    if b == 0:
                        dve.wait_ge(s_w2, 16 * 7)
                    for t in range(T):
                        wait(dve, "F.pe.v%d" % t, b)
                        wait(dve, "G.pe.kv", (b - 2) * T + 3)
                        did(dve.tensor_tensor(vv[i][:, t, :], of("F.v%d" % t, b)[:], bv1[:], ALU.add), "F.dve.v%d" % t, b)
                if ph == 9:
                    wait(dve, "F.act.l", b)
                    for j in range(PAIRS):
                        did(dve.tensor_tensor_scan(lb[:, j, :], la[:, j, :], la[:, j, :], 0.0, ALU.add, ALU.bypass),
                            "F.dve.sum%d" % j, b)
                if ph == 10:
                    wait(dve, "F.dve.sum3", b)
                    did(dve.tensor_scalar(la[:].rearrange("p a b -> p (a b)"), lb[:].rearrange("p a b -> p (a b)"),
                                          LN_INV_MAX, None, ALU.min), "F.dve.cut", b)
                if 13 <= ph < 17:
                    j = ph - 13
                    wait(dve, "F.act.inv", b)
                    wait(dve, "G.pe.av", (b - 2) * T + 3)
                    dve.wait_ge(s_qz, min(b + 1, 2))
                    wait(dve, "F.pe.q%d" % j, b)
                    for m, name in enumerate(("qa", "qb")):
                        rows = slice(m * HD1, (m + 1) * HD1)
                        did(dve.scalar_tensor_tensor(qz[i][rows, j, m, :], of("F.q%d" % j, b)[rows, :], bq1[rows, 0, j:j + 1],
                                                     lb[rows, j, :], ALU.add, ALU.mult), "F.dve.%s%d" % (name, j), b)
                    wait(dve, "F.pe.k%d" % j, b)
                    did(dve.scalar_tensor_tensor(kk[i][:, j, :], of("F.k%d" % j, b)[:], bq1[:, 1, j:j + 1], la[:, j, :],
                                                 ALU.add, ALU.mult), "F.dve.k%d" % j, b)

            def section_G(n, ph):
                if ph == 1:
                    if n == 0:
                        wait(dve, "E.dve.h", B - 1)
                    for m in range(2):
                        wait(dve, "G.pe.qk%d" % m, n)
                        wait(dve, "G.pe.av", n - 2)
                        did(dve.tensor_tensor(sim[n % 2][:, 2 * m:2 * m + 2].rearrange("p a b c -> p (a b c)"),
                                              of("G.qk%d" % m, n)[:], causal[:], ALU.mult), "G.dve.m%d" % m, n)
                if ph == 5:
                    wait(dve, "G.pe.out", n)
                    wait(dve, "F.pool.hb", n // T)
                    did(dve.tensor_tensor(h[:, n, :], h[:, n, :], of("G.out", n)[:, 0:D], ALU.add), "G.dve.h", n)

            def section_I(b, ph):
                i = b % 2
                hb = h[:, b * T:(b + 1) * T, :]
                if ph == 0:
                    wait(dve, "G.dve.h", b * T + 3)
                    statistics("I", b, hb, stat[i], mv[i], ve[i][:, 0])
                    did(dve.tensor_scalar(ve[i][:, 0], mv[i][:, :, 1], EPS, None, ALU.add), "I.dve.ve", b)
                    did(dve.tensor_scalar(ve[i][:, 1], mv[i][:, :, 1], 1.0 + EPS, EPS * EPS, ALU.mult, ALU.add), "I.dve.vv", b)
                if ph == 2:
                    normalise("I", b, hb, mv[i], rstd[i][:, 0], xn[1])
                    wait(dve, "I.pe.tr", b - 1)
                    for t in range(T):
                        did(dve.tensor_scalar(xn[0][:, t, :], hb[:, t, :], mv[i][:, t, 0:1], rstd[i][:, 1, t:t + 1],
                                              ALU.subtract, ALU.mult), "I.dve.y%d" % t, b)
                if ph == 3:
                    wait(dve, "I.dve.y3", b)
                    did(dve.tensor_tensor(hb, hb, xn[1][:], ALU.add), "I.dve.h", b)
                if ph == 6:
                    wait(dve, "I.pe.lg", b)
                    lgt = of("I.lg", b)[:, 0:T * E].rearrange("p (t e) -> p t e", t=T)
                    did(dve.tensor_reduce(r1[:, 0], lgt, X, ALU.max), "I.dve.max", b)
                    wait(dve, "I.dve.max", b)
                    did(dve.tensor_tensor(rt[:, 0], lgt, r1[:, 0].unsqueeze(2).to_broadcast([P, T, E]), ALU.subtract),
                        "I.dve.sub", b)
                if ph == 8:
                    wait(dve, "I.act.exp", b)
                    did(dve.tensor_reduce(r1[:, 1], rt[:, 1], X, ALU.add), "I.dve.den", b)
                    wait(dve, "I.dve.den", b)
                    did(dve.reciprocal(r1[:, 2], r1[:, 1]), "I.dve.rden", b)
                    wait(dve, "I.dve.rden", b)
                    did(dve.tensor_tensor(rt[:, 2], rt[:, 1], r1[:, 2].unsqueeze(2).to_broadcast([P, T, E]), ALU.mult),
                        "I.dve.p", b)
                    wait(dve, "I.dve.p", b)
                    for t in range(T):
                        did(dve.max(rt[:, 3, t, :], rt[:, 2, t, :]), "I.dve.top%d" % t, b)
                    wait(dve, "I.dve.top3", b)
                    for t in range(T):
                        did(dve.max_index(rix[:, t, :], rt[:, 3, t, :], rt[:, 2, t, :]), "I.dve.at%d" % t, b)
                    wait(dve, "I.dve.at3", b)
                    for n in range(2):
                        did(dve.tensor_tensor(rt[:, 4 + n], rix[:, :, n:n + 1].to_broadcast([P, T, E]),
                                              iota[:].unsqueeze(1).to_broadcast([P, T, E]), ALU.is_equal), "I.dve.is%d" % n, b)
                    wait(dve, "I.dve.is1", b)
                    for n in range(2):
                        did(dve.tensor_tensor(rt[:, 6 + n], rt[:, 4 + n], rt[:, 3, :, n:n + 1].to_broadcast([P, T, E]),
                                              ALU.mult), "I.dve.c%d" % n, b)
                    wait(dve, "I.dve.c1", b)
                    did(dve.tensor_tensor(cmb[b][:], rt[:, 6], rt[:, 7], ALU.add), "I.dve.c", b)
                if ph == 12:
                    wait(dve, "I.pe.b2", b)
                    did(dve.tensor_tensor(hb, hb, of("I.b2", b)[:].rearrange("p (t c) -> p t c", t=T), ALU.add),
                        "I.dve2.h", b)

            def section_J(n, ph):
                b, e = n // E, n % E
                if ph == 3:
                    wait(dve, "J.pe.down", n)
                    wait(dve, "I.dve2.h", b)
                    wait(dve, "J.dve.y3", n - 1)
                    for t in range(T):
                        ht_ = h[:, b * T + t, :]
                        did(dve.scalar_tensor_tensor(ht_, of("J.down", n)[:, t * P:(t + 1) * P], cmb[b][:, t, e:e + 1], ht_,
                                                     ALU.mult, ALU.add), "J.dve.y%d" % t, n)

            each(order, {"T": section_T, "A": section_A, "B": section_B, "C": section_C, "O": section_O,
                         "D": section_D, "H": section_H, "E": section_E, "F": section_F, "G": section_G,
                         "I": section_I, "J": section_J})


def lay(i):
    import numpy as np

    def col(x):
        return np.asarray(x).reshape(-1, P).T

    a = {}
    a["idx"] = np.asarray(i["x"]).reshape(B * T, P).T
    names = ("glove", "fast", "levy")
    a["tables"] = np.concatenate([np.asarray(i["L0_tok_%s_tab" % n]) for n in names], axis=1)
    a["gw1"] = np.stack([np.concatenate([i["L0_tok_gW1_" + n], np.asarray(i["L0_tok_gb1_" + n])[:, None]], axis=1)
                         for n in names], axis=1)
    a["gw2"] = np.stack([np.asarray(i["L0_tok_gW2_" + n])[0] for n in names], axis=1)
    a["gb2"] = np.concatenate([i["L0_tok_gb2_" + n] for n in names])
    a["wtok"] = np.concatenate([np.asarray(i["L0_tok_W_" + n]).T for n in names]
                               + [np.asarray(i["L0_tok_b_" + n])[None] for n in names])
    a["wqkv0"] = i["L0_attn_qkv_w"]
    a["bqkv0"] = i["L0_attn_qkv_b"]
    a["wo0"] = i["L0_attn_out_w"]
    a["bo0"] = i["L0_attn_out_b"]
    a["lngb0"] = np.stack([i["L0_attn_ln_g"], i["L0_attn_ln_b"]], axis=1)
    f = {k[7:]: np.asarray(v) for k, v in i.items() if k.startswith("L0_ffn_")}
    a["g1t"] = f["gfc1_w"].T
    a["g2r"] = np.repeat(f["gfc2_w"].T, J, axis=1)
    a["gcol"] = np.stack([f["gfc1_b"], np.repeat(f["gfc2_b"], J)], axis=1)
    a["w1t"] = f["W1"].T
    a["w2t"] = f["W2"].T.reshape(FC, P, D).transpose(1, 0, 2).reshape(P, FC * D)
    a["tv1"] = f["tv_W1"].transpose(0, 2, 1).reshape(E, D // J, J, FF).transpose(0, 2, 1, 3).reshape(P, D // J, FF)
    a["tv2"] = f["tv_W2"].transpose(0, 2, 1).reshape(E, FC, P // J, J, D).transpose(0, 3, 2, 1, 4).reshape(P, P // J, FC * D)
    a["tvb1"] = f["tv_b1"]
    a["tvb2"] = f["tv_b2"]
    a["b1t"] = col(f["b1"])
    a["b2"] = f["b2"]
    sel = np.zeros((P, 2, 2 * J), np.float32)
    for p in range(P):
        for r in range(2):
            sel[p, r, J * r + p % J] = 1
    a["sel"] = sel
    a["lnr"] = np.concatenate([np.concatenate([f["tv_ln_g"], f["tv_ln_b"]], axis=1),
                               np.concatenate([f["ln_g"], f["ln_b"]])[None]])
    g = {k[8:]: np.asarray(v) for k, v in i.items() if k.startswith("L1_attn_")}
    inner = HEADS1 * HD1
    a["wq"] = np.concatenate([g["w_qkv"], g["w_a"]], axis=1)
    a["wo1"] = g["w_out"].reshape(PAIRS, P, D).transpose(1, 0, 2)
    a["bq1"] = np.stack([col(g["b_qkv"][0:inner]), col(g["b_qkv"][inner:2 * inner]), col(g["b_a"])], axis=1)
    a["bv1"] = g["b_qkv"][2 * inner:]
    a["bo1"] = g["b_out"]
    a["gam"] = g["gamma"].reshape(P, 1)
    a["causal"] = np.tile(np.triu(np.full((P, P), HD1 ** -0.5, np.float32)), (1, 4))
    m = {k[7:]: np.asarray(v) for k, v in i.items() if k.startswith("L1_ffn_")}
    a["gate"] = m["gate_w"]
    a["lngb1"] = np.stack([m["ln_g"], m["ln_b"]], axis=1)
    a["eb1"] = m["b1"].reshape(E, FC, P).transpose(2, 0, 1)
    a["eb2"] = m["b2"]
    a["iota"] = np.tile(np.arange(E, dtype=np.float32), (P, 1))
    a["ew1"] = m["w1"].transpose(1, 0, 2)
    a["ew2"] = m["w2"].reshape(E, FC, P, D).transpose(2, 0, 1, 3).reshape(P, E, FC * D)
    return {k: np.ascontiguousarray(v) for k, v in a.items()}


def kernel(**inputs):
    import numpy as np
    import concourse.bacc as bacc
    from concourse.bass_utils import run_bass_kernel_spmd

    nc = bacc.Bacc("TRN2", target_bir_lowering=False, num_devices=1)
    arrays = lay(inputs)
    a = {name: nc.dram_tensor("in_" + name, x.shape, mybir.dt.from_np(x.dtype), kind="ExternalInput").ap()
         for name, x in arrays.items()}
    out = nc.dram_tensor("out", (B * S, D), F32, kind="ExternalOutput").ap()
    lm_tower(nc, a, out)
    got = run_bass_kernel_spmd(nc, [{"in_" + name: x for name, x in arrays.items()}], core_ids=[0])
    return np.asarray(got.results[0]["out"]).reshape(B, S, D)
```

```python
from contextlib import ExitStack

import concourse.bass as bass
from concourse import mybir

ALU = mybir.AluOpType
ACT = mybir.ActivationFunctionType
F32 = mybir.dt.float32
I32 = mybir.dt.int32
X = mybir.AxisListType.X
HALF_PI = 1.5707963267948966

P = 128
B, S, D = 4, 512, 128
T = S // P
DIM, TABLES = 75, 3
GATE_H = 10
HEADS0 = 8
HD0 = D // HEADS0
E, FF = 8, 512
FC = FF // P
J = P // E
HEADS1, HD1 = 8, 64
PAIRS = HEADS1 * HD1 // P
EPS = 1e-5
LN_MERGE = 0.03
SPARSE = B - 1
TILES = (2 * S - E) // P + E
LN_INV_MAX = 18.420680743952367

STEPS = {
    "T.dve": ["prod", "sum", "bias", "max", "sub", "den", "rden", "alpha", "scaled", "h"],
    "T.act": ["exp", "eT1", "eT2"],
    "T.pe": ["tr1", "tr2", "h"],
    "A.dve": ["st%d" % t for t in range(T)] + ["mv%d" % t for t in range(T)] + ["eps"] + ["x%d" % t for t in range(T)]
    + ["qkv%d" % t for t in range(T)],
    "A.pool": ["rstd", "hb"],
    "A.pe": ["tr"] + ["qkv%d" % t for t in range(T)],
    "A.act": ["xT"],
    "B.act": ["sq", "ln", "rn", "qn", "uu", "lnu", "kabs", "tq", "tanh", "qt", "sin", "cos"],
    "B.dve": ["n2", "u", "pw", "pl", "fs", "fc"],
    "B.pool": ["k3"],
    "C.pe": ["trc", "trs", "kv", "o0", "o1"],
    "C.act": ["qc", "qs"],
    "C.dve": ["kv0", "kv1", "km0", "km1", "den0", "den1", "z", "o0", "o1"],
    "O.pe": ["tr", "out"],
    "O.act": ["oT"],
    "O.dve": ["st%d" % t for t in range(T)] + ["mv%d" % t for t in range(T)] + ["eps"] + ["x%d" % t for t in range(T)] + ["h"],
    "O.pool": ["rstd"],
    "D.dve": ["st%d" % t for t in range(T)] + ["mv%d" % t for t in range(T)] + ["eps"] + ["x%d" % t for t in range(T)],
    "D.pool": ["rstd", "hb"],
    "D.pe": ["tr"],
    "D.act": ["xT"],
    "H.pe": ["gh", "g", "w1", "w2", "b"],
    "H.act": ["gh"],
    "H.dve": ["g", "sel", "gb", "w1", "w2", "b1", "b2"],
    "H.pool": ["xb"],
    "E.pe": ["up%d" % c for c in range(FC)] + ["down"],
    "E.act": ["ht%d" % c for c in range(FC)],
    "E.dve": ["res"] + ["st%d" % t for t in range(T)] + ["mv%d" % t for t in range(T)] + ["eps"]
    + ["x%d" % t for t in range(T)] + ["g", "h"],
    "E.pool": ["rstd"],
    "F.dve": ["st%d" % t for t in range(T)] + ["mv%d" % t for t in range(T)] + ["lo", "var"]
    + ["x%d" % t for t in range(T)] + ["e"] + ["v%d" % t for t in range(T)] + ["sum%d" % p for p in range(PAIRS)]
    + ["cut"] + [x % p for p in range(PAIRS) for x in ("qa%d", "qb%d", "k%d")],
    "F.pool": ["rstd", "hb"],
    "F.pe": ["tr"] + ["a%d" % p for p in range(PAIRS)] + ["v%d" % t for t in range(T)]
    + [x % p for p in range(PAIRS) for x in ("q%d", "k%d")],
    "F.act": ["xT"] + ["e%d" % p for p in range(PAIRS)] + ["l", "cum", "inv"],
    "G.pe": ["tr", "qk0", "qk1", "av", "kv", "out"],
    "G.act": ["kt", "o", "s"],
    "G.dve": ["m0", "m1", "h"],
    "I.dve": ["st%d" % t for t in range(T)] + ["mv%d" % t for t in range(T)] + ["ve", "vv"] + ["x%d" % t for t in range(T)]
    + ["y%d" % t for t in range(T)] + ["h", "max", "sub", "den", "rden", "p"] + ["top%d" % t for t in range(T)]
    + ["at%d" % t for t in range(T)] + ["is0", "is1", "c0", "c1", "c"],
    "I.pool": ["rstd"],
    "I.pe": ["tr", "lg", "cT", "b2"],
    "I.act": ["xT", "exp", "cT"],
    "I.dve2": ["h"],
    "R.dve": ["m"] + ["c%d" % t for t in range(T)] + ["gt", "nt", "in", "ex", "pb", "pos", "pk", "pr", "pi",
                                                       "ej", "er", "em", "ei", "w"],
    "R.pe": ["cnt"],
    "Q.pe": ["tr"],
    "Q.act": ["x"],
    "K.dve": ["w1"],
    "K.dve2": ["y"],
    "K.pe": ["up"],
    "K.pe2": ["down"],
    "K.act": ["ht"],
    "Y.dve": [x % t for t in range(T) for x in ("a%d", "b%d")],
    "J.pe": ["up%d" % c for c in range(FC)] + ["down"],
    "J.act": ["ht%d" % c for c in range(FC)],
    "J.dve": ["y%d" % t for t in range(T)],
}



def lm_tower(nc, a, out):
    xs, ys = ([nc.dram_tensor(name + str(b), (TILES * P, D), F32, kind="Internal").ap() for b in range(SPARSE)]
              for name in ("dealt", "experts_out"))
    ctx = ExitStack()
    with ctx:
        def sb(name, shape, dt=F32):
            return ctx.enter_context(nc.sbuf_tensor(name, shape, dt))

        sem = {name: ctx.enter_context(nc.semaphore(name.replace(".", "_"))) for name in STEPS}

        def count(step, b):
            section, engine, what = step.split(".")
            steps = STEPS[section + "." + engine]
            return b * len(steps) + steps.index(what) + 1

        def wait(eng, step, b):
            if b >= 0:
                eng.wait_ge(sem[step.rsplit(".", 1)[0]], count(step, b))

        emitted = {}

        def did(ins, step, b):
            name = step.rsplit(".", 1)[0]
            emitted[name] = emitted.get(name, 0) + 1
            assert emitted[name] == count(step, b), (step, b, emitted[name])
            ins.then_inc(sem[name], 1)

        def carve(arena, size):
            used = [0]

            def take(shape):
                n = 1
                for k in shape[1:]:
                    n *= k
                view = arena[0:shape[0], used[0]:used[0] + n]
                used[0] += n
                assert used[0] <= size, used[0]
                if len(shape) == 3:
                    view = view.rearrange("p (a b) -> p a b", a=shape[1])
                elif len(shape) == 4:
                    view = view.rearrange("p (a b c) -> p a b c", a=shape[1], b=shape[2])
                return view
            return take

        h = sb("h", [P, B * T, D])
        ident = sb("ident", [P, P])
        idx = sb("idx", [P, B * T], I32)
        ES = TABLES * DIM + TABLES

        SIZE1 = 8448
        arena1 = sb("arena1", [P, SIZE1])
        arena3 = sb("arena3", [P, FC * S])
        take = carve(arena1, SIZE1)
        e_in = [take([P, T, TABLES * DIM]) for i in range(B)]
        e_sc = [take([P, T, ES]) for i in range(2)]
        e_pr = take([P, T, TABLES * DIM])
        eT1 = [take([P, S]) for i in range(2)]
        eT2 = [take([ES - P, S]) for i in range(2)]
        take = carve(arena1, SIZE1)
        ht = [take([P, FC, S]) for i in range(2)]
        w1m = [take([P, FF]) for i in range(2)]
        w2m = [take([P, FF]) for i in range(2)]
        res = take([P, T, D])
        rn = take([P, T, D])
        wide = take([P, D])
        junk = take([P, S])
        gb = take([P, P])

        take = carve(arena1, SIZE1)
        kt = [take([P, PAIRS, P]) for i in range(2)]
        sim = [take([P, PAIRS, 2, P]) for i in range(2)]
        oc = [take([P, PAIRS, P]) for i in range(2)]
        ss = [take([P, PAIRS, P]) for i in range(2)]
        hj = [take([P, FC, S]), arena3[:].rearrange("p (a b) -> p a b", a=FC)]
        rt = take([P, 8, T, E])
        cmb = [take([P, T, E]) for i in range(B)]
        cT = take([E, S])
        posi = [take([P, 2, T]).bitcast(I32) for i in range(2)]
        eid = [take([P, TILES]).bitcast(I32) for i in range(2)]
        wts = [take([P, T, 2]) for i in range(2)]
        posf = take([P, 2, T])
        before = take([P, T + 1, E])
        ntile = take([P, 3, E])
        first = take([P, T, E])
        ej = take([P, TILES, E])
        ejr = take([P, 2, TILES])
        xg = hj[0].rearrange("p c s -> p (c s)")[:, 0:TILES * D].rearrange("p (j d) -> p j d", j=TILES)
        hid = [hj[1].rearrange("p c s -> p (c s)")[:, i * S:(i + 1) * S] for i in range(2)]
        w1s = [hj[1].rearrange("p c s -> p (c s)")[:, (2 + i) * S:(3 + i) * S] for i in range(2)]

        gatev = sb("gatev", [P, TABLES, DIM + 1])
        gw1 = sb("gw1", [GATE_H, TABLES, DIM + 1])
        gw2 = sb("gw2", [GATE_H, TABLES])
        arena4 = sb("arena4", [P, 2 * T * D])
        take = carve(arena4, 2 * T * D)
        gw2b = take([GATE_H, TABLES, P])
        wtok1 = take([P, D])
        wtok2 = take([ES - P, D])
        wqkv0 = take([P, 3 * D])
        yg = arena4[:].rearrange("p (k t d) -> p k t d", k=2, t=T)
        gb2 = sb("gb2", [P, TABLES])
        lg = [sb("lg%d" % i, [P, 5, T, TABLES]) for i in range(2)]
        stat = [sb("stat%d" % i, [P, T, 6]) for i in range(2)]
        mv = [sb("mv%d" % i, [P, T, 2]) for i in range(2)]
        rstd = [sb("rstd%d" % i, [P, 2, T]) for i in range(2)]
        ve = [sb("ve%d" % i, [P, 2, T]) for i in range(2)]
        stat_o = sb("stat_o", [P, T, 6])
        mv_o = sb("mv_o", [P, T, 2])
        ve_o = sb("ve_o", [P, T])
        rstd_o = sb("rstd_o", [P, T])
        stat_e = sb("stat_e", [P, T, 6])
        mv_e = sb("mv_e", [P, T, 2])
        ve_e = sb("ve_e", [P, T])
        rstd_e = sb("rstd_e", [P, T])
        mhalf = sb("mhalf", [P, 2, T])
        xn = [sb("xn%d" % i, [P, T, D]) for i in range(2)]
        xT = [sb("xT%d" % i, [P, S]) for i in range(2)]
        stat_f = sb("stat_f", [P, T, 6])
        mv_f = sb("mv_f", [P, T, 2])
        ve_f = sb("ve_f", [P, T])
        rstd_f = sb("rstd_f", [P, T])
        xn_f = sb("xn_f", [P, T, D])
        xT_f = sb("xT_f", [P, S])
        take = carve(arena3, FC * S)
        w1t, w2t, tvb1, bqkv0, wo0 = (take([P, n]) for n in (FF, FF, FF, 3 * D, D))
        half_pi = sb("half_pi", [P, 1])
        tiny = sb("tiny", [P, 1])
        bo0 = sb("bo0", [P, D])
        lngb0 = sb("lngb0", [P, 2])
        blk = sb("blk", [P, D + HEADS0])

        SIZE2 = 20 * 1024 + 512
        arena2 = sb("arena2", [P, SIZE2])
        take = carve(arena2, SIZE2)
        qkv = [take([P, T, 3 * D + 1]) for i in range(2)]
        sq = [take([P, T, 2 * D]) for i in range(2)]
        n2 = [take([P, 4, T * 16]) for i in range(2)]
        u = take([P, T, 2 * D])
        pw = take([P, T * HEADS0])
        lnu = take([P, T, D])
        kab = take([P, T, D])
        tq = take([P, T, HEADS0])
        th = take([P, T, 2 * D])
        amp = take([P, T, 2 * D])
        fs = [take([P, T, 2 * D]) for i in range(2)]
        fc = [take([P, T, 2 * D]) for i in range(2)]
        sn = take([P, T, 2 * D])
        cs = take([P, T, 2 * D])
        qc = take([P, S])
        qs = take([P, S])
        kvm = take([P, 2, D + HEADS0])
        den = take([P, T * HEADS0])
        rden = take([P, T * HEADS0])
        o = take([P, T, D])
        on = take([P, T, D])
        oT = take([P, S])
        take = carve(arena2, SIZE2)
        qz = [take([P, PAIRS, 2, S]) for i in range(2)]
        kk = [take([P, PAIRS, S]) for i in range(2)]
        vv = [take([P, T, HEADS1 * HD1]) for i in range(2)]
        la = take([P, PAIRS, S])
        lb = take([P, PAIRS, S])

        big = sb("big", [P, 2 * E * FF])
        tv1 = big[:, 0:E * FF].rearrange("p (i f) -> p i f", i=E)
        tv2 = big[:, E * FF:].rearrange("p (i f) -> p i f", i=E)
        ew1 = tv1
        ew2 = tv2
        g1t = sb("g1t", [P, D])
        g2r = sb("g2r", [P, P])
        gcol = sb("gcol", [P, 2])
        tvb2 = sb("tvb2", [P, D])
        b1t = sb("b1t", [P, FC])
        b2w = sb("b2w", [P, D])
        sel = sb("sel", [P, 2, 2 * J])
        lnr = sb("lnr", [E + 1, 2 * D])
        lnco = sb("lnco", [E + 1, P])
        lnw = sb("lnw", [P, 2, D])
        gs = [sb("gs%d" % i, [P, 1]) for i in range(2)]
        grow = [sb("grow%d" % i, [P, 1]) for i in range(2)]
        selg = [sb("selg%d" % i, [P, 2, 2 * J]) for i in range(2)]
        b1m = [sb("b1m%d" % i, [P, FC]) for i in range(2)]
        xb = sb("xb", [P, T, D])
        rank = xb[:].rearrange("p t d -> p (t d)")
        iota = rank[:, 2 * P:2 * P + E]
        full = rank[:, 2 * P + E:2 * P + E + T]
        number = rank[:, 2 * P + E + T:2 * P + E + T + TILES]

        wq = sb("wq", [P, 4 * 512])
        wo1 = sb("wo1", [P, PAIRS, D])
        bq1 = sb("bq1", [P, 3, PAIRS])
        nba = sb("nba", [P, PAIRS])
        bv1 = sb("bv1", [P, HEADS1 * HD1])
        bo1 = sb("bo1", [P, D])
        gam = sb("gam", [P, 1])
        gam2 = sb("gam2", [P, 1])
        causal = sb("causal", [P, 4 * P])
        low = sb("low", [P, T])

        gate = sb("gate", [P, E])
        lngb1 = sb("lngb1", [P, 2])
        eb1 = sb("eb1", [P, E, FC])
        eb2 = sb("eb2", [E, D])
        rix = sb("rix", [P, T, E], mybir.dt.uint32)
        r1 = sb("r1", [P, 4, T])
        one = sb("one", [P, 1])

        bank = [ctx.enter_context(nc.psum_tensor("bank%d" % i, [P, S], F32)) for i in range(8)]
        READ = {"T.tr1": "T.act.eT1", "T.tr2": "T.act.eT2", "T.h": "T.dve.h", "A.tr": "A.act.xT",
                "C.trc": "C.act.qc", "C.trs": "C.act.qs", "C.kv": "C.dve.km1", "C.o0": "C.dve.o0",
                "C.o1": "C.dve.o1", "O.tr": "O.act.oT", "O.out": "O.dve.h",
                "D.tr": "D.act.xT", "H.gh": "H.act.gh", "H.g": "H.dve.g", "H.w1": "H.dve.w1", "H.w2": "H.dve.w2",
                "H.b": "H.dve.b2", "E.down": "E.dve.res", "F.tr": "F.act.xT", "G.tr": "G.act.kt",
                "G.qk0": "G.dve.m0", "G.qk1": "G.dve.m1", "G.av": "G.act.o", "G.out": "G.dve.h",
                "I.tr": "I.act.xT", "I.lg": "I.dve.sub", "I.cT": "I.act.cT", "I.b2": "I.dve2.h",
                "J.down": "J.dve.y3", "R.cnt": "R.dve.pos", "Q.tr": "Q.act.x",
                "K.up": "K.act.ht", "K.down": "K.dve2.y"}
        READ.update({"E.up%d" % c: "E.act.ht%d" % c for c in range(FC)})
        READ.update({"J.up%d" % c: "J.act.ht%d" % c for c in range(FC)})
        READ.update({"F.a%d" % p: "F.act.e%d" % p for p in range(PAIRS)})
        READ.update({"F.v%d" % t: "F.dve.v%d" % t for t in range(T)})
        READ.update({"F.q%d" % p: "F.dve.qb%d" % p for p in range(PAIRS)})
        READ.update({"F.k%d" % p: "F.dve.k%d" % p for p in range(PAIRS)})
        READ.update({"A.qkv%d" % t: "A.dve.qkv%d" % t for t in range(T)})
        GROUPS = {("T", 3): ["tr1", "tr2"], ("T", 5): ["h"], ("A", 3): ["tr"],
                  ("A", 5): ["qkv%d" % t for t in range(T)],
                  ("C", 0): ["trc", "trs", "kv"], ("C", 2): ["o0", "o1"], ("O", 3): ["tr"], ("O", 5): ["out"],
                  ("D", 3): ["tr"], ("H", 0): ["gh"], ("H", 2): ["g"], ("H", 4): ["w1", "w2", "b"],
                  ("E", 0): ["up0", "up1"], ("E", 1): ["up2", "up3"], ("E", 3): ["down"],
                  ("F", 3): ["tr"], ("F", 5): ["a%d" % p for p in range(PAIRS)], ("F", 6): ["v%d" % t for t in range(T)],
                  ("F", 12): ["q0", "k0"], ("F", 13): ["q1", "k1"], ("F", 14): ["q2", "k2"], ("F", 15): ["q3", "k3"],
                  ("G", 0): ["tr", "qk0", "qk1"], ("G", 2): ["av"], ("G", 4): ["out"],
                  ("I", 3): ["tr"], ("I", 5): ["lg"], ("I", 9): ["cT"], ("I", 11): ["b2"],
                  ("J", 0): ["up%d" % c for c in range(FC)], ("J", 2): ["down"],
                  ("R", 1): ["cnt"], ("Q", 0): ["tr"], ("K", 1): ["up"], ("K", 3): ["down"]}
        PHASES = {"T": 7, "A": 7, "B": 8, "C": 4, "O": 7, "D": 5, "H": 7, "E": 8, "F": 17, "G": 6, "I": 13, "J": 4, "R": 4, "Q": 2, "K": 5, "Y": 2}
        starts = []
        for b in range(B):
            for s, at in (("T", 0), ("A", 7.5), ("B", 14), ("C", 22.5), ("O", 25.5)):
                starts.append((at + 8 * b, 1, s, b))
        for b in range(B):
            for s, at in (("D", 33.5), ("H", 39), ("E", 46)):
                starts.append((at + 7.5 * b, 1, s, b))
        for b in range(B):
            at = 56.5 + 20.5 * b
            starts.append((at, 1, "F", b))
            for c in range(T):
                starts.append((at + 17 + 4.75 * c, 1, "G", b * T + c))
            at += 36.75
            starts.append((at, 1, "I", b))
            if b < SPARSE:
                starts.append((at + 8, 1, "R", b))
                for q in range(-(-TILES // T)):
                    starts.append((at + (17, 17, 15)[b] + 1.5 * q, 1, "Q", b * T + q))
                for j in range(TILES):
                    starts.append((at + (17, 17, 15)[b] + 1.25 + 0.9 * j, 1, "K", b * TILES + j))
                starts.append((at + (17, 17, 15)[b] + 0.9 * TILES + 5, 3, "Y", b))
            else:
                for e in range(E):
                    starts.append((at + 14.5 + 2.4 * e, 1, "J", e))
        order = sorted((at + k * ph, n, s, b, ph) for n, (at, k, s, b) in enumerate(starts) for ph in range(PHASES[s]))
        order = [x[2:] for x in order]
        RING = 7
        place = {}
        ring = [g for s, b, ph in order for g in [(s + "." + x, b) for x in GROUPS.get((s, ph), [])]]
        for i, (g, b) in enumerate(ring):
            place[g, b] = (bank[i % RING], ring[i - RING] if i >= RING else None)

        def room(pe, g, b):
            at, last = place[g, b]
            if last:
                wait(pe, READ[last[0]], last[1])
            else:
                pe.wait_ge(s_banks, 1)
            return at

        def of(g, b):
            return place[g, b][0]

        s_const = ctx.enter_context(nc.semaphore("s_const"))
        s_ident = ctx.enter_context(nc.semaphore("s_ident"))
        s_banks = ctx.enter_context(nc.semaphore("s_banks"))
        s_gather = [ctx.enter_context(nc.semaphore("s_gather%d" % b)) for b in range(B)]
        s_idx = ctx.enter_context(nc.semaphore("s_idx"))
        s_wtok = ctx.enter_context(nc.semaphore("s_wtok"))
        s_w0 = ctx.enter_context(nc.semaphore("s_w0"))
        s_w1 = ctx.enter_context(nc.semaphore("s_w1"))
        s_w2 = ctx.enter_context(nc.semaphore("s_w2"))
        s_w3 = ctx.enter_context(nc.semaphore("s_w3"))
        s_lnw = ctx.enter_context(nc.semaphore("s_lnw"))
        s_lnb = ctx.enter_context(nc.semaphore("s_lnb"))
        s_qz = ctx.enter_context(nc.semaphore("s_qz"))
        s_gam = ctx.enter_context(nc.semaphore("s_gam"))
        s_gw2b = ctx.enter_context(nc.semaphore("s_gw2b"))
        s_gv = ctx.enter_context(nc.semaphore("s_gv"))
        s_gatev = ctx.enter_context(nc.semaphore("s_gatev"))
        s_before = ctx.enter_context(nc.semaphore("s_before"))
        s_zero = ctx.enter_context(nc.semaphore("s_zero"))
        s_deal = [ctx.enter_context(nc.semaphore("s_deal%d" % b)) for b in range(SPARSE)]
        s_xg = [ctx.enter_context(nc.semaphore("s_xg%d" % b)) for b in range(SPARSE)]
        s_ys = [ctx.enter_context(nc.semaphore("s_ys%d" % b)) for b in range(SPARSE)]
        s_yg = [ctx.enter_context(nc.semaphore("s_yg%d" % b)) for b in range(SPARSE)]
        s_out = ctx.enter_context(nc.semaphore("s_out"))
        block = ctx.enter_context(nc.Block())

        def row(name, n):
            return a[name].rearrange("(o n) -> o n", o=1).to_broadcast([P, n])

        @block.sync
        def _(sp):
            sp.dma_start(idx[:], a["idx"]).then_inc(s_idx, 16)
            for dst, src in ((gw1, a["gw1"]), (gw2, a["gw2"]), (gb2, row("gb2", TABLES)),
                             (wtok1, a["wtok"][0:P, :]), (wtok2, a["wtok"][P:ES, :]), (lnr, a["lnr"])):
                sp.dma_start(dst[:], src).then_inc(s_wtok, 16)
            for dst, src in ((wqkv0, a["wqkv0"]), (bqkv0, row("bqkv0", 3 * D)), (wo0, a["wo0"]),
                             (bo0, row("bo0", D)), (lngb0, a["lngb0"])):
                sp.dma_start(dst[:], src).then_inc(s_w0, 16)
            for dst, src in ((g1t, a["g1t"]), (g2r, a["g2r"]), (gcol, a["gcol"]), (w1t, a["w1t"]), (w2t, a["w2t"]),
                             (tvb2[0:P:J, :], a["tvb2"]), (tvb1[0:P:J, :], a["tvb1"]), (b1t, a["b1t"]),
                             (b2w, row("b2", D)), (sel, a["sel"]), (tv1, a["tv1"]), (tv2, a["tv2"])):
                if src is a["tvb2"]:
                    sp.wait_ge(s_const, 2)
                sp.dma_start(dst[:], src).then_inc(s_w1, 16)
            for dst, src in ((wq, a["wq"]), (wo1, a["wo1"]), (bq1, a["bq1"]), (bv1, row("bv1", HEADS1 * HD1)),
                             (bo1, row("bo1", D)), (gam, a["gam"]), (causal, a["causal"])):
                sp.dma_start(dst[:], src).then_inc(s_w2, 16)
            for dst, src in ((gate, a["gate"]), (lngb1, a["lngb1"]), (eb1, a["eb1"]), (eb2, a["eb2"])):
                sp.dma_start(dst[:], src).then_inc(s_w3, 16)
            wait(sp, "H.pe.w2", B - 1)
            sp.dma_start(ew1, a["ew1"]).then_inc(s_w3, 16)
            sp.dma_start(ew2, a["ew2"]).then_inc(s_w3, 16)
            wait(sp, "E.dve.res", B - 1)
            sp.dma_start(rank[:, 0:a["rank"].shape[1]], a["rank"]).then_inc(s_w3, 16)
            sp.wait_ge(s_qz, 2)
            zeros = qz[1].rearrange("p a b c -> p (a b c)")[:, 0:TILES * D]
            for b in range(SPARSE):
                sp.dma_start(xs[b].rearrange("(p j) d -> p (j d)", p=P), zeros).then_inc(s_zero, 16)

            def result(b):
                sp.dma_start(out[b * S:(b + 1) * S, :].rearrange("(t p) d -> p t d", p=P),
                             h[:, b * T:(b + 1) * T, :]).then_inc(s_out, 16)

            for b in range(SPARSE):
                sp.wait_ge(s_deal[b], 16 * 2 * T)
                if b:
                    sp.wait_ge(s_ys[b - 1], 16)
                sp.dma_start(xg, xs[b].rearrange("(j p) d -> p j d", p=P)).then_inc(s_xg[b], 16)
                if b:
                    wait(sp, "Y.dve.b3", b - 1)
                    result(b - 1)
                wait(sp, "K.dve2.y", b * TILES + TILES - 1)
                sp.dma_start(ys[b].rearrange("(j p) d -> p j d", p=P), xg).then_inc(s_ys[b], 16)
            wait(sp, "Y.dve.b3", SPARSE - 1)
            result(SPARSE - 1)
            wait(sp, "J.dve.y3", E - 1)
            result(B - 1)
            sp.wait_ge(s_out, 16 * B)

        def each(order, programs):
            for section, b, ph in order:
                if section in programs:
                    programs[section](b, ph)

        @block.gpsimd
        def _(pool):
            pool.memset(ident[:], 0.0).then_inc(s_ident, 1)
            pool.memset(tvb1[:], 0.0).then_inc(s_const, 1)
            pool.memset(tvb2[:], 0.0).then_inc(s_const, 1)
            pool.memset(lnco[:], 1.0 - E * LN_MERGE).then_inc(s_const, 1)
            pool.wait_ge(s_const, 3)
            pool.memset(lnco[0:E, :], LN_MERGE).then_inc(s_const, 1)
            pool.memset(blk[:], 1.0 / S).then_inc(s_const, 1)
            pool.memset(mhalf[:], -0.5).then_inc(s_const, 1)
            pool.memset(half_pi[:], HALF_PI).then_inc(s_const, 1)
            pool.memset(tiny[:], 1e-19).then_inc(s_const, 1)
            pool.memset(one[:], 1.0).then_inc(s_const, 1)
            for i in range(2):
                pool.memset(qkv[i][:, :, 3 * D:3 * D + 1], 1.0).then_inc(s_const, 1)
            pool.wait_ge(s_ident, 1)
            pool.affine_select(out=ident[:], in_=ident[:], compare_op=ALU.not_equal, fill=1.0, base=0,
                               pattern=[[-1, P]], channel_multiplier=1).then_inc(s_ident, 1)
            pool.wait_ge(s_const, 11)
            for cols, step in ((blk[:, 0:D].rearrange("p (g c) -> p g c", c=HD0), 1), (blk[:, D:].unsqueeze(2), 1)):
                w = cols.shape[2]
                pool.affine_select(out=cols, in_=cols, compare_op=ALU.is_ge, fill=0.0, base=0,
                                   pattern=[[-HD0, HEADS0], [0, w]], channel_multiplier=1).then_inc(s_const, 1)
            pool.wait_ge(s_const, 13)
            for cols in (blk[:, 0:D].rearrange("p (g c) -> p g c", c=HD0), blk[:, D:].unsqueeze(2)):
                w = cols.shape[2]
                pool.affine_select(out=cols, in_=cols, compare_op=ALU.is_ge, fill=0.0, base=HD0 - 1,
                                   pattern=[[HD0, HEADS0], [0, w]], channel_multiplier=-1).then_inc(s_const, 1)
            pool.wait_ge(s_idx, 16)
            for b in range(B):
                for t in range(T):
                    pool.indirect_dma_start(
                        e_in[b][:, t, :], None, a["tables"],
                        bass.IndirectOffsetOnAxis(ap=idx[:, b * T + t:b * T + t + 1], axis=0)).then_inc(s_gather[b], 16)

            def section_A(b, ph):
                i = b % 2
                if ph == 1:
                    wait(pool, "A.dve.eps", b)
                    did(pool.tensor_tensor(rstd[i][:, 0], ve[i][:, 0], mhalf[:, 0], ALU.pow), "A.pool.rstd", b)
                if ph == 3:
                    if b == 0:
                        pool.wait_ge(s_w0, 16 * 5)
                    wait(pool, "A.dve.x3", b)
                    hb = h[:, b * T:(b + 1) * T, :]
                    did(pool.tensor_tensor(hb, hb, bo0[:].unsqueeze(1).to_broadcast([P, T, D]), ALU.add), "A.pool.hb", b)

            def section_B(b, ph):
                i = b % 2
                if ph == 5:
                    wait(pool, "B.act.kabs", b)
                    wait(pool, "B.act.sq", b)
                    wait(pool, "B.dve.fc", b - 1)
                    did(pool.tensor_tensor(amp[:, :, D:], kab[:], sq[i][:, :, D:], ALU.mult), "B.pool.k3", b)

            def section_O(b, ph):
                if ph == 1:
                    wait(pool, "O.dve.eps", b)
                    did(pool.tensor_tensor(rstd_o[:], ve_o[:], mhalf[:, 0], ALU.pow), "O.pool.rstd", b)

            def section_D(b, ph):
                i = b % 2
                hb = h[:, b * T:(b + 1) * T, :]
                if ph == 1:
                    wait(pool, "D.dve.eps", b)
                    did(pool.tensor_tensor(rstd[i][:, 0], ve[i][:, 0], mhalf[:, 0], ALU.pow), "D.pool.rstd", b)
                if ph == 3:
                    pool.wait_ge(s_lnb, 1)
                    wait(pool, "D.dve.x3", b)
                    did(pool.tensor_tensor(hb, hb, lnw[:, 1, :].unsqueeze(1).to_broadcast([P, T, D]), ALU.add),
                        "D.pool.hb", b)

            def section_H(b, ph):
                i = b % 2
                hb = h[:, b * T:(b + 1) * T, :]
                if ph == 6:
                    wait(pool, "H.dve.b2", b)
                    wait(pool, "E.dve.res", b - 1)
                    did(pool.tensor_tensor(xb[:], xn[i][:], wide[:].unsqueeze(1).to_broadcast([P, T, D]), ALU.add),
                        "H.pool.xb", b)

            def section_E(b, ph):
                if ph == 5:
                    wait(pool, "E.dve.eps", b)
                    did(pool.tensor_tensor(rstd_e[:], ve_e[:], mhalf[:, 0], ALU.pow), "E.pool.rstd", b)

            def section_F(b, ph):
                i = b % 2
                hb = h[:, b * T:(b + 1) * T, :]
                if ph == 0:
                    if b == 0:
                        wait(pool, "O.dve.h", B - 1)
                        for j in range(2):
                            pool.memset(qz[j], 0.0).then_inc(s_qz, 1)
                if ph == 1:
                    wait(pool, "F.dve.var", b)
                    did(pool.tensor_tensor(rstd_f[:], ve_f[:], mhalf[:, 0], ALU.pow), "F.pool.rstd", b)
                if ph == 3:
                    if b == 0:
                        pool.wait_ge(s_w2, 16 * 7)
                    wait(pool, "F.dve.x3", b)
                    did(pool.tensor_tensor(hb, hb, bo1[:].unsqueeze(1).to_broadcast([P, T, D]), ALU.add), "F.pool.hb", b)

            def section_I(b, ph):
                i = b % 2
                if ph == 1:
                    wait(pool, "I.dve.vv", b)
                    did(pool.tensor_tensor(rstd[i][:], ve[i][:], mhalf[:], ALU.pow), "I.pool.rstd", b)

            def section_R(b, ph):
                if ph == 3:
                    if b == 0:
                        pool.wait_ge(s_zero, 16 * SPARSE)
                    wait(pool, "R.dve.pi", b)
                    for t in range(T):
                        for k in range(2):
                            pool.indirect_dma_start(
                                xs[b], bass.IndirectOffsetOnAxis(ap=posi[b % 2][:, k, t:t + 1], axis=0),
                                xn[0][:, t, :], None).then_inc(s_deal[b], 16)

            def section_Y(b, ph):
                if ph == 0:
                    pool.wait_ge(s_ys[b], 16)
                    wait(pool, "Y.dve.b3", b - 1)
                    for t in range(T):
                        for k in range(2):
                            pool.indirect_dma_start(
                                yg[:, k, t, :], None, ys[b],
                                bass.IndirectOffsetOnAxis(ap=posi[b % 2][:, k, t:t + 1], axis=0)).then_inc(s_yg[b], 16)

            each(order, {"A": section_A, "B": section_B, "O": section_O, "D": section_D, "H": section_H,
                         "E": section_E, "F": section_F, "I": section_I, "R": section_R, "Y": section_Y})

        @block.tensor
        def _(pe):
            pe.wait_ge(s_gw2b, 1)
            for t in range(TABLES):
                last = pe.matmul(bank[7][:, t * (DIM + 1):(t + 1) * (DIM + 1)], gw2b[:, t, :], gw1[:, t, :],
                                 start=True, stop=True)
            last.then_inc(s_gv, 1)
            pe.wait_ge(s_ident, 2)
            pe.wait_ge(s_wtok, 16 * 6)
            pe.wait_ge(s_const, 4)
            pe.matmul(bank[6][:, 0:2 * D], lnco[:], lnr[:], start=True, stop=True).then_inc(s_lnw, 1)

            def section_T(b, ph):
                i = b % 2
                if ph == 3:
                    p1 = room(pe, "T.tr1", b)
                    wait(pe, "T.dve.scaled", b)
                    for t in range(T):
                        last = pe.transpose(p1[:, t * P:(t + 1) * P], e_sc[i][:, t, 0:P], ident[:])
                    did(last, "T.pe.tr1", b)
                    p2 = room(pe, "T.tr2", b)
                    for t in range(T):
                        last = pe.transpose(p2[0:ES - P, t * P:(t + 1) * P], e_sc[i][:, t, P:ES], ident[:])
                    did(last, "T.pe.tr2", b)
                if ph == 5:
                    p3 = room(pe, "T.h", b)
                    if b == 0:
                        pe.wait_ge(s_wtok, 16 * 6)
                    wait(pe, "T.act.eT1", b)
                    wait(pe, "T.act.eT2", b)
                    for t in range(T):
                        tk = slice(t * P, (t + 1) * P)
                        pe.matmul(p3[:, tk], eT1[i][:, tk], wtok1[:], start=True, stop=False)
                        last = pe.matmul(p3[:, tk], eT2[i][:, tk], wtok2[:], start=False, stop=True)
                    did(last, "T.pe.h", b)

            def section_A(b, ph):
                i = b % 2
                if ph == 3:
                    p = room(pe, "A.tr", b)
                    wait(pe, "A.dve.x3", b)
                    for t in range(T):
                        last = pe.transpose(p[:, t * P:(t + 1) * P], xn[i][:, t, :], ident[:])
                    did(last, "A.pe.tr", b)
                if ph == 5:
                    if b == 0:
                        pe.wait_ge(s_w0, 16 * 5)
                    for t in range(T):
                        p = room(pe, "A.qkv%d" % t, b)
                        wait(pe, "A.act.xT", b)
                        did(pe.matmul(p[:, 0:3 * D], xT[i][:, t * P:(t + 1) * P], wqkv0[:], start=True, stop=True),
                            "A.pe.qkv%d" % t, b)

            def section_C(b, ph):
                i = b % 2
                if ph == 0:
                    p = room(pe, "C.trc", b)
                    wait(pe, "B.dve.fc", b)
                    for t in range(T):
                        last = pe.transpose(p[:, t * P:(t + 1) * P], fc[i][:, t, 0:D], ident[:])
                    did(last, "C.pe.trc", b)
                    p = room(pe, "C.trs", b)
                    for t in range(T):
                        last = pe.transpose(p[:, t * P:(t + 1) * P], fs[i][:, t, 0:D], ident[:])
                    did(last, "C.pe.trs", b)
                    p = room(pe, "C.kv", b)
                    for half, f in enumerate((fc, fs)):
                        for t in range(T):
                            last = pe.matmul(p[:, half * (D + 1):(half + 1) * (D + 1)], f[i][:, t, D:2 * D],
                                             qkv[i][:, t, 2 * D:3 * D + 1], start=(t == 0), stop=(t == T - 1))
                    did(last, "C.pe.kv", b)
                if ph == 2:
                    for n in range(2):
                        p = room(pe, "C.o%d" % n, b)
                        wait(pe, "C.act.qs", b)
                        wait(pe, "C.dve.km1", b)
                        for j in range(2):
                            t = 2 * n + j
                            at = p[:, j * (D + HEADS0):(j + 1) * (D + HEADS0)]
                            pe.matmul(at, qc[:, t * P:(t + 1) * P], kvm[:, 0, :], start=True, stop=False)
                            last = pe.matmul(at, qs[:, t * P:(t + 1) * P], kvm[:, 1, :], start=False, stop=True)
                        did(last, "C.pe.o%d" % n, b)

            def section_O(b, ph):
                i = b % 2
                if ph == 3:
                    p = room(pe, "O.tr", b)
                    wait(pe, "O.dve.x3", b)
                    for t in range(T):
                        last = pe.transpose(p[:, t * P:(t + 1) * P], on[:, t, :], ident[:])
                    did(last, "O.pe.tr", b)
                if ph == 5:
                    p = room(pe, "O.out", b)
                    wait(pe, "O.act.oT", b)
                    for t in range(T):
                        last = pe.matmul(p[:, t * P:(t + 1) * P], oT[:, t * P:(t + 1) * P], wo0[:], start=True, stop=True)
                    did(last, "O.pe.out", b)

            def section_D(b, ph):
                i = b % 2
                if ph == 3:
                    p = room(pe, "D.tr", b)
                    wait(pe, "D.dve.x3", b)
                    for t in range(T):
                        last = pe.transpose(p[:, t * P:(t + 1) * P], xn[i][:, t, :], ident[:])
                    did(last, "D.pe.tr", b)

            def section_H(b, ph):
                i = b % 2
                if ph == 0:
                    p = room(pe, "H.gh", b)
                    if b == 0:
                        pe.wait_ge(s_w1, 16 * 12)
                    wait(pe, "D.act.xT", b)
                    did(pe.matmul(p[:], g1t[:], xT[i][:], start=True, stop=True), "H.pe.gh", b)
                if ph == 2:
                    p = room(pe, "H.g", b)
                    wait(pe, "H.act.gh", b)
                    did(pe.matmul(p[:, 0:1], g2r[:], gs[i][:], start=True, stop=True), "H.pe.g", b)
                if ph == 4:
                    for name, w in (("w1", tv1), ("w2", tv2)):
                        p = room(pe, "H." + name, b)
                        wait(pe, "H.dve.sel", b)
                        for r in range(2):
                            for c in range(4):
                                last = pe.matmul(p[2 * J * c:2 * J * (c + 1), :], selg[i][:, r, :], w[:, 2 * c + r, :],
                                                 start=(r == 0), stop=(r == 1), skip_group_check=True)
                        did(last, "H.pe." + name, b)
                    p = room(pe, "H.b", b)
                    wait(pe, "H.dve.gb", b)
                    for c in range(FC):
                        pe.matmul(p[:, c:c + 1], tvb1[:, c * P:(c + 1) * P], grow[i][:], start=True, stop=True)
                    did(pe.matmul(p[:, P:2 * P], gb[:], tvb2[:], start=True, stop=True), "H.pe.b", b)

            def feed(name, n, x, w1, w2, hid, ph, last_x):
                if ph < 2:
                    for c in (range(FC) if name == "J" else range(2 * ph, 2 * ph + 2)):
                        p = room(pe, "%s.up%d" % (name, c), n)
                        if last_x:
                            wait(pe, *last_x)
                        did(pe.matmul(p[:], w1[:, c * P:(c + 1) * P], x, start=True, stop=True),
                            "%s.pe.up%d" % (name, c), n)
                else:
                    p = room(pe, name + ".down", n)
                    wait(pe, "%s.act.ht3" % name, n)
                    for t in range(T):
                        for c in range(FC):
                            last = pe.matmul(p[:, t * P:(t + 1) * P], hid[:, c, t * P:(t + 1) * P],
                                             w2[:, c * D:(c + 1) * D], start=(c == 0), stop=(c == FC - 1))
                    did(last, name + ".pe.down", n)

            def section_E(b, ph):
                i = b % 2
                if ph in (0, 1, 3):
                    feed("E", b, xT[i][:], w1m[i], w2m[i], ht[i], ph, ("H.dve.b1", b))

            def section_F(b, ph):
                i = b % 2
                if ph == 3:
                    p = room(pe, "F.tr", b)
                    wait(pe, "F.dve.x3", b)
                    for t in range(T):
                        last = pe.transpose(p[:, t * P:(t + 1) * P], xn_f[:, t, :], ident[:])
                    did(last, "F.pe.tr", b)
                if ph == 5:
                    if b == 0:
                        pe.wait_ge(s_w2, 16 * 7)
                    for j in range(PAIRS):
                        p = room(pe, "F.a%d" % j, b)
                        wait(pe, "F.act.xT", b)
                        did(pe.matmul(p[:], wq[:, 3 * 512 + j * P:3 * 512 + (j + 1) * P], xT_f[:], start=True, stop=True),
                            "F.pe.a%d" % j, b)
                if ph == 6:
                    for t in range(T):
                        p = room(pe, "F.v%d" % t, b)
                        did(pe.matmul(p[:], xT_f[:, t * P:(t + 1) * P], wq[:, 2 * 512:3 * 512], start=True, stop=True),
                            "F.pe.v%d" % t, b)
                if 12 <= ph < 16:
                    j = ph - 12
                    for at, name in enumerate("qk"):
                        p = room(pe, "F.%s%d" % (name, j), b)
                        did(pe.matmul(p[:], wq[:, at * 512 + j * P:at * 512 + (j + 1) * P], xT_f[:], start=True, stop=True),
                            "F.pe.%s%d" % (name, j), b)

            def section_G(n, ph):
                b, c = n // T, n % T
                i, k = b % 2, n % 2
                tk = slice(c * P, (c + 1) * P)
                if ph == 0:
                    p = room(pe, "G.tr", n)
                    wait(pe, "F.dve.k3", b)
                    for j in range(PAIRS):
                        last = pe.transpose(p[:, j * P:(j + 1) * P], kk[i][:, j, tk], ident[:])
                    did(last, "G.pe.tr", n)
                    for m in range(2):
                        p = room(pe, "G.qk%d" % m, n)
                        for j in (2 * m, 2 * m + 1):
                            at = p[:, (j % 2) * 2 * P:(j % 2 + 1) * 2 * P].rearrange("p (g s) -> p g s", g=2)
                            last = pe.matmul(at, kk[i][:, j, tk], qz[i][:, j, :, tk], start=True, stop=True)
                        did(last, "G.pe.qk%d" % m, n)
                if ph == 2:
                    p = room(pe, "G.av", n)
                    wait(pe, "G.dve.m1", n)
                    if c:
                        wait(pe, "G.act.s", n - 1)
                    for j in range(PAIRS):
                        for m in range(2):
                            last = pe.matmul(p[m * HD1:(m + 1) * HD1, j * P:(j + 1) * P],
                                             vv[i][:, c, (2 * j + m) * HD1:(2 * j + m + 1) * HD1], sim[k][:, j, m, :],
                                             start=True, stop=(c == 0), skip_group_check=True)
                        if c:
                            for m in range(2):
                                last = pe.matmul(p[m * HD1:(m + 1) * HD1, j * P:(j + 1) * P],
                                                 ss[(n - 1) % 2][:, j, m * HD1:(m + 1) * HD1], qz[i][:, j, m, tk],
                                                 start=False, stop=True, skip_group_check=True)
                    did(last, "G.pe.av", n)
                    wait(pe, "G.act.kt", n)
                    wait(pe, "G.act.s", n - 1)
                    for j in range(PAIRS):
                        last = pe.matmul(bank[7][:, j * P:(j + 1) * P], kt[k][:, j, :], vv[i][:, c, j * P:(j + 1) * P],
                                         start=(c == 0 and j == 0), stop=True, skip_group_check=True)
                    did(last, "G.pe.kv", n)
                if ph == 4:
                    p = room(pe, "G.out", n)
                    wait(pe, "G.act.o", n)
                    for j in range(PAIRS):
                        last = pe.matmul(p[:, 0:D], oc[k][:, j, :], wo1[:, j, :], start=(j == 0), stop=(j == PAIRS - 1))
                    did(last, "G.pe.out", n)

            def section_I(b, ph):
                if ph == 3:
                    p = room(pe, "I.tr", b)
                    wait(pe, "I.dve.y3", b)
                    for t in range(T):
                        last = pe.transpose(p[:, t * P:(t + 1) * P], xn[0][:, t, :], ident[:])
                    did(last, "I.pe.tr", b)
                if ph == 5:
                    p = room(pe, "I.lg", b)
                    wait(pe, "I.act.xT", b)
                    for t in range(T):
                        last = pe.matmul(p[:, t * E:(t + 1) * E], xT[b % 2][:, t * P:(t + 1) * P], gate[:], start=True, stop=True)
                    did(last, "I.pe.lg", b)
                if ph == 9:
                    p = room(pe, "I.cT", b)
                    wait(pe, "I.dve.c", b)
                    for t in range(T):
                        last = pe.transpose(p[0:E, t * P:(t + 1) * P], cmb[b][:, t, :], ident[:])
                    did(last, "I.pe.cT", b)
                if ph == 11:
                    p = room(pe, "I.b2", b)
                    wait(pe, "I.act.cT", b)
                    for t in range(T):
                        last = pe.matmul(p[:, t * P:(t + 1) * P], cT[:, t * P:(t + 1) * P], eb2[:], start=True, stop=True)
                    did(last, "I.pe.b2", b)

            def section_J(n, ph):
                e = n % E
                if ph in (0, 2):
                    feed("J", n, xT[(B - 1) % 2][:], ew1[:, e, :], ew2[:, e, :], hj[(n + 1) % 2], ph, None)

            def section_R(b, ph):
                if ph == 1:
                    p = room(pe, "R.cnt", b)
                    wait(pe, "R.dve.m", b)
                    pe.matmul(p[:, 0:T * E], rank[:, 0:P], rt[:, 0].rearrange("p t e -> p (t e)"), start=True, stop=True)
                    did(pe.matmul(p[:, T * E:2 * T * E], rank[:, P:2 * P], rt[:, 0].rearrange("p t e -> p (t e)"),
                                  start=True, stop=True), "R.pe.cnt", b)

            def section_Q(n, ph):
                b, q = n // T, n % T
                if ph == 0:
                    p = room(pe, "Q.tr", n)
                    pe.wait_ge(s_xg[b], 16)
                    for j in range(T * q, min(T * q + T, TILES)):
                        last = pe.transpose(p[:, (j % T) * P:(j % T + 1) * P], xg[:, j, :], ident[:])
                    did(last, "Q.pe.tr", n)

            def section_K(n, ph):
                b, j = n // TILES, n % TILES
                if ph == 1:
                    p = room(pe, "K.up", n)
                    wait(pe, "Q.act.x", b * T + j // T)
                    wait(pe, "K.dve.w1", n)
                    for c in range(FC):
                        last = pe.matmul(p[:, c * P:(c + 1) * P], w1s[n % 2][:, c * P:(c + 1) * P], xg[:, j, :],
                                         start=True, stop=True)
                    did(last, "K.pe.up", n)
                if ph == 3:
                    p = room(pe, "K.down", n)
                    wait(pe, "K.act.ht", n)
                    e = pe.value_load(eid[b % 2][0:1, j:j + 1], min_val=0, max_val=E - 1)
                    for c in range(FC):
                        last = pe.matmul(p[:, 0:D], hid[n % 2][:, c * P:(c + 1) * P],
                                         big[:, bass.ds(e * FF + (E * FF + c * D), D)], start=(c == 0), stop=(c == FC - 1))
                    did(last, "K.pe2.down", n)

            each(order, {"T": section_T, "A": section_A, "C": section_C, "O": section_O, "D": section_D,
                         "H": section_H, "E": section_E, "F": section_F, "G": section_G, "I": section_I,
                         "J": section_J, "R": section_R, "Q": section_Q, "K": section_K})

        @block.scalar
        def _(act):
            act.wait_ge(s_const, 15)

            def section_T(b, ph):
                i = b % 2
                if ph == 1:
                    wait(act, "T.dve.sub", b)
                    did(act.activation(lg[i][:, 3], lg[i][:, 2], ACT.Exp), "T.act.exp", b)
                if ph == 4:
                    wait(act, "T.pe.tr1", b)
                    wait(act, "T.pe.h", b - 2)
                    did(act.activation(eT1[i][:], of("T.tr1", b)[:], ACT.Copy), "T.act.eT1", b)
                    wait(act, "T.pe.tr2", b)
                    did(act.activation(eT2[i][:], of("T.tr2", b)[0:ES - P, :], ACT.Copy), "T.act.eT2", b)

            def section_A(b, ph):
                if ph == 4:
                    wait(act, "A.pe.tr", b)
                    wait(act, "A.pe.qkv3", b - 2)
                    did(act.activation(xT[b % 2][:], of("A.tr", b)[:], ACT.Copy), "A.act.xT", b)

            def section_B(b, ph):
                i = b % 2
                qk = qkv[i][:, :, 0:2 * D]
                if ph == 0:
                    wait(act, "A.dve.qkv3", b)
                    wait(act, "B.pool.k3", b - 2)
                    did(act.activation(sq[i][:], qk, ACT.Square), "B.act.sq", b)
                if ph == 2:
                    wait(act, "B.dve.n2", b)
                    did(act.activation(n2[i][:, 1], n2[i][:, 0], ACT.Ln), "B.act.ln", b)
                    wait(act, "B.act.ln", b)
                    did(act.activation(n2[i][:, 2], n2[i][:, 1], ACT.Exp, scale=-0.5), "B.act.rn", b)
                    did(act.activation(n2[i][:, 3], n2[i][:, 1], ACT.Exp, scale=0.5), "B.act.qn", b)
                if ph == 4:
                    wait(act, "B.dve.u", b)
                    did(act.activation(lnu[:], u[:, :, 0:D], ACT.Square), "B.act.uu", b)
                    wait(act, "B.act.uu", b)
                    did(act.activation(lnu[:], lnu[:], ACT.Ln, bias=tiny[:]), "B.act.lnu", b)
                    wait(act, "B.pool.k3", b - 1)
                    did(act.activation(kab[:], qk[:, :, D:], ACT.Abs), "B.act.kabs", b)
                    did(act.activation(tq[:], n2[i][:, 3].rearrange("p (t g) -> p t g", g=16)[:, :, 0:HEADS0], ACT.Tanh),
                        "B.act.tq", b)
                    wait(act, "B.act.cos", b - 1)
                    did(act.activation(th[:], u[:], ACT.Tanh, scale=20.0), "B.act.tanh", b)
                if ph == 6:
                    wait(act, "B.dve.pl", b)
                    wait(act, "B.dve.fc", b - 1)
                    did(act.activation(amp[:, :, 0:D], lnu[:], ACT.Exp, scale=1.5), "B.act.qt", b)
                    wait(act, "B.act.tanh", b)
                    did(act.activation(sn[:], th[:], ACT.Sin, scale=HALF_PI / 2), "B.act.sin", b)
                    did(act.activation(cs[:], th[:], ACT.Sin, scale=HALF_PI / 2, bias=half_pi[:]), "B.act.cos", b)

            def section_C(b, ph):
                if ph == 1:
                    wait(act, "C.pe.trc", b)
                    wait(act, "C.pe.o1", b - 1)
                    did(act.activation(qc[:], of("C.trc", b)[:], ACT.Copy), "C.act.qc", b)
                    wait(act, "C.pe.trs", b)
                    did(act.activation(qs[:], of("C.trs", b)[:], ACT.Copy), "C.act.qs", b)

            def section_O(b, ph):
                if ph == 4:
                    wait(act, "O.pe.tr", b)
                    wait(act, "O.pe.out", b - 1)
                    did(act.activation(oT[:], of("O.tr", b)[:], ACT.Identity, bias=lngb0[:, 1:2], scale=lngb0[:, 0:1]),
                        "O.act.oT", b)

            act.wait_ge(s_w0, 16 * 5)
            def section_D(b, ph):
                i = b % 2
                if ph == 4:
                    wait(act, "D.pe.tr", b)
                    wait(act, "E.pe.up3", b - 2)
                    wait(act, "A.pe.qkv3", B - 1 - (b + 1) % 2)
                    did(act.activation(xT[i][:], of("D.tr", b)[:], ACT.Copy), "D.act.xT", b)

            def section_H(b, ph):
                i = b % 2
                if ph == 1:
                    wait(act, "H.pe.gh", b)
                    wait(act, "H.act.gh", b - 1)
                    did(act.activation(junk, of("H.gh", b)[:], ACT.Relu, bias=gcol[:, 0:1], accum_out=gs[i][:]), "H.act.gh", b)

            def section_E(b, ph):
                i = b % 2
                if ph in (1, 2):
                    for c in (2 * ph - 2, 2 * ph - 1):
                        wait(act, "E.pe.up%d" % c, b)
                        wait(act, "E.pe.down", b - 2)
                        did(act.activation(ht[i][:, c, :], of("E.up%d" % c, b)[:], ACT.Relu, bias=b1m[i][:, c:c + 1]),
                            "E.act.ht%d" % c, b)

            def section_F(b, ph):
                i = b % 2
                if ph == 4:
                    if b == 0:
                        act.wait_ge(s_w2, 16 * 7)
                        act.activation(gam2[:], gam[:], ACT.Copy, scale=float(D) ** 0.5).then_inc(s_gam, 1)
                        act.activation(nba[:], bq1[:, 2, :], ACT.Copy, scale=-1.0).then_inc(s_gam, 1)
                        act.wait_ge(s_gam, 2)
                    wait(act, "F.pe.tr", b)
                    wait(act, "F.pe.k3", b - 1)
                    did(act.activation(xT_f[:], of("F.tr", b)[:], ACT.Copy, scale=gam2[:]), "F.act.xT", b)
                if ph == 6:
                    if b == 0:
                        wait(act, "O.dve.h", B - 1)
                    for j in range(PAIRS):
                        wait(act, "F.pe.a%d" % j, b)
                        wait(act, "F.dve.k3", b - 1)
                        did(act.activation(la[:, j, :], of("F.a%d" % j, b)[:], ACT.Exp, scale=-1.0, bias=nba[:, j:j + 1]),
                            "F.act.e%d" % j, b)
                if ph == 8:
                    wait(act, "F.dve.e", b)
                    did(act.activation(la[:], la[:], ACT.Ln, bias=one[:]), "F.act.l", b)
                if ph == 11:
                    wait(act, "F.dve.cut", b)
                    did(act.activation(lb[:], lb[:], ACT.Exp, scale=-1.0), "F.act.cum", b)
                    did(act.activation(la[:], la[:], ACT.Exp), "F.act.inv", b)

            def section_G(n, ph):
                k = n % 2
                if ph == 1:
                    if n == 0:
                        wait(act, "E.dve.h", B - 1)
                    wait(act, "G.pe.tr", n)
                    wait(act, "G.pe.kv", n - 2)
                    did(act.activation(kt[k][:].rearrange("p a b -> p (a b)"), of("G.tr", n)[:], ACT.Copy), "G.act.kt", n)
                if ph == 3:
                    wait(act, "G.pe.av", n)
                    wait(act, "G.pe.out", n - 2)
                    did(act.activation(oc[k][:].rearrange("p a b -> p (a b)"), of("G.av", n)[:], ACT.Copy), "G.act.o", n)
                    wait(act, "G.pe.kv", n)
                    did(act.activation(ss[k][:].rearrange("p a b -> p (a b)"), bank[7][:], ACT.Copy, scale=HD1 ** -0.5),
                        "G.act.s", n)

            def section_I(b, ph):
                if ph == 4:
                    if b == 0:
                        act.wait_ge(s_w3, 16 * 7)
                    wait(act, "I.pe.tr", b)
                    wait(act, "I.pe.lg", b - 2)
                    did(act.activation(xT[b % 2][:], of("I.tr", b)[:], ACT.Identity, bias=lngb1[:, 1:2], scale=lngb1[:, 0:1]),
                        "I.act.xT", b)
                if ph == 7:
                    wait(act, "I.dve.sub", b)
                    did(act.activation(rt[:, 1], rt[:, 0], ACT.Exp), "I.act.exp", b)
                if ph == 10:
                    wait(act, "I.pe.cT", b)
                    wait(act, "I.pe.b2", b - 1)
                    did(act.activation(cT[:], of("I.cT", b)[0:E, :], ACT.Copy), "I.act.cT", b)

            def section_Q(n, ph):
                b, q = n // T, n % T
                if ph == 1:
                    wait(act, "Q.pe.tr", n)
                    m = min(T, TILES - T * q)
                    did(act.activation(xg[:, T * q:T * q + m, :].rearrange("p j d -> p (j d)"), of("Q.tr", n)[:, 0:m * P],
                                       ACT.Identity, bias=lngb1[:, 1:2], scale=lngb1[:, 0:1]), "Q.act.x", n)

            def section_K(n, ph):
                b, j = n // TILES, n % TILES
                if ph == 2:
                    wait(act, "K.pe.up", n)
                    wait(act, "K.pe2.down", n - 2)
                    e = act.value_load(eid[b % 2][0:1, j:j + 1], min_val=0, max_val=E - 1)
                    for c in range(FC):
                        last = act.activation(hid[n % 2][:, c * P:(c + 1) * P], of("K.up", n)[:, c * P:(c + 1) * P], ACT.Gelu,
                                              bias=eb1[:].rearrange("p e c -> p (e c)")[:, bass.ds(e * FC + c, 1)])
                    did(last, "K.act.ht", n)

            def section_J(n, ph):
                e = n % E
                if ph == 1:
                    if n == 0:
                        wait(act, "K.pe2.down", SPARSE * TILES - 1)
                    if n == 1:
                        act.wait_ge(s_ys[SPARSE - 1], 16)
                    for c in range(FC):
                        wait(act, "J.pe.up%d" % c, n)
                        wait(act, "J.pe.down", n - 2)
                        did(act.activation(hj[(n + 1) % 2][:, c, :], of("J.up%d" % c, n)[:], ACT.Gelu, bias=eb1[:, e, c:c + 1]),
                            "J.act.ht%d" % c, n)

            each(order, {"T": section_T, "A": section_A, "B": section_B, "C": section_C, "O": section_O,
                         "D": section_D, "H": section_H, "E": section_E, "F": section_F, "G": section_G,
                         "I": section_I, "J": section_J, "Q": section_Q, "K": section_K})

        @block.vector
        def _(dve):
            dve.wait_ge(s_wtok, 16 * 6)
            dve.tensor_copy(gw2b[:], gw2[:].unsqueeze(2).to_broadcast([GATE_H, TABLES, P])).then_inc(s_gw2b, 1)
            dve.wait_ge(s_gv, 1)
            dve.tensor_copy(gatev[:], bank[7][:, 0:TABLES * (DIM + 1)].rearrange("p (t c) -> p t c", t=TABLES))\
               .then_inc(s_gatev, 1)
            dve.wait_ge(s_gatev, 1)
            dve.tensor_tensor(gb2[:], gb2[:], gatev[:, :, DIM], ALU.add).then_inc(s_banks, 1)
            dve.wait_ge(s_banks, 1)

            def statistics(name, b, src, stats, means, v_eps=None):
                for t in range(T):
                    did(dve.bn_stats(stats[:, t, :], src[:, t, :]), "%s.dve.st%d" % (name, t), b)
                for t in range(T):
                    wait(dve, "%s.dve.st%d" % (name, t), b)
                    did(dve.bn_aggr(means[:, t, :], stats[:, t, :]), "%s.dve.mv%d" % (name, t), b)
                wait(dve, "%s.dve.mv3" % name, b)
                if name in "AODE":
                    did(dve.tensor_scalar(v_eps, means[:, :, 1], EPS, None, ALU.add), name + ".dve.eps", b)

            def normalise(name, b, src, means, scale, dst):
                wait(dve, "%s.pool.rstd" % name, b)
                for t in range(T):
                    did(dve.tensor_scalar(dst[:, t, :], src[:, t, :], means[:, t, 0:1], scale[:, t:t + 1],
                                          ALU.subtract, ALU.mult), "%s.dve.x%d" % (name, t), b)

            dve.wait_ge(s_lnw, 1)
            dve.tensor_copy(lnw[:], bank[6][:, 0:2 * D].rearrange("p (a c) -> p a c", a=2)).then_inc(s_lnb, 1)
            dve.wait_ge(s_lnb, 1)

            def section_T(b, ph):
                i = b % 2
                ein = e_in[b][:].rearrange("p t (a c) -> p t a c", a=TABLES)
                epr = e_pr[:].rearrange("p t (a c) -> p t a c", a=TABLES)
                esc = e_sc[i][:, :, 0:TABLES * DIM].rearrange("p t (a c) -> p t a c", a=TABLES)
                alpha = e_sc[i][:, :, TABLES * DIM:]
                if ph == 0:
                    dve.wait_ge(s_gather[b], 16 * T)
                    did(dve.tensor_tensor(epr, ein, gatev[:, :, 0:DIM].unsqueeze(1).to_broadcast([P, T, TABLES, DIM]),
                                          ALU.mult), "T.dve.prod", b)
                    wait(dve, "T.dve.prod", b)
                    did(dve.tensor_reduce(lg[i][:, 0], epr, X, ALU.add), "T.dve.sum", b)
                    wait(dve, "T.dve.sum", b)
                    did(dve.tensor_tensor(lg[i][:, 1], lg[i][:, 0], gb2[:].unsqueeze(1).to_broadcast([P, T, TABLES]),
                                          ALU.add), "T.dve.bias", b)
                    wait(dve, "T.dve.bias", b)
                    did(dve.tensor_reduce(lg[i][:, 4, :, 0], lg[i][:, 1], X, ALU.max), "T.dve.max", b)
                    wait(dve, "T.dve.max", b)
                    did(dve.tensor_tensor(lg[i][:, 2], lg[i][:, 1], lg[i][:, 4, :, 0:1].to_broadcast([P, T, TABLES]),
                                          ALU.subtract), "T.dve.sub", b)
                if ph == 2:
                    wait(dve, "T.act.exp", b)
                    did(dve.tensor_reduce(lg[i][:, 4, :, 1], lg[i][:, 3], X, ALU.add), "T.dve.den", b)
                    wait(dve, "T.dve.den", b)
                    did(dve.reciprocal(lg[i][:, 4, :, 2], lg[i][:, 4, :, 1]), "T.dve.rden", b)
                    wait(dve, "T.dve.rden", b)
                    wait(dve, "T.pe.tr2", b - 2)
                    did(dve.tensor_tensor(alpha, lg[i][:, 3], lg[i][:, 4, :, 2:3].to_broadcast([P, T, TABLES]),
                                          ALU.mult), "T.dve.alpha", b)
                    wait(dve, "T.dve.alpha", b)
                    did(dve.tensor_tensor(esc, ein, alpha.unsqueeze(3).to_broadcast([P, T, TABLES, DIM]),
                                          ALU.mult), "T.dve.scaled", b)
                if ph == 6:
                    wait(dve, "T.pe.h", b)
                    did(dve.tensor_copy(h[:, b * T:(b + 1) * T, :], of("T.h", b)[:].rearrange("p (t c) -> p t c", t=T)), "T.dve.h", b)

            def section_A(b, ph):
                i = b % 2
                if ph == 0:
                    wait(dve, "T.dve.h", b)
                    statistics("A", b, h[:, b * T:(b + 1) * T, :], stat[i], mv[i], ve[i][:, 0])
                if ph == 2:
                    wait(dve, "A.pe.tr", b - 2)
                    normalise("A", b, h[:, b * T:(b + 1) * T, :], mv[i], rstd[i][:, 0], xn[i])
                if ph == 6:
                    if b == 0:
                        dve.wait_ge(s_w0, 16 * 5)
                    for t in range(T):
                        wait(dve, "A.pe.qkv%d" % t, b)
                        wait(dve, "C.pe.kv", b - 2)
                        did(dve.tensor_tensor(qkv[i][:, t, 0:3 * D], of("A.qkv%d" % t, b)[:, 0:3 * D], bqkv0[:], ALU.add),
                            "A.dve.qkv%d" % t, b)

            def section_B(b, ph):
                i = b % 2
                qk = qkv[i][:, :, 0:2 * D].rearrange("p t (g c) -> p t g c", c=HD0)
                if ph == 1:
                    wait(dve, "B.act.sq", b)
                    did(dve.tensor_reduce(n2[i][:, 0].rearrange("p (t g) -> p t g", t=T),
                                          sq[i][:].rearrange("p t (g c) -> p t g c", c=HD0), X, ALU.add), "B.dve.n2", b)
                if ph == 3:
                    wait(dve, "B.act.rn", b)
                    wait(dve, "B.act.tanh", b - 1)
                    rn = n2[i][:, 2].rearrange("p (t g) -> p t g", t=T)
                    did(dve.tensor_tensor(u[:].rearrange("p t (g c) -> p t g c", c=HD0), qk,
                                          rn.unsqueeze(3).to_broadcast([P, T, 16, HD0]), ALU.mult), "B.dve.u", b)
                if ph == 5:
                    wait(dve, "B.act.tq", b)
                    did(dve.tensor_scalar(pw[:], tq[:].rearrange("p t g -> p (t g)"), 0.5, None, ALU.add), "B.dve.pw", b)
                    wait(dve, "B.dve.pw", b)
                    l = lnu[:].rearrange("p t (g c) -> p (t g) c", c=HD0)
                    did(dve.tensor_tensor(l, l, pw[:].unsqueeze(2).to_broadcast([P, T * HEADS0, HD0]), ALU.mult), "B.dve.pl", b)
                if ph == 7:
                    wait(dve, "B.act.sin", b)
                    wait(dve, "B.pool.k3", b)
                    wait(dve, "C.pe.kv", b - 2)
                    did(dve.tensor_tensor(fs[i][:], amp[:], sn[:], ALU.mult), "B.dve.fs", b)
                    wait(dve, "B.act.cos", b)
                    did(dve.tensor_tensor(fc[i][:], amp[:], cs[:], ALU.mult), "B.dve.fc", b)

            def section_C(b, ph):
                i = b % 2
                if ph == 1:
                    wait(dve, "C.pe.kv", b)
                    wait(dve, "C.pe.o1", b - 1)
                    p = of("C.kv", b)
                    for n in range(2):
                        did(dve.tensor_tensor(kvm[:, n, 0:D], p[:, n * (D + 1):n * (D + 1) + D], blk[:, 0:D], ALU.mult),
                            "C.dve.kv%d" % n, b)
                    for n in range(2):
                        did(dve.tensor_scalar(kvm[:, n, D:], blk[:, D:], p[:, n * (D + 1) + D:(n + 1) * (D + 1)], None, ALU.mult),
                            "C.dve.km%d" % n, b)
                if ph == 3:
                    part = [of("C.o%d" % n, b)[:, 0:2 * (D + HEADS0)].rearrange("p (t c) -> p t c", t=2) for n in range(2)]
                    for n in range(2):
                        wait(dve, "C.pe.o%d" % n, b)
                        did(dve.tensor_scalar(den[:, n * 16:(n + 1) * 16].rearrange("p (t g) -> p t g", t=2),
                                              part[n][:, :, D:], 1e-6, None, ALU.add), "C.dve.den%d" % n, b)
                    wait(dve, "C.dve.den1", b)
                    did(dve.reciprocal(rden[:], den[:]), "C.dve.z", b)
                    wait(dve, "C.dve.z", b)
                    for n in range(2):
                        z = rden[:, n * 16:(n + 1) * 16].rearrange("p (t g) -> p t g", t=2).unsqueeze(3).to_broadcast([P, 2, HEADS0, HD0])
                        did(dve.tensor_tensor(o[:, 2 * n:2 * n + 2, :].rearrange("p t (g c) -> p t g c", c=HD0),
                                              part[n][:, :, 0:D].rearrange("p t (g c) -> p t g c", c=HD0), z, ALU.mult),
                            "C.dve.o%d" % n, b)

            def section_O(b, ph):
                i = b % 2
                if ph == 0:
                    wait(dve, "C.dve.o1", b)
                    statistics("O", b, o, stat_o, mv_o, ve_o[:])
                if ph == 2:
                    normalise("O", b, o, mv_o, rstd_o, on)
                if ph == 6:
                    hb = h[:, b * T:(b + 1) * T, :]
                    wait(dve, "O.pe.out", b)
                    wait(dve, "A.pool.hb", b)
                    did(dve.tensor_tensor(hb, hb, of("O.out", b)[:].rearrange("p (t c) -> p t c", t=T), ALU.add), "O.dve.h", b)

            def section_D(b, ph):
                i = b % 2
                hb = h[:, b * T:(b + 1) * T, :]
                if ph == 0:
                    wait(dve, "O.dve.h", b)
                    statistics("D", b, hb, stat[i], mv[i], ve[i][:, 0])
                if ph == 2:
                    wait(dve, "H.pool.xb", b - 2)
                    wait(dve, "A.pe.tr", B - 1 - (b + 1) % 2)
                    normalise("D", b, hb, mv[i], rstd[i][:, 0], xn[i])

            def section_H(b, ph):
                i = b % 2
                hb = h[:, b * T:(b + 1) * T, :]
                if ph == 3:
                    wait(dve, "H.pe.g", b)
                    did(dve.tensor_scalar(grow[i][:], of("H.g", b)[:, 0:1], 1.0 / S, gcol[:, 1:2], ALU.mult, ALU.add),
                        "H.dve.g", b)
                    wait(dve, "H.dve.g", b)
                    did(dve.tensor_scalar(selg[i][:], sel[:], grow[i][:], None, ALU.mult), "H.dve.sel", b)
                    wait(dve, "H.pe.b", b - 1)
                    did(dve.tensor_copy(gb[:], grow[i][:].to_broadcast([P, P])), "H.dve.gb", b)
                if ph == 5:
                    if b == 0:
                        wait(dve, "T.pe.h", B - 1)
                    wait(dve, "H.pe.w1", b)
                    wait(dve, "E.pe.down", b - 2)
                    did(dve.tensor_tensor(w1m[i][:], of("H.w1", b)[:], w1t[:], ALU.add), "H.dve.w1", b)
                    wait(dve, "H.pe.w2", b)
                    did(dve.tensor_tensor(w2m[i][:], of("H.w2", b)[:], w2t[:], ALU.add), "H.dve.w2", b)
                    wait(dve, "H.pe.b", b)
                    did(dve.tensor_tensor(b1m[i][:], of("H.b", b)[:, 0:FC], b1t[:], ALU.add), "H.dve.b1", b)
                    wait(dve, "H.pool.xb", b - 1)
                    did(dve.tensor_tensor(wide[:], of("H.b", b)[:, P:2 * P], b2w[:], ALU.add), "H.dve.b2", b)

            def section_E(b, ph):
                hb = h[:, b * T:(b + 1) * T, :]
                if ph == 4:
                    wait(dve, "E.pe.down", b)
                    wait(dve, "H.pool.xb", b)
                    did(dve.tensor_tensor(res[:], of("E.down", b)[:].rearrange("p (t c) -> p t c", t=T), xb[:], ALU.add),
                        "E.dve.res", b)
                    wait(dve, "E.dve.res", b)
                    statistics("E", b, res, stat_e, mv_e, ve_e[:])
                if ph == 6:
                    normalise("E", b, res, mv_e, rstd_e, rn)
                    wait(dve, "E.dve.x3", b)
                    did(dve.tensor_tensor(rn[:], rn[:], lnw[:, 0, :].unsqueeze(1).to_broadcast([P, T, D]), ALU.mult),
                        "E.dve.g", b)
                    wait(dve, "E.dve.g", b)
                    wait(dve, "D.pool.hb", b)
                    did(dve.tensor_tensor(hb, hb, rn[:], ALU.add), "E.dve.h", b)

            def section_F(b, ph):
                i = b % 2
                hb = h[:, b * T:(b + 1) * T, :]
                if ph == 0:
                    wait(dve, "E.dve.h", b)
                    statistics("F", b, hb, stat_f, mv_f)
                    did(dve.tensor_scalar(low[:], mv_f[:, :, 1], EPS, 1e-24, ALU.add, ALU.mult), "F.dve.lo", b)
                    wait(dve, "F.dve.lo", b)
                    did(dve.scalar_tensor_tensor(ve_f[:], mv_f[:, :, 1], float(D), low[:], ALU.mult, ALU.max),
                        "F.dve.var", b)
                if ph == 2:
                    wait(dve, "F.pe.tr", b - 1)
                    normalise("F", b, hb, mv_f, rstd_f[:], xn_f)
                if ph == 7:
                    wait(dve, "F.act.e3", b)
                    la2 = la[:].rearrange("p a b -> p (a b)")
                    did(dve.tensor_scalar(la2, la2, 1e10, None, ALU.min), "F.dve.e", b)
                    if b == 0:
                        dve.wait_ge(s_w2, 16 * 7)
                    for t in range(T):
                        wait(dve, "F.pe.v%d" % t, b)
                        wait(dve, "G.pe.kv", (b - 2) * T + 3)
                        did(dve.tensor_tensor(vv[i][:, t, :], of("F.v%d" % t, b)[:], bv1[:], ALU.add), "F.dve.v%d" % t, b)
                if ph == 9:
                    wait(dve, "F.act.l", b)
                    for j in range(PAIRS):
                        did(dve.tensor_tensor_scan(lb[:, j, :], la[:, j, :], la[:, j, :], 0.0, ALU.add, ALU.bypass),
                            "F.dve.sum%d" % j, b)
                if ph == 10:
                    wait(dve, "F.dve.sum3", b)
                    did(dve.tensor_scalar(la[:].rearrange("p a b -> p (a b)"), lb[:].rearrange("p a b -> p (a b)"),
                                          LN_INV_MAX, None, ALU.min), "F.dve.cut", b)
                if 13 <= ph < 17:
                    j = ph - 13
                    wait(dve, "F.act.inv", b)
                    wait(dve, "G.pe.av", (b - 2) * T + 3)
                    dve.wait_ge(s_qz, min(b + 1, 2))
                    if b == 1:
                        dve.wait_ge(s_zero, 16 * SPARSE)
                    wait(dve, "F.pe.q%d" % j, b)
                    for m, name in enumerate(("qa", "qb")):
                        rows = slice(m * HD1, (m + 1) * HD1)
                        did(dve.scalar_tensor_tensor(qz[i][rows, j, m, :], of("F.q%d" % j, b)[rows, :], bq1[rows, 0, j:j + 1],
                                                     lb[rows, j, :], ALU.add, ALU.mult), "F.dve.%s%d" % (name, j), b)
                    wait(dve, "F.pe.k%d" % j, b)
                    did(dve.scalar_tensor_tensor(kk[i][:, j, :], of("F.k%d" % j, b)[:], bq1[:, 1, j:j + 1], la[:, j, :],
                                                 ALU.add, ALU.mult), "F.dve.k%d" % j, b)

            def section_G(n, ph):
                if ph == 1:
                    if n == 0:
                        wait(dve, "E.dve.h", B - 1)
                    for m in range(2):
                        wait(dve, "G.pe.qk%d" % m, n)
                        wait(dve, "G.pe.av", n - 2)
                        did(dve.tensor_tensor(sim[n % 2][:, 2 * m:2 * m + 2].rearrange("p a b c -> p (a b c)"),
                                              of("G.qk%d" % m, n)[:], causal[:], ALU.mult), "G.dve.m%d" % m, n)
                if ph == 5:
                    wait(dve, "G.pe.out", n)
                    wait(dve, "F.pool.hb", n // T)
                    did(dve.tensor_tensor(h[:, n, :], h[:, n, :], of("G.out", n)[:, 0:D], ALU.add), "G.dve.h", n)

            def section_I(b, ph):
                i = b % 2
                hb = h[:, b * T:(b + 1) * T, :]
                if ph == 0:
                    wait(dve, "G.dve.h", b * T + 3)
                    statistics("I", b, hb, stat[i], mv[i], ve[i][:, 0])
                    did(dve.tensor_scalar(ve[i][:, 0], mv[i][:, :, 1], EPS, None, ALU.add), "I.dve.ve", b)
                    did(dve.tensor_scalar(ve[i][:, 1], mv[i][:, :, 1], 1.0 + EPS, EPS * EPS, ALU.mult, ALU.add), "I.dve.vv", b)
                if ph == 2:
                    normalise("I", b, hb, mv[i], rstd[i][:, 0], xn[1])
                    wait(dve, "I.pe.tr", b - 1)
                    if b:
                        dve.wait_ge(s_deal[b - 1], 16 * 2 * T)
                    for t in range(T):
                        did(dve.tensor_scalar(xn[0][:, t, :], hb[:, t, :], mv[i][:, t, 0:1], rstd[i][:, 1, t:t + 1],
                                              ALU.subtract, ALU.mult), "I.dve.y%d" % t, b)
                if ph == 3:
                    wait(dve, "I.dve.y3", b)
                    did(dve.tensor_tensor(hb, hb, xn[1][:], ALU.add), "I.dve.h", b)
                if ph == 6:
                    wait(dve, "I.pe.lg", b)
                    lgt = of("I.lg", b)[:, 0:T * E].rearrange("p (t e) -> p t e", t=T)
                    did(dve.tensor_reduce(r1[:, 0], lgt, X, ALU.max), "I.dve.max", b)
                    wait(dve, "I.dve.max", b)
                    did(dve.tensor_tensor(rt[:, 0], lgt, r1[:, 0].unsqueeze(2).to_broadcast([P, T, E]), ALU.subtract),
                        "I.dve.sub", b)
                if ph == 8:
                    wait(dve, "I.act.exp", b)
                    did(dve.tensor_reduce(r1[:, 1], rt[:, 1], X, ALU.add), "I.dve.den", b)
                    wait(dve, "I.dve.den", b)
                    did(dve.reciprocal(r1[:, 2], r1[:, 1]), "I.dve.rden", b)
                    wait(dve, "I.dve.rden", b)
                    did(dve.tensor_tensor(rt[:, 2], rt[:, 1], r1[:, 2].unsqueeze(2).to_broadcast([P, T, E]), ALU.mult),
                        "I.dve.p", b)
                    wait(dve, "I.dve.p", b)
                    for t in range(T):
                        did(dve.max(rt[:, 3, t, :], rt[:, 2, t, :]), "I.dve.top%d" % t, b)
                    wait(dve, "I.dve.top3", b)
                    for t in range(T):
                        did(dve.max_index(rix[:, t, :], rt[:, 3, t, :], rt[:, 2, t, :]), "I.dve.at%d" % t, b)
                    wait(dve, "I.dve.at3", b)
                    for n in range(2):
                        did(dve.tensor_tensor(rt[:, 4 + n], rix[:, :, n:n + 1].to_broadcast([P, T, E]),
                                              iota.unsqueeze(1).to_broadcast([P, T, E]), ALU.is_equal), "I.dve.is%d" % n, b)
                    wait(dve, "I.dve.is1", b)
                    for n in range(2):
                        did(dve.tensor_tensor(rt[:, 6 + n], rt[:, 4 + n], rt[:, 3, :, n:n + 1].to_broadcast([P, T, E]),
                                              ALU.mult), "I.dve.c%d" % n, b)
                    wait(dve, "I.dve.c1", b)
                    did(dve.tensor_tensor(cmb[b][:], rt[:, 6], rt[:, 7], ALU.add), "I.dve.c", b)
                if ph == 12:
                    wait(dve, "I.pe.b2", b)
                    did(dve.tensor_tensor(hb, hb, of("I.b2", b)[:].rearrange("p (t c) -> p t c", t=T), ALU.add),
                        "I.dve2.h", b)

            def section_J(n, ph):
                b, e = B - 1, n
                if ph == 3:
                    wait(dve, "J.pe.down", n)
                    wait(dve, "I.dve2.h", b)
                    wait(dve, "J.dve.y3", n - 1)
                    for t in range(T):
                        ht_ = h[:, b * T + t, :]
                        did(dve.scalar_tensor_tensor(ht_, of("J.down", n)[:, t * P:(t + 1) * P], cmb[b][:, t, e:e + 1], ht_,
                                                     ALU.mult, ALU.add), "J.dve.y%d" % t, n)

            def section_R(b, ph):
                i = b % 2
                if ph == 0:
                    wait(dve, "I.dve.is1", b)
                    wait(dve, "I.dve.c", b)
                    did(dve.tensor_tensor(rt[:, 0], rt[:, 4], rt[:, 5], ALU.add), "R.dve.m", b)
                if ph == 2:
                    if b == 0:
                        dve.memset(before[:, 0, :], 0.0).then_inc(s_before, 1)
                        dve.wait_ge(s_before, 1)
                    wait(dve, "R.pe.cnt", b)
                    cnt = of("R.cnt", b)
                    for t in range(T):
                        did(dve.tensor_tensor(before[:, t + 1, :], before[:, t, :], cnt[:, (T + t) * E:(T + t + 1) * E],
                                              ALU.add), "R.dve.c%d" % t, b)
                        wait(dve, "R.dve.c%d" % t, b)
                    did(dve.tensor_tensor(rt[:, 1].rearrange("p t e -> p (t e)").rearrange("p (e t) -> p e t", t=T),
                                          before[:, T, :].unsqueeze(2).to_broadcast([P, E, T]),
                                          full.unsqueeze(1).to_broadcast([P, E, T]), ALU.is_gt), "R.dve.gt", b)
                    wait(dve, "R.dve.gt", b)
                    did(dve.tensor_reduce(ntile[:, 0], rt[:, 1].rearrange("p t e -> p (t e)").rearrange("p (e t) -> p e t", t=T),
                                          X, ALU.add), "R.dve.nt", b)
                    wait(dve, "R.dve.nt", b)
                    did(dve.tensor_tensor_scan(ntile[:, 1], ntile[:, 0], ntile[:, 0], 0.0, ALU.add, ALU.bypass), "R.dve.in", b)
                    wait(dve, "R.dve.in", b)
                    did(dve.tensor_tensor(ntile[:, 2], ntile[:, 1], ntile[:, 0], ALU.subtract), "R.dve.ex", b)
                    wait(dve, "R.dve.ex", b)
                    did(dve.scalar_tensor_tensor(first[:], ntile[:, 2].unsqueeze(1).to_broadcast([P, T, E]), float(P),
                                                 before[:, 0:T, :], ALU.mult, ALU.add), "R.dve.pb", b)
                    wait(dve, "R.dve.pb", b)
                    did(dve.tensor_tensor(rt[:, 2], first[:], cnt[:, 0:T * E].rearrange("p (t e) -> p t e", t=T), ALU.add),
                        "R.dve.pos", b)
                    wait(dve, "R.dve.pos", b)
                    did(dve.tensor_tensor(rt[:, 6:8], rt[:, 4:6], rt[:, 2].unsqueeze(1).to_broadcast([P, 2, T, E]), ALU.mult),
                        "R.dve.pk", b)
                    wait(dve, "R.dve.pk", b)
                    did(dve.tensor_reduce(posf[:], rt[:, 6:8], X, ALU.add), "R.dve.pr", b)
                    wait(dve, "R.dve.pr", b)
                    if b >= 2:
                        dve.wait_ge(s_yg[b - 2], 16 * 2 * T)
                    did(dve.tensor_copy(posi[i], posf[:]), "R.dve.pi", b)
                    did(dve.tensor_tensor(ej[:], number.unsqueeze(2).to_broadcast([P, TILES, E]),
                                          ntile[:, 1].unsqueeze(1).to_broadcast([P, TILES, E]), ALU.is_ge), "R.dve.ej", b)
                    wait(dve, "R.dve.ej", b)
                    did(dve.tensor_reduce(ejr[:, 0], ej[:], X, ALU.add), "R.dve.er", b)
                    wait(dve, "R.dve.er", b)
                    did(dve.tensor_scalar(ejr[:, 1], ejr[:, 0], float(E - 1), None, ALU.min), "R.dve.em", b)
                    wait(dve, "R.dve.em", b)
                    did(dve.tensor_copy(eid[i], ejr[:, 1]), "R.dve.ei", b)
                    did(dve.tensor_copy(wts[i], rt[:, 3, :, 0:2]), "R.dve.w", b)

            def section_K(n, ph):
                b, j = n // TILES, n % TILES
                if ph == 0:
                    if n == 0:
                        dve.wait_ge(s_w3, 16 * 7)
                    wait(dve, "R.dve.ei", b)
                    wait(dve, "K.pe.up", n - 2)
                    e = dve.value_load(eid[b % 2][0:1, j:j + 1], min_val=0, max_val=E - 1)
                    did(dve.tensor_copy(w1s[n % 2], big[:, bass.ds(e * FF, FF)]), "K.dve.w1", n)
                if ph == 4:
                    wait(dve, "K.pe2.down", n)
                    did(dve.tensor_copy(xg[:, j, :], of("K.down", n)[:, 0:D]), "K.dve2.y", n)

            def section_Y(b, ph):
                if ph == 1:
                    dve.wait_ge(s_yg[b], 16 * 2 * T)
                    wait(dve, "R.dve.w", b)
                    wait(dve, "I.dve2.h", b)
                    for t in range(T):
                        hb = h[:, b * T + t, :]
                        for k, name in enumerate("ab"):
                            did(dve.scalar_tensor_tensor(hb, yg[:, k, t, :], wts[b % 2][:, t, k:k + 1], hb, ALU.mult, ALU.add),
                                "Y.dve.%s%d" % (name, t), b)
                            wait(dve, "Y.dve.%s%d" % (name, t), b)

            each(order, {"T": section_T, "A": section_A, "B": section_B, "C": section_C, "O": section_O,
                         "D": section_D, "H": section_H, "E": section_E, "F": section_F, "G": section_G,
                         "I": section_I, "J": section_J, "R": section_R,
                         "K": section_K, "Y": section_Y})


def lay(i):
    import numpy as np

    def col(x):
        return np.asarray(x).reshape(-1, P).T

    a = {}
    a["idx"] = np.asarray(i["x"]).reshape(B * T, P).T
    names = ("glove", "fast", "levy")
    a["tables"] = np.concatenate([np.asarray(i["L0_tok_%s_tab" % n]) for n in names], axis=1)
    a["gw1"] = np.stack([np.concatenate([i["L0_tok_gW1_" + n], np.asarray(i["L0_tok_gb1_" + n])[:, None]], axis=1)
                         for n in names], axis=1)
    a["gw2"] = np.stack([np.asarray(i["L0_tok_gW2_" + n])[0] for n in names], axis=1)
    a["gb2"] = np.concatenate([i["L0_tok_gb2_" + n] for n in names])
    a["wtok"] = np.concatenate([np.asarray(i["L0_tok_W_" + n]).T for n in names]
                               + [np.asarray(i["L0_tok_b_" + n])[None] for n in names])
    a["wqkv0"] = i["L0_attn_qkv_w"]
    a["bqkv0"] = i["L0_attn_qkv_b"]
    a["wo0"] = i["L0_attn_out_w"]
    a["bo0"] = i["L0_attn_out_b"]
    a["lngb0"] = np.stack([i["L0_attn_ln_g"], i["L0_attn_ln_b"]], axis=1)
    f = {k[7:]: np.asarray(v) for k, v in i.items() if k.startswith("L0_ffn_")}
    a["g1t"] = f["gfc1_w"].T
    a["g2r"] = np.repeat(f["gfc2_w"].T, J, axis=1)
    a["gcol"] = np.stack([f["gfc1_b"], np.repeat(f["gfc2_b"], J)], axis=1)
    a["w1t"] = f["W1"].T
    a["w2t"] = f["W2"].T.reshape(FC, P, D).transpose(1, 0, 2).reshape(P, FC * D)
    a["tv1"] = f["tv_W1"].transpose(0, 2, 1).reshape(E, D // J, J, FF).transpose(0, 2, 1, 3).reshape(P, D // J, FF)
    a["tv2"] = f["tv_W2"].transpose(0, 2, 1).reshape(E, FC, P // J, J, D).transpose(0, 3, 2, 1, 4).reshape(P, P // J, FC * D)
    a["tvb1"] = f["tv_b1"]
    a["tvb2"] = f["tv_b2"]
    a["b1t"] = col(f["b1"])
    a["b2"] = f["b2"]
    sel = np.zeros((P, 2, 2 * J), np.float32)
    for p in range(P):
        for r in range(2):
            sel[p, r, J * r + p % J] = 1
    a["sel"] = sel
    a["lnr"] = np.concatenate([np.concatenate([f["tv_ln_g"], f["tv_ln_b"]], axis=1),
                               np.concatenate([f["ln_g"], f["ln_b"]])[None]])
    g = {k[8:]: np.asarray(v) for k, v in i.items() if k.startswith("L1_attn_")}
    inner = HEADS1 * HD1
    a["wq"] = np.concatenate([g["w_qkv"], g["w_a"]], axis=1)
    a["wo1"] = g["w_out"].reshape(PAIRS, P, D).transpose(1, 0, 2)
    a["bq1"] = np.stack([col(g["b_qkv"][0:inner]), col(g["b_qkv"][inner:2 * inner]), col(g["b_a"])], axis=1)
    a["bv1"] = g["b_qkv"][2 * inner:]
    a["bo1"] = g["b_out"]
    a["gam"] = g["gamma"].reshape(P, 1)
    a["causal"] = np.tile(np.triu(np.full((P, P), HD1 ** -0.5, np.float32)), (1, 4))
    m = {k[7:]: np.asarray(v) for k, v in i.items() if k.startswith("L1_ffn_")}
    a["gate"] = m["gate_w"]
    a["lngb1"] = np.stack([m["ln_g"], m["ln_b"]], axis=1)
    a["eb1"] = m["b1"].reshape(E, FC, P).transpose(2, 0, 1)
    a["eb2"] = m["b2"]
    a["rank"] = np.concatenate([np.triu(np.ones((P, P), np.float32), 1), np.ones((P, P), np.float32)]
                               + [np.tile(np.arange(n, dtype=np.float32) * k, (P, 1))
                                  for n, k in ((E, 1), (T, P), (TILES, 1))], axis=1).astype(np.float32)
    a["ew1"] = m["w1"].transpose(1, 0, 2)
    a["ew2"] = m["w2"].reshape(E, FC, P, D).transpose(2, 0, 1, 3).reshape(P, E, FC * D)
    return {k: np.ascontiguousarray(v) for k, v in a.items()}


def kernel(**inputs):
    import numpy as np
    import concourse.bacc as bacc
    from concourse.bass_utils import run_bass_kernel_spmd

    nc = bacc.Bacc("TRN2", target_bir_lowering=False, num_devices=1)
    arrays = lay(inputs)
    a = {name: nc.dram_tensor("in_" + name, x.shape, mybir.dt.from_np(x.dtype), kind="ExternalInput").ap()
         for name, x in arrays.items()}
    out = nc.dram_tensor("out", (B * S, D), F32, kind="ExternalOutput").ap()
    lm_tower(nc, a, out)
    got = run_bass_kernel_spmd(nc, [{"in_" + name: x for name, x in arrays.items()}], core_ids=[0])
    return np.asarray(got.results[0]["out"]).reshape(B, S, D)
```
